# Optimizing a Trainium2 kernel written in Bass

```python
import numpy as np
import jax
import jax.numpy as jnp

def _softmax(x, axis=-1):
    return jax.nn.softmax(x, axis=axis)

def _gelu(x):
    return jax.nn.gelu(x, approximate=True)

def _silu(x):
    return jax.nn.silu(x)

def _sigmoid(x):
    return jax.nn.sigmoid(x)

def _layernorm(x, axis=-1, eps=1e-05):
    m = jnp.mean(x, axis=axis, keepdims=True)
    v = jnp.var(x, axis=axis, keepdims=True)
    return (x - m) / jnp.sqrt(v + eps)

def _scatter_add(tgt, idx, src, axis=0):
    return tgt.at[idx].add(src)

def _segment_sum(src, seg, n):
    return jax.ops.segment_sum(src, seg, n)
kernel_name = 'mk_decoder_preln_d2_seqx_r8_f837d8'

def setup_inputs(seed: int=0):
    np.random.seed(seed)
    _w = jnp.asarray

    def _rec_inputs():
        import jax
        import jax.numpy as jnp
        _rk = jax.random.key(seed)
        x = 7.22e-05 + 1 * jax.random.normal(jax.random.fold_in(_rk, 1), (4, 256, 128), jnp.float32)
        _lenS = 256 - jax.random.randint(jax.random.fold_in(_rk, 7), (4,), 0, max(1, 256 // 4) + 1, jnp.int32)
        _lenS2 = 256 - jax.random.randint(jax.random.fold_in(_rk, 8), (4,), 0, max(1, 256 // 4) + 1, jnp.int32)
        _ctx_1024P = jax.random.normal(jax.random.fold_in(_rk, 11), (4, 16, 128), jnp.float32)
        _ctx_1024c = jax.random.dirichlet(jax.random.fold_in(_rk, 511), 0.3 * jnp.ones((16,), jnp.float32), (4, 256))
        _ctx_1024t = jnp.einsum('bsk,bkd->bsd', _ctx_1024c, _ctx_1024P)
        _ctx_1024t = _ctx_1024t * jax.lax.rsqrt(jnp.mean(jnp.square(_ctx_1024t)) + 1e-12) * 0.953939
        ctx_1024 = 4.13588e-05 + 0.999923 * (_ctx_1024t + 0.3 * jax.random.normal(jax.random.fold_in(_rk, 611), (4, 256, 128), jnp.float32))
        return (x, ctx_1024)
    x, ctx_1024 = _rec_inputs()

    def _L0_attn_setup():
        import jax, jax.numpy as jnp
        import numpy as np
        N_HEADS = 16
        SEG = 64
        EPS = 1e-06

        def _sigma(x):
            return jax.nn.elu(x) + 1.0

        def _infini_attention(x, W_q, W_k, W_v, W_o, beta_param):
            B, T, D = x.shape
            H = N_HEADS
            dk = D // H
            assert T % SEG == 0
            S = T // SEG

            def proj(W):
                y = (x @ W.T).reshape(B, T, H, dk).transpose(0, 2, 1, 3)
                return y.reshape(B, H, S, SEG, dk).transpose(2, 0, 1, 3, 4)
            Qs, Ks, Vs = (proj(W_q), proj(W_k), proj(W_v))
            beta = jax.nn.sigmoid(beta_param).reshape(1, H, 1, 1)
            causal = jnp.triu(jnp.ones((SEG, SEG), dtype=bool), k=1)
            inv_sqrt_dk = 1.0 / jnp.sqrt(jnp.asarray(dk, x.dtype))
            M0 = jnp.zeros((B, H, dk, dk), dtype=x.dtype)
            z0 = jnp.zeros((B, H, dk), dtype=x.dtype)

            def step(carry, qkv):
                M, z = carry
                q, k, v = qkv
                sq = _sigma(q)
                denom_q = jnp.sum(sq * z[:, :, None, :], axis=-1, keepdims=True) + EPS
                A_mem = jnp.matmul(sq, M) / denom_q
                scores = jnp.matmul(q, jnp.swapaxes(k, -2, -1)) * inv_sqrt_dk
                scores = jnp.where(causal, -jnp.inf, scores)
                A_dot = jnp.matmul(jax.nn.softmax(scores, axis=-1), v)
                A_s = beta * A_mem + (1.0 - beta) * A_dot
                sk = _sigma(k)
                denom_k = jnp.sum(sk * z[:, :, None, :], axis=-1, keepdims=True) + EPS
                V_prev = jnp.matmul(sk, M) / denom_k
                M_new = M + jnp.einsum('bhtk,bhtv->bhkv', sk, v - V_prev)
                z_new = z + jnp.sum(sk, axis=-2)
                return ((M_new, z_new), A_s)
            (M, z), outs = jax.lax.scan(step, (M0, z0), (Qs, Ks, Vs))
            out = outs.transpose(1, 3, 0, 2, 4).reshape(B, S * SEG, H, dk)
            out = outs.transpose(1, 2, 0, 3, 4).reshape(B, H, T, dk)
            out = out.transpose(0, 2, 1, 3).reshape(B, T, D)
            out = out @ W_o.T
            return (out, M.mean(0), z.mean(0))

        def _reference_tuple_inner(x, W_q, W_k, W_v, W_o, beta_param):
            return _infini_attention(x, W_q, W_k, W_v, W_o, beta_param)
        key = jax.random.key(seed)
        kx, kq, kk, kv, ko = jax.random.split(key, 5)
        B, T, D = (4, 512, 128)
        scale = D ** (-0.5)
        return {'x': jax.random.normal(kx, (B, T, D), dtype=jnp.float32), 'W_q': jax.random.normal(kq, (D, D), dtype=jnp.float32) * scale, 'W_k': jax.random.normal(kk, (D, D), dtype=jnp.float32) * scale, 'W_v': jax.random.normal(kv, (D, D), dtype=jnp.float32) * scale, 'W_o': jax.random.normal(ko, (D, D), dtype=jnp.float32) * scale, 'beta_param': jnp.zeros((N_HEADS,), dtype=jnp.float32)}
    _L0_attn_all = _L0_attn_setup()
    _L0_attn_in = {k: v for k, v in _L0_attn_all.items() if k in ('W_q', 'W_k', 'W_v', 'W_o', 'beta_param')}
    del _L0_attn_all

    def _L0_xattn_setup():
        import jax, jax.numpy as jnp
        import numpy as np
        D_MODEL = 128
        NUM_HEADS = 16
        D_K = D_MODEL // NUM_HEADS

        def _mha(query, key, value, Wq, bq, Wk, bk, Wv, bv, Wo, bo):
            B, S, D = query.shape
            H, dk = (NUM_HEADS, D_K)

            def split_heads(x):
                return x.reshape(B, S, H, dk).transpose(0, 2, 1, 3)
            Q = split_heads(query @ Wq + bq)
            K = split_heads(key @ Wk + bk)
            V = split_heads(value @ Wv + bv)
            scores = jnp.einsum('bhqd,bhkd->bhqk', Q, K) / jnp.sqrt(jnp.float32(dk)).astype(Q.dtype)
            attn = jax.nn.softmax(scores, axis=-1)
            ctx = jnp.einsum('bhqk,bhkd->bhqd', attn, V)
            ctx = ctx.transpose(0, 2, 1, 3).reshape(B, S, D)
            return ctx @ Wo + bo
        key = jax.random.key(seed)
        ks = jax.random.split(key, 11)
        B, S, D = (4, 256, D_MODEL)
        scale = 1.0 / np.sqrt(D)
        inp = {'query': jax.random.normal(ks[0], (B, S, D), jnp.float32), 'key': jax.random.normal(ks[1], (B, S, D), jnp.float32), 'value': jax.random.normal(ks[2], (B, S, D), jnp.float32), 'Wq': jax.random.normal(ks[3], (D, D), jnp.float32) * scale, 'bq': jnp.zeros((D,), jnp.float32), 'Wk': jax.random.normal(ks[4], (D, D), jnp.float32) * scale, 'bk': jnp.zeros((D,), jnp.float32), 'Wv': jax.random.normal(ks[5], (D, D), jnp.float32) * scale, 'bv': jnp.zeros((D,), jnp.float32), 'Wo': jax.random.normal(ks[6], (D, D), jnp.float32) * scale, 'bo': jnp.zeros((D,), jnp.float32)}
        return inp
    _L0_xattn_all = _L0_xattn_setup()
    _L0_xattn_in = {k: v for k, v in _L0_xattn_all.items() if k in ('Wq', 'bq', 'Wk', 'bk', 'Wv', 'bv', 'Wo', 'bo')}
    del _L0_xattn_all

    def _L0_ffn_setup():
        import jax, jax.numpy as jnp
        import numpy as np
        B, T, C = (4, 128, 128)
        E = 8
        TOP_K = 2
        H = 64
        HS = 256
        key = jax.random.key(seed)
        ks = jax.random.split(key, 7)
        std = 0.02
        return {'x': jax.random.normal(ks[0], (B, T, C), dtype=jnp.float32), 'router_w': jax.random.normal(ks[1], (E, C), dtype=jnp.float32) * std, 'gate_up_w': jax.random.normal(ks[2], (E, C, 2 * H), dtype=jnp.float32) * std, 'down_w': jax.random.normal(ks[3], (E, H, C), dtype=jnp.float32) * std, 'shared_gate_w': jax.random.normal(ks[4], (HS, C), dtype=jnp.float32) * std, 'shared_up_w': jax.random.normal(ks[5], (HS, C), dtype=jnp.float32) * std, 'shared_down_w': jax.random.normal(ks[6], (C, HS), dtype=jnp.float32) * std}
    _L0_ffn_all = _L0_ffn_setup()
    _L0_ffn_in = {k: v for k, v in _L0_ffn_all.items() if k in ('router_w', 'gate_up_w', 'down_w', 'shared_gate_w', 'shared_up_w', 'shared_down_w')}
    del _L0_ffn_all

    def _L1_attn_setup():
        import jax, jax.numpy as jnp
        import numpy as np
        B, T, C, H = (2, 256, 128, 16)
        key = jax.random.key(seed)
        ks = jax.random.split(key, 6)
        x = jax.random.normal(ks[0], (B, T, C), dtype=jnp.float32)
        wq = jax.random.normal(ks[1], (C, H * 3), dtype=jnp.float32) * C ** (-0.5)
        wk = jax.random.normal(ks[2], (C, H * 3), dtype=jnp.float32) * C ** (-0.5)
        wv = jax.random.normal(ks[3], (C, C), dtype=jnp.float32) * C ** (-0.5)
        wo = jax.random.normal(ks[4], (C, C), dtype=jnp.float32) * C ** (-0.5)
        dirs = jax.random.normal(ks[5], (H, 3), dtype=jnp.float32)
        head_dirs = dirs / jnp.linalg.norm(dirs, axis=1, keepdims=True)
        scale = jnp.full((1,), 1.0 / np.sqrt(3.0), dtype=jnp.float32)
        return {'x': x, 'wq': wq, 'wk': wk, 'wv': wv, 'wo': wo, 'head_dirs': head_dirs, 'scale': scale}
    _L1_attn_all = _L1_attn_setup()
    _L1_attn_in = {k: v for k, v in _L1_attn_all.items() if k in ('wq', 'wk', 'wv', 'wo', 'head_dirs', 'scale')}
    del _L1_attn_all

    def _L1_xattn_setup():
        import jax, jax.numpy as jnp
        import numpy as np
        HIDDEN = 128
        HEADS = 16
        HEAD_DIM = 64
        key = jax.random.key(seed)
        ks = jax.random.split(key, 7)
        B, Q, K = (2, 256, 512)
        s = 1.0 / np.sqrt(HIDDEN)
        return {'query': jax.random.normal(ks[0], (B, Q, HIDDEN), dtype=jnp.float32), 'key': jax.random.normal(ks[1], (B, K, HIDDEN), dtype=jnp.float32), 'value': jax.random.normal(ks[2], (B, K, HIDDEN), dtype=jnp.float32), 'w_q': jax.random.normal(ks[3], (HIDDEN, HEADS * HEAD_DIM), dtype=jnp.float32) * s, 'w_k': jax.random.normal(ks[4], (HIDDEN, HEADS * HEAD_DIM), dtype=jnp.float32) * s, 'w_v': jax.random.normal(ks[5], (HIDDEN, HEADS * HEAD_DIM), dtype=jnp.float32) * s, 'w_o': jax.random.normal(ks[6], (HEADS * HEAD_DIM, HIDDEN), dtype=jnp.float32) * s}
    _L1_xattn_all = _L1_xattn_setup()
    _L1_xattn_in = {k: v for k, v in _L1_xattn_all.items() if k in ('w_q', 'w_k', 'w_v', 'w_o')}
    del _L1_xattn_all

    def _L1_ffn_setup():
        import jax, jax.numpy as jnp
        import numpy as np
        DIM = 128

        def _reference_tuple_inner(x, W_r, W_k, W_v, mu_r, mu_k):
            B, T, C = x.shape
            x_prev = jnp.concatenate([jnp.zeros((B, 1, C), x.dtype), x[:, :-1, :]], axis=1)
            xr = mu_r * x + (1.0 - mu_r) * x_prev
            xk = mu_k * x + (1.0 - mu_k) * x_prev
            r = jax.nn.sigmoid(jnp.einsum('btc,dc->btd', xr, W_r))
            k = jnp.einsum('btc,dc->btd', xk, W_k)
            k_act = jnp.square(jax.nn.relu(k))
            out = r * jnp.einsum('btc,dc->btd', k_act, W_v)
            new_state = x[:, -1, :]
            return (out, new_state)
        key = jax.random.key(seed)
        ks = jax.random.split(key, 6)
        B, T, C = (8, 256, DIM)
        x = jax.random.normal(ks[0], (B, T, C), dtype=jnp.float32)
        s = 1.0 / np.sqrt(C)
        W_r = jax.random.uniform(ks[1], (C, C), jnp.float32, -s, s)
        W_k = jax.random.uniform(ks[2], (C, C), jnp.float32, -s, s)
        W_v = jax.random.uniform(ks[3], (C, C), jnp.float32, -s, s)
        mu_r = jax.random.uniform(ks[4], (C,), jnp.float32)
        mu_k = jax.random.uniform(ks[5], (C,), jnp.float32)
        return {'x': x, 'W_r': W_r, 'W_k': W_k, 'W_v': W_v, 'mu_r': mu_r, 'mu_k': mu_k}
    _L1_ffn_all = _L1_ffn_setup()
    _L1_ffn_in = {k: v for k, v in _L1_ffn_all.items() if k in ('W_r', 'W_k', 'W_v', 'mu_r', 'mu_k')}
    del _L1_ffn_all
    return {'x': x, 'ctx_1024': ctx_1024, 'L0_attn_W_q': _L0_attn_in['W_q'], 'L0_attn_W_k': _L0_attn_in['W_k'], 'L0_attn_W_v': _L0_attn_in['W_v'], 'L0_attn_W_o': _L0_attn_in['W_o'], 'L0_attn_beta_param': _L0_attn_in['beta_param'], 'L0_xattn_Wq': _L0_xattn_in['Wq'], 'L0_xattn_bq': _L0_xattn_in['bq'], 'L0_xattn_Wk': _L0_xattn_in['Wk'], 'L0_xattn_bk': _L0_xattn_in['bk'], 'L0_xattn_Wv': _L0_xattn_in['Wv'], 'L0_xattn_bv': _L0_xattn_in['bv'], 'L0_xattn_Wo': _L0_xattn_in['Wo'], 'L0_xattn_bo': _L0_xattn_in['bo'], 'L0_ffn_router_w': _L0_ffn_in['router_w'], 'L0_ffn_gate_up_w': _L0_ffn_in['gate_up_w'], 'L0_ffn_down_w': _L0_ffn_in['down_w'], 'L0_ffn_shared_gate_w': _L0_ffn_in['shared_gate_w'], 'L0_ffn_shared_up_w': _L0_ffn_in['shared_up_w'], 'L0_ffn_shared_down_w': _L0_ffn_in['shared_down_w'], 'L1_attn_wq': _L1_attn_in['wq'], 'L1_attn_wk': _L1_attn_in['wk'], 'L1_attn_wv': _L1_attn_in['wv'], 'L1_attn_wo': _L1_attn_in['wo'], 'L1_attn_head_dirs': _L1_attn_in['head_dirs'], 'L1_attn_scale': _L1_attn_in['scale'], 'L1_xattn_w_q': _L1_xattn_in['w_q'], 'L1_xattn_w_k': _L1_xattn_in['w_k'], 'L1_xattn_w_v': _L1_xattn_in['w_v'], 'L1_xattn_w_o': _L1_xattn_in['w_o'], 'L1_ffn_W_r': _L1_ffn_in['W_r'], 'L1_ffn_W_k': _L1_ffn_in['W_k'], 'L1_ffn_W_v': _L1_ffn_in['W_v'], 'L1_ffn_mu_r': _L1_ffn_in['mu_r'], 'L1_ffn_mu_k': _L1_ffn_in['mu_k']}

def reference(x, ctx_1024, L0_attn_W_q, L0_attn_W_k, L0_attn_W_v, L0_attn_W_o, L0_attn_beta_param, L0_xattn_Wq, L0_xattn_bq, L0_xattn_Wk, L0_xattn_bk, L0_xattn_Wv, L0_xattn_bv, L0_xattn_Wo, L0_xattn_bo, L0_ffn_router_w, L0_ffn_gate_up_w, L0_ffn_down_w, L0_ffn_shared_gate_w, L0_ffn_shared_up_w, L0_ffn_shared_down_w, L1_attn_wq, L1_attn_wk, L1_attn_wv, L1_attn_wo, L1_attn_head_dirs, L1_attn_scale, L1_xattn_w_q, L1_xattn_w_k, L1_xattn_w_v, L1_xattn_w_o, L1_ffn_W_r, L1_ffn_W_k, L1_ffn_W_v, L1_ffn_mu_r, L1_ffn_mu_k):
    import jax
    import jax.numpy as jnp

    def _L0_attn_ref(x, W_q, W_k, W_v, W_o, beta_param):
        import jax, jax.numpy as jnp
        import numpy as np
        N_HEADS = 16
        SEG = 64
        EPS = 1e-06

        def _sigma(x):
            return jax.nn.elu(x) + 1.0

        def _infini_attention(x, W_q, W_k, W_v, W_o, beta_param):
            B, T, D = x.shape
            H = N_HEADS
            dk = D // H
            assert T % SEG == 0
            S = T // SEG

            def proj(W):
                y = (x @ W.T).reshape(B, T, H, dk).transpose(0, 2, 1, 3)
                return y.reshape(B, H, S, SEG, dk).transpose(2, 0, 1, 3, 4)
            Qs, Ks, Vs = (proj(W_q), proj(W_k), proj(W_v))
            beta = jax.nn.sigmoid(beta_param).reshape(1, H, 1, 1)
            causal = jnp.triu(jnp.ones((SEG, SEG), dtype=bool), k=1)
            inv_sqrt_dk = 1.0 / jnp.sqrt(jnp.asarray(dk, x.dtype))
            M0 = jnp.zeros((B, H, dk, dk), dtype=x.dtype)
            z0 = jnp.zeros((B, H, dk), dtype=x.dtype)

            def step(carry, qkv):
                M, z = carry
                q, k, v = qkv
                sq = _sigma(q)
                denom_q = jnp.sum(sq * z[:, :, None, :], axis=-1, keepdims=True) + EPS
                A_mem = jnp.matmul(sq, M) / denom_q
                scores = jnp.matmul(q, jnp.swapaxes(k, -2, -1)) * inv_sqrt_dk
                scores = jnp.where(causal, -jnp.inf, scores)
                A_dot = jnp.matmul(jax.nn.softmax(scores, axis=-1), v)
                A_s = beta * A_mem + (1.0 - beta) * A_dot
                sk = _sigma(k)
                denom_k = jnp.sum(sk * z[:, :, None, :], axis=-1, keepdims=True) + EPS
                V_prev = jnp.matmul(sk, M) / denom_k
                M_new = M + jnp.einsum('bhtk,bhtv->bhkv', sk, v - V_prev)
                z_new = z + jnp.sum(sk, axis=-2)
                return ((M_new, z_new), A_s)
            (M, z), outs = jax.lax.scan(step, (M0, z0), (Qs, Ks, Vs))
            out = outs.transpose(1, 3, 0, 2, 4).reshape(B, S * SEG, H, dk)
            out = outs.transpose(1, 2, 0, 3, 4).reshape(B, H, T, dk)
            out = out.transpose(0, 2, 1, 3).reshape(B, T, D)
            out = out @ W_o.T
            return (out, M.mean(0), z.mean(0))

        def _reference_tuple_inner(x, W_q, W_k, W_v, W_o, beta_param):
            return _infini_attention(x, W_q, W_k, W_v, W_o, beta_param)
        return _reference_tuple_inner(x, W_q, W_k, W_v, W_o, beta_param)[0]

    def _L0_xattn_ref(query, key, value, Wq, bq, Wk, bk, Wv, bv, Wo, bo):
        import jax, jax.numpy as jnp
        import numpy as np
        D_MODEL = 128
        NUM_HEADS = 16
        D_K = D_MODEL // NUM_HEADS

        def _mha(query, key, value, Wq, bq, Wk, bk, Wv, bv, Wo, bo):
            B, S, D = query.shape
            H, dk = (NUM_HEADS, D_K)

            def split_heads(x):
                return x.reshape(B, S, H, dk).transpose(0, 2, 1, 3)
            Q = split_heads(query @ Wq + bq)
            K = split_heads(key @ Wk + bk)
            V = split_heads(value @ Wv + bv)
            scores = jnp.einsum('bhqd,bhkd->bhqk', Q, K) / jnp.sqrt(jnp.float32(dk)).astype(Q.dtype)
            attn = jax.nn.softmax(scores, axis=-1)
            ctx = jnp.einsum('bhqk,bhkd->bhqd', attn, V)
            ctx = ctx.transpose(0, 2, 1, 3).reshape(B, S, D)
            return ctx @ Wo + bo
        return _mha(query, key, value, Wq, bq, Wk, bk, Wv, bv, Wo, bo)

    def _L0_ffn_ref(x, router_w, gate_up_w, down_w, shared_gate_w, shared_up_w, shared_down_w):
        import jax, jax.numpy as jnp
        import numpy as np
        B, T, C = (4, 128, 128)
        E = 8
        TOP_K = 2
        H = 64
        HS = 256
        b, t, c = x.shape
        n = b * t
        xf = x.reshape(n, c)
        logits = xf @ router_w.T
        top_vals, top_idx = jax.lax.top_k(logits, TOP_K)
        gates = jax.nn.sigmoid(top_vals)
        combine = jnp.zeros((n, E), dtype=x.dtype)
        combine = combine.at[jnp.arange(n)[:, None], top_idx].add(gates)
        gu = jnp.einsum('nc,ecH->enH', xf, gate_up_w)
        gate, up = jnp.split(gu, 2, axis=-1)
        hidden = jax.nn.silu(gate) * up
        expert_out = jnp.einsum('enh,ehc->enc', hidden, down_w)
        moe_out = jnp.einsum('ne,enc->nc', combine, expert_out)
        shared = jax.nn.silu(xf @ shared_gate_w.T) * (xf @ shared_up_w.T) @ shared_down_w.T
        return (moe_out + shared).reshape(b, t, c)

    def _L1_attn_ref(x, wq, wk, wv, wo, head_dirs, scale):
        import jax, jax.numpy as jnp
        import numpy as np
        B, T, C, H = (2, 256, 128, 16)
        b, t, c = x.shape
        h = head_dirs.shape[0]
        hd = c // h
        q3 = (x @ wq).reshape(b, t, h, 3).transpose(0, 2, 1, 3)
        k3 = (x @ wk).reshape(b, t, h, 3).transpose(0, 2, 1, 3)
        v = (x @ wv).reshape(b, t, h, hd).transpose(0, 2, 1, 3)
        q_on_dir = jnp.einsum('bhtd,hd->bht', q3, head_dirs)
        k_on_dir = jnp.einsum('bhtd,hd->bht', k3, head_dirs)
        dot_scores = jnp.einsum('bhtd,bhsd->bhts', q3, k3) * scale
        geo_bias = q_on_dir[..., :, None] * k_on_dir[..., None, :]
        scores = dot_scores + geo_bias
        causal = jnp.tril(jnp.ones((t, t), dtype=bool))
        scores = jnp.where(causal, scores, -jnp.inf)
        attn = jax.nn.softmax(scores, axis=-1)
        out = jnp.einsum('bhts,bhsd->bhtd', attn, v)
        out = out.transpose(0, 2, 1, 3).reshape(b, t, c)
        return out @ wo

    def _L1_xattn_ref(query, key, value, w_q, w_k, w_v, w_o):
        import jax, jax.numpy as jnp
        import numpy as np
        HIDDEN = 128
        HEADS = 16
        HEAD_DIM = 64
        B, Q, _ = query.shape
        Kl = key.shape[1]
        scale = HEAD_DIM ** (-0.5)
        q = (query @ w_q).reshape(B, Q, HEADS, HEAD_DIM).transpose(0, 2, 1, 3)
        k = (key @ w_k).reshape(B, Kl, HEADS, HEAD_DIM).transpose(0, 2, 1, 3)
        v = (value @ w_v).reshape(B, Kl, HEADS, HEAD_DIM).transpose(0, 2, 1, 3)
        scores = jnp.einsum('bhqd,bhkd->bhqk', q, k) * scale
        attn = jax.nn.softmax(scores, axis=-1)
        out = jnp.einsum('bhqk,bhkd->bhqd', attn, v)
        out = out.transpose(0, 2, 1, 3).reshape(B, Q, HEADS * HEAD_DIM)
        return out @ w_o

    def _L1_ffn_ref(x, W_r, W_k, W_v, mu_r, mu_k):
        import jax, jax.numpy as jnp
        import numpy as np
        DIM = 128

        def _reference_tuple_inner(x, W_r, W_k, W_v, mu_r, mu_k):
            B, T, C = x.shape
            x_prev = jnp.concatenate([jnp.zeros((B, 1, C), x.dtype), x[:, :-1, :]], axis=1)
            xr = mu_r * x + (1.0 - mu_r) * x_prev
            xk = mu_k * x + (1.0 - mu_k) * x_prev
            r = jax.nn.sigmoid(jnp.einsum('btc,dc->btd', xr, W_r))
            k = jnp.einsum('btc,dc->btd', xk, W_k)
            k_act = jnp.square(jax.nn.relu(k))
            out = r * jnp.einsum('btc,dc->btd', k_act, W_v)
            new_state = x[:, -1, :]
            return (out, new_state)
        return _reference_tuple_inner(x, W_r, W_k, W_v, mu_r, mu_k)[0]
    x = x + _L0_attn_ref(_layernorm(x, axis=-1), L0_attn_W_q, L0_attn_W_k, L0_attn_W_v, L0_attn_W_o, L0_attn_beta_param)
    x = x + _L0_xattn_ref(_layernorm(x, axis=-1), ctx_1024, ctx_1024, L0_xattn_Wq, L0_xattn_bq, L0_xattn_Wk, L0_xattn_bk, L0_xattn_Wv, L0_xattn_bv, L0_xattn_Wo, L0_xattn_bo)
    x = x + _L0_ffn_ref(_layernorm(x, axis=-1), L0_ffn_router_w, L0_ffn_gate_up_w, L0_ffn_down_w, L0_ffn_shared_gate_w, L0_ffn_shared_up_w, L0_ffn_shared_down_w)
    x = x + _L1_attn_ref(_layernorm(x, axis=-1), L1_attn_wq, L1_attn_wk, L1_attn_wv, L1_attn_wo, L1_attn_head_dirs, L1_attn_scale)
    x = x + _L1_xattn_ref(_layernorm(x, axis=-1), ctx_1024, ctx_1024, L1_xattn_w_q, L1_xattn_w_k, L1_xattn_w_v, L1_xattn_w_o)
    x = x + _L1_ffn_ref(_layernorm(x, axis=-1), L1_ffn_W_r, L1_ffn_W_k, L1_ffn_W_v, L1_ffn_mu_r, L1_ffn_mu_k)
    return x

_drawn_inputs = setup_inputs


def setup_inputs(seed=0):
    import zlib

    import numpy as np

    out = dict(_drawn_inputs(seed))
    spreads = {'L0_attn_beta_param': (0.0, 0.8),
     'L0_xattn_bq': (0.0, 0.448),
     'L0_xattn_bk': (0.0, 0.8),
     'L0_xattn_bv': (0.0, 0.1),
     'L0_xattn_bo': (0.0, 0.1)}
    factors = {'L0_ffn_router_w': 8.0,
     'L0_ffn_gate_up_w': 8.0,
     'L0_ffn_down_w': 8.0,
     'L0_ffn_shared_gate_w': 8.0,
     'L0_ffn_shared_up_w': 8.0,
     'L0_ffn_shared_down_w': 8.0,
     'L1_ffn_W_r': 4.127,
     'L1_ffn_mu_r': 8.0,
     'L1_ffn_mu_k': 3.262}
    for name, (base, spread) in spreads.items():
        noise = np.random.default_rng([zlib.crc32(name.encode()), seed]).standard_normal(out[name].shape)
        drawn = base * np.exp(spread * noise) if base else spread * noise
        out[name] = jnp.asarray(drawn.astype(out[name].dtype))
    for name, factor in factors.items():
        out[name] = (out[name] * factor).astype(out[name].dtype)
    return out
```

```python
from contextlib import ExitStack

import numpy as np

import concourse.bass as bass
from concourse import mybir

F32 = mybir.dt.float32
F32R = mybir.dt.float32r
BF16 = mybir.dt.bfloat16
U32 = mybir.dt.uint32
ALU = mybir.AluOpType
ACT = mybir.ActivationFunctionType
AX = mybir.AxisListType

P = 128
B, S, D = 4, 256, 128
H = 16
QT = S // P
DK = D // H
HD = 64
SEG = 64
NSEG = S // SEG
EXPERTS = 8
GROUP = 4
NG = H // GROUP
STRIP = P // GROUP
BLOCKS = 6
PAIRS = H * HD // P
LN_EPS = 1e-5
MEM_EPS = 1e-6
NEG = -1e30
IN_FLIGHT = 2
ROUNDS = B // IN_FLIGHT

INFINI, CROSS, MOE, GEO, WIDE, FFN = range(6)
LAYERS = 6
NARROW = (INFINI, CROSS, GEO)
CHUNKS = LAYERS * IN_FLIGHT
UNITS = 4 * CHUNKS
SCALE = {INFINI: DK ** -0.5, CROSS: DK ** -0.5, GEO: 1.0, WIDE: HD ** -0.5}

COLUMNS = {
    INFINI: [("q", 512), ("k", 512), ("qc", 128), ("kc", 128), ("v", 128), ("o", 128), ("beta", 1)],
    CROSS: [("q", 512), ("k", 512), ("v", 128), ("o", 128), ("bq", 4), ("bk", 4), ("bv", 1), ("bo", 128)],
    MOE: [("router", 8), ("gate", BLOCKS * P), ("up", BLOCKS * P), ("o", BLOCKS * P)],
    GEO: [("q3", 128), ("k3", 128), ("q", 512), ("k", 512), ("v", 128), ("o", 128)],
    WIDE: [("q", 1024), ("k", 1024), ("v", 1024), ("o", 1024)],
    FFN: [("r", 128), ("k", 128), ("o", 128), ("mu_r", 1), ("mu_k", 1)],
}
CONSTANTS = [("ident", 128), ("masks", 512), ("head_pick", 512), ("expert_pick", 512), ("blocks", 128),
             ("lo_rows", 2), ("iota", 8)]


def offsets(columns):
    at, out = 0, {}
    for name, n in columns:
        out[name] = (at, n)
        at += n
    return out, at


class Tally:

    def __init__(self):
        self.n = {}

    def next(self, name, by=1):
        self.n[name] = self.n.get(name, 0) + by
        return self.n[name]


def schedule():
    steps = []
    for u in range(IN_FLIGHT):
        steps.append(("enter", u, 0))
    for s in range(-2, UNITS + 6):
        def chunk_at(offset):
            c, r = divmod(s - offset, 4)
            return c if r == 0 and 0 <= c < CHUNKS else None

        def unit(i):
            return 0 <= i < UNITS

        def kind(i):
            return (i // 4) // IN_FLIGHT

        def attends(i):
            return unit(i) and kind(i) in (INFINI, CROSS, GEO, WIDE)

        c = chunk_at(6)
        if c is not None and c // IN_FLIGHT < LAYERS - 1:
            steps.append(("scale", c, 0))
            steps.append(("to_columns", c, 0))
        c = chunk_at(-2)
        if c is not None:
            steps.append(("prepare", c, 0))
        if attends(s):
            steps.append(("turn_max", s // 4, s % 4))
        for c in range(IN_FLIGHT):
            if 0 <= s - (4 * c - 1) < NSEG - 1:
                steps.append(("recall", c, s - (4 * c - 1)))
        c = chunk_at(5)
        if c is not None and c // IN_FLIGHT in (INFINI, CROSS, GEO, WIDE):
            steps.append(("merge", c, 0))
        if attends(s + 1):
            steps.append(("maxima", (s + 1) // 4, (s + 1) % 4))
        if attends(s):
            steps.append(("exps", s // 4, s % 4))
        if unit(s + 2):
            steps.append(("project", (s + 2) // 4, (s + 2) % 4))
        c = chunk_at(5)
        if c is not None:
            steps.append(("output", c, 0))
        for c in range(IN_FLIGHT):
            if 0 <= s - (4 * c - 1) < NSEG - 1:
                steps.append(("remember", c, s - (4 * c - 1)))
        if attends(s - 1):
            steps.append(("normalise", (s - 1) // 4, (s - 1) % 4))
        if attends(s):
            steps.append(("values", s // 4, s % 4))
        for c in range(IN_FLIGHT):
            if 0 <= s - (4 * c - 1) < NSEG - 1:
                steps.append(("answer", c, s - (4 * c - 1)))
    return steps


def v_jobs(what, layer, g):
    if what == "prepare":
        return {INFINI: 3, MOE: 2}.get(layer, 0)
    if what == "project":
        return (4, 4, 1, 1)[g] if layer == MOE else 0
    if what == "maxima":
        return {INFINI: 2, GEO: 3}.get(layer, 4)
    if what == "normalise":
        return 1 if layer in NARROW else 2
    if what in ("values", "merge"):
        return int(layer in NARROW)
    if what == "recall":
        return int(g > 0)
    return int(what in ("turn_max", "remember", "answer", "output"))


def a_jobs(what, layer, g):
    if what == "prepare":
        return {INFINI: 1, CROSS: 1, GEO: 2, FFN: 2}.get(layer, 0)
    if what == "project":
        return 1 if layer in NARROW else 3 * (layer == WIDE)
    if what == "exps":
        return 1 if layer == INFINI else 2
    if what in ("values", "merge"):
        return {"values": 1, "merge": 2}[what] * (layer == WIDE)
    return {"enter": 2, "to_columns": 1}.get(what, 0)


def job_numbers(steps, jobs):
    n, after = 0, {}
    for what, c, g in steps:
        n += jobs(what, c // IN_FLIGHT if what != "enter" else -1, g)
        after[what, c, g] = n
    return after


def build(nc, x, ctx_in, tables, constants, out):
    OFF = {}
    WIDTH = {}
    for layer in range(LAYERS):
        OFF[layer], WIDTH[layer] = offsets(COLUMNS[layer])
    CO, CW = offsets(CONSTANTS)
    STEPS = schedule()
    v_after = job_numbers(STEPS, v_jobs)
    a_after = job_numbers(STEPS, a_jobs)

    def columns_after(c):
        return a_after["to_columns", c - IN_FLIGHT, 0] if c >= IN_FLIGHT else a_after["enter", c, 0]

    with ExitStack() as stack:
        def sb(name, shape, dt=F32):
            return stack.enter_context(nc.sbuf_tensor(name, shape, dt))

        def sem(name):
            return stack.enter_context(nc.semaphore(name))

        table = [sb(f"table{i}", [P, WIDTH[i]]) for i in range(LAYERS)]
        consts = sb("consts", [P, CW])

        def W(layer, name):
            a, n = OFF[layer][name]
            return table[layer][:, a:a + n]

        def C(name):
            a, n = CO[name]
            return consts[:, a:a + n]

        ident = C("ident")
        lo_q, lo_k = C("lo_rows")[:, 0:1], C("lo_rows")[:, 1:2]
        ident16 = sb("ident16", [P, P], BF16)
        masks = sb("masks", [P, 4, GROUP, P], BF16)
        head_pick = sb("head_pick", [P, GROUP, P], F32R)
        beta = sb("beta", [P, 1])
        one_less_beta = sb("one_less_beta", [P, 1])
        beta_tanh = sb("beta_tanh", [P, 1])
        one_less_mu = sb("one_less_mu", [P, 2])
        ln_power = sb("ln_power", [P, QT])

        def two(name, shape, dt=F32):
            return [sb(f"{name}{u}", shape, dt) for u in range(IN_FLIGHT)]

        X = two("x", [P, QT, D])
        ctx_rows = two("ctx_rows", [P, QT, D])
        ctxT = two("ctxT", [P, S])
        xn = two("xn", [P, QT, D])
        xnT = two("xnT", [P, S])
        stats = two("stats", [P, QT, 6])
        meanvar = two("meanvar", [P, QT, 2])
        var_eps = two("var_eps", [P, QT])
        rstd = two("rstd", [P, QT])
        V = two("v_ones", [P, QT, H, STRIP])
        q3T = two("q3T", [P, 2, S])
        mixed = two("mixed", [P, QT, D])
        mixedT = two("mixedT", [P, S])
        wide_mixed = sb("wide_mixed", [P, QT, H * HD])
        wide_mixedT = sb("wide_mixedT", [P, PAIRS, S])
        sigT = two("sigT", [P, 2, S])
        sig_e = sb("sig_e", [P, 2, S])
        ktok = two("ktok", [SEG, NSEG - 1, D])
        ktok_e = sb("ktok_e", [SEG, NSEG - 1, D])
        vtok = two("vtok", [SEG, NSEG - 1, D])
        MZ = two("mz", [P, 2, D])
        mz_new = two("mz_new", [P, 2, D])
        told = two("told", [SEG, 2, D])
        v_prev = two("v_prev", [SEG, 2, D])
        recalled = two("recalled", [P, S])
        rec_den = two("rec_den", [P, SEG])
        top8 = two("top8", [P, QT, 8])
        top_at = two("top_at", [P, QT, 8], U32)
        top_atf = two("top_atf", [P, QT, 2])
        gates = two("gates", [P, QT, 2])
        combine = two("combine", [P, QT, 8])
        combine2 = two("combine2", [P, QT, 8])
        logits = two("logits", [P, QT, 8])
        combineT = two("combineT", [P, S])
        gate_tanh = sb("gate_tanh", [P, 2, S])
        hidden_a = sb("hidden_a", [P, S])
        hidden_b = sb("hidden_b", [P, S])
        hidden = [wide_mixed[:].rearrange("p t (k s) -> p (t k) s", s=S)[:, 0:BLOCKS, :], wide_mixedT[:, 0:BLOCKS, :]]
        shifted = q3T
        mixed_in = sigT
        k_relu = two("k_relu", [P, S])
        k_act = two("k_act", [P, S])
        r_tanh = two("r_tanh", [P, QT, D])
        gated = two("gated", [P, QT, D])

        Y = [sb(f"y{i}", [P, 2, S]) for i in range(2)]
        Yhi = [sb(f"yhi{i}", [P, 2, S], F32R) for i in range(2)]
        QZ = [sb(f"qz{i}", [P, GROUP, S], F32R) for i in range(2)]
        KZ = [sb(f"kz{i}", [P, S], F32R) for i in range(2)]
        QW = [sb(f"qw{i}", [P, 2, 2, 2, S], F32R) for i in range(2)]
        KW = [sb(f"kw{i}", [P, 2, 2, S], F32R) for i in range(2)]
        VW = [sb(f"vw{i}", [P, QT, GROUP, HD + 2]) for i in range(3)]
        max_neg = sb("max_neg", [P, QT, GROUP])
        NM = sb("nm", [P, S], F32R)
        PT = sb("pt", [P, QT, GROUP, S])
        raw = sb("raw", [P, S])
        raw_wide = sb("raw_wide", [HD + 2, GROUP, S])
        rec = sb("rec", [P, QT, GROUP])

        VSLOTS, ASLOTS = 4, 2
        psv = [stack.enter_context(nc.psum_tensor(f"psv{i}", [P, 512], F32)) for i in range(VSLOTS)]
        psa = [stack.enter_context(nc.psum_tensor(f"psa{i}", [P, 1024], F32)) for i in range(ASLOTS)]

        table_loaded = [sem(f"table_loaded{i}") for i in range(LAYERS)]
        consts_loaded = sem("consts_loaded")
        vector_consts = sem("vector_consts")
        pool_consts = sem("pool_consts")
        scalar_consts = sem("scalar_consts")
        x_loaded = sem("x_loaded")
        stored = sem("stored")
        psv_ready = sem("psv_ready")
        psv_taken = sem("psv_taken")
        psa_ready = sem("psa_ready")
        psa_taken = sem("psa_taken")
        split_done = sem("split_done")
        var_found = sem("var_found")
        var_shifted = sem("var_shifted")
        rstd_found = sem("rstd_found")
        xn_written = sem("xn_written")
        clipped = sem("clipped")
        clip_exp = sem("clip_exp")
        top_found = sem("top_found")
        top_gated = sem("top_gated")
        gate_done = sem("gate_done")
        mixes_done = sem("mixes_done")
        relu_done = sem("relu_done")
        x_final = sem("x_final")
        dve_wrote = sem("dve_wrote")
        round_over = {e: sem(f"{e}_round_over") for e in ("pe", "dve", "act", "pool")}
        next_round = sem("next_round")
        ROUND_SEMS = [x_loaded, stored, psv_ready, psv_taken, psa_ready, psa_taken, split_done, var_found,
                      var_shifted, rstd_found, xn_written, clipped, clip_exp, top_found, top_gated,
                      gate_done, mixes_done, relu_done, x_final, dve_wrote, *round_over.values()]
        POOL_CONSTS, VECTOR_CONSTS = 8, 19

        block = stack.enter_context(nc.Block())

        @block.sync
        def _(sp):
            def load_x(it):
                for u in range(IN_FLIGHT):
                    b = it * IN_FLIGHT + u
                    sp.dma_start(X[u][:], x[bass.ds(b, 1), :, :].rearrange("b (t p) d -> p (b t) d", p=P)).then_inc(x_loaded, 16)
                    sp.dma_start(ctx_rows[u][:], ctx_in[bass.ds(b, 1), :, :].rearrange("b (t p) d -> p (b t) d", p=P)).then_inc(x_loaded, 16)

            sp.dma_start(consts[:], constants).then_inc(consts_loaded, 16)
            for i in range(LAYERS):
                sp.dma_start(table[i][:], tables[i]).then_inc(table_loaded[i], 16)
            with sp.Fori(0, ROUNDS) as it:
                load_x(it)
                for u in range(IN_FLIGHT):
                    sp.wait_ge(x_final, u + 1)
                    b = it * IN_FLIGHT + u
                    sp.dma_start(out[bass.ds(b, 1), :, :].rearrange("b (t p) d -> p (b t) d", p=P), X[u][:]).then_inc(stored, 16)
                sp.wait_ge(stored, 16 * IN_FLIGHT)
                for s in round_over.values():
                    sp.wait_ge(s, 1)
                for s in ROUND_SEMS:
                    sp.sem_clear(s)
                sp.nop().then_inc(next_round, 1)

        @block.tensor
        def _(pe):
            def a_slot(seen):
                n = seen.next("psa")
                if n > ASLOTS:
                    pe.wait_ge(psa_taken, n - ASLOTS)
                return psa[(n - 1) % ASLOTS]

            def v_slot(seen):
                n = seen.next("psv")
                if n > VSLOTS:
                    pe.wait_ge(psv_taken, n - VSLOTS)
                return psv[(n - 1) % VSLOTS]

            def mm(o, l, r, start=True, stop=True):
                return pe.matmul(o, l, r, start=start, stop=stop)

            def turn(o, i, idn):
                return pe.transpose(o, i, idn)

            def enter(seen, u):
                if u == 0:
                    pe.wait_ge(consts_loaded, 16)
                pe.wait_ge(x_loaded, 32 * IN_FLIGHT)
                o = a_slot(seen)
                for t in range(QT):
                    last = turn(o[:, t * P:(t + 1) * P], ctx_rows[u][:, t, :], ident)
                last.then_inc(psa_ready, 1)
                to_columns(seen, u)

            def to_columns(seen, u):
                pe.wait_ge(xn_written, seen.next("xn_written"))
                o = a_slot(seen)
                for t in range(QT):
                    last = turn(o[:, t * P:(t + 1) * P], xn[u][:, t, :], ident)
                last.then_inc(psa_ready, 1)

            def prepare(seen, layer, u, c):
                pe.wait_ge(psa_taken, columns_after(c))
                if u == 0:
                    pe.wait_ge(table_loaded[layer], 16)
                if layer == INFINI and u == 0:
                    pe.wait_ge(vector_consts, VECTOR_CONSTS)
                    pe.wait_ge(pool_consts, POOL_CONSTS)
                src = ctxT[u] if layer == CROSS else xnT[u]
                if layer in NARROW:
                    o = a_slot(seen)
                    for t in range(QT):
                        last = mm(o[:, t * P:(t + 1) * P], src[:, t * P:(t + 1) * P], W(layer, "v"))
                    last.then_inc(psa_ready, 1)
                if layer == GEO:
                    o = a_slot(seen)
                    mm(o[:, 0:S], W(GEO, "q3"), xnT[u][:])
                    mm(o[:, S:2 * S], W(GEO, "k3"), xnT[u][:]).then_inc(psa_ready, 1)
                if layer == INFINI:
                    o = v_slot(seen)
                    mm(o[:, 0:S], W(INFINI, "qc"), xnT[u][:])
                    mm(o[:, S:2 * S], W(INFINI, "kc"), xnT[u][:]).then_inc(psv_ready, 1)
                    for name in ("kc", "v"):
                        o = v_slot(seen)
                        for s in range(NSEG - 1):
                            last = mm(o[0:SEG, s * D:(s + 1) * D], xnT[u][:, s * SEG:(s + 1) * SEG], W(INFINI, name))
                        last.then_inc(psv_ready, 1)
                if layer == MOE:
                    o = v_slot(seen)
                    for t in range(QT):
                        last = mm(o[:, 8 * t:8 * t + 8], xnT[u][:, t * P:(t + 1) * P], W(MOE, "router"))
                    last.then_inc(psv_ready, 1)
                    pe.wait_ge(psv_taken, v_after["prepare", c, 0] - 1)
                    o = v_slot(seen)
                    for t in range(QT):
                        last = turn(o[0:8, t * P:(t + 1) * P], combine[u][:, t, :], ident)
                    last.then_inc(psv_ready, 1)
                if layer == FFN:
                    pe.wait_ge(mixes_done, seen.next("mixes_done"))
                    o = a_slot(seen)
                    mm(o[:, 0:S], W(FFN, "k"), mixed_in[u][:, 1, :]).then_inc(psa_ready, 1)
                    o = a_slot(seen)
                    for t in range(QT):
                        last = mm(o[:, t * D:(t + 1) * D], mixed_in[u][:, 0, t * P:(t + 1) * P], W(FFN, "r"))
                    last.then_inc(psa_ready, 1)

            def project(seen, layer, u, c, g, i):
                if layer in NARROW:
                    if layer == GEO and g == 0:
                        pe.wait_ge(psa_taken, a_after["prepare", c, 0])
                    qs = q3T[u][:, 0, :] if layer == GEO else xnT[u][:]
                    ks = q3T[u][:, 1, :] if layer == GEO else (ctxT[u][:] if layer == CROSS else xnT[u][:])
                    o = a_slot(seen)
                    mm(o[:, 0:S], W(layer, "q")[:, g * P:(g + 1) * P], qs)
                    mm(o[:, S:2 * S], W(layer, "k")[:, g * P:(g + 1) * P], ks).then_inc(psa_ready, 1)
                if layer == WIDE:
                    o = a_slot(seen)
                    for t in range(QT):
                        last = mm(o[:, t * S:(t + 1) * S], ctxT[u][:, t * P:(t + 1) * P],
                                  W(WIDE, "v")[:, g * S:(g + 1) * S])
                    last.then_inc(psa_ready, 1)
                    for p in range(2):
                        w = (2 * g + p) * P
                        o = a_slot(seen)
                        mm(o[:, 0:S], W(WIDE, "q")[:, w:w + P], xnT[u][:])
                        mm(o[:, S:2 * S], W(WIDE, "k")[:, w:w + P], ctxT[u][:]).then_inc(psa_ready, 1)
                if layer == MOE:
                    if g == 0:
                        pe.wait_ge(psv_taken, v_after["prepare", c, 0])
                    for blk in ([0, 1], [2, 3], [4], [5])[g]:
                        o = v_slot(seen)
                        w = slice(blk * P, (blk + 1) * P)
                        mm(o[:, 0:S], W(MOE, "gate")[:, w], xnT[u][:])
                        mm(o[:, S:2 * S], W(MOE, "up")[:, w], xnT[u][:]).then_inc(psv_ready, 1)
                        if blk < EXPERTS // 2:
                            o = v_slot(seen)
                            mm(o[:, 0:S], C("expert_pick")[:, w], combineT[u][:]).then_inc(psv_ready, 1)

            def score_terms(layer, i):
                if layer in NARROW:
                    return lambda j, q: [(QZ[i % 2][:, j, q], KZ[i % 2][:])]
                w, k = QW[i % 2], KW[i % 2]
                return lambda j, q: [(w[:, 0, j // 2, j % 2, q], k[:, 0, j // 2, :]),
                                     (w[:, 0, j // 2, j % 2, q], k[:, 1, j // 2, :]),
                                     (w[:, 1, j // 2, j % 2, q], k[:, 0, j // 2, :])]

            def maxima(seen, layer, u, c, g, i):
                pe.wait_ge(split_done, seen.next("split", 2 if layer == WIDE else 1))
                terms = score_terms(layer, i)
                kind = 0 if layer == INFINI else 1
                for t in range(QT):
                    q = slice(t * P, (t + 1) * P)
                    if layer == INFINI or (layer == GEO and t == 0):
                        o = v_slot(seen)
                        mm(o[:], ident16[:], masks[:, 2 * kind, :, :], stop=False)
                        for j in range(GROUP):
                            (qa, ka), = terms(j, q)
                            last = mm(o[:, j * P:(j + 1) * P], qa, ka[:, q], start=False, stop=j == GROUP - 1)
                        last.then_inc(psv_ready, 1)
                    else:
                        for p in range(2):
                            o = v_slot(seen)
                            for h in range(2):
                                tt = terms(2 * p + h, q)
                                for n, (qa, ka) in enumerate(tt):
                                    last = mm(o[:, h * S:(h + 1) * S], qa, ka, start=n == 0,
                                              stop=n == len(tt) - 1 and layer != GEO)
                                if layer == GEO:
                                    last = mm(o[:, h * S + P:(h + 1) * S], ident16[:], masks[:, 2, 0, :],
                                              start=False)
                            last.then_inc(psv_ready, 1)

            def turn_max(seen, layer, u, c, g, i):
                pe.wait_ge(psv_taken, v_after["maxima", c, g])
                o = v_slot(seen)
                for t in range(QT):
                    last = turn(o[0:GROUP, t * P:(t + 1) * P], max_neg[:, t, :], ident)
                last.then_inc(psv_ready, 1)

            def exps(seen, layer, u, c, g, i):
                pe.wait_ge(psv_taken, v_after["turn_max", c, g])
                terms = score_terms(layer, i)
                nm = NM
                if layer == INFINI:
                    o = a_slot(seen)
                    for t in range(QT):
                        q = slice(t * P, (t + 1) * P)
                        c0 = t * GROUP * P
                        mm(o[:, c0:c0 + GROUP * P], ident16[:], masks[:, 1, :, :], stop=False)
                        for j in range(GROUP):
                            (qa, ka), = terms(j, q)
                            mm(o[:, c0 + j * P:c0 + (j + 1) * P], ka[:, q], qa, start=False, stop=False)
                            last = mm(o[:, c0 + j * P:c0 + (j + 1) * P], head_pick[:, j, :], nm[:, q],
                                      start=False, stop=j == GROUP - 1)
                    last.then_inc(psa_ready, 1)
                    return
                for t in range(QT):
                    k = slice(t * P, (t + 1) * P)
                    o = a_slot(seen)
                    if layer == GEO and t == 1:
                        mm(o[:, 0:GROUP * P], ident16[:], masks[:, 3, :, :], stop=False)
                        for j in range(GROUP):
                            (qa, ka), = terms(j, k)
                            mm(o[:, j * P:(j + 1) * P], ka[:, k], qa, start=False, stop=False)
                            last = mm(o[:, j * P:(j + 1) * P], head_pick[:, j, :], nm[:, k],
                                      start=False, stop=j == GROUP - 1)
                    else:
                        for j in range(GROUP):
                            oj = o[:, j * S:(j + 1) * S]
                            for n, (qa, ka) in enumerate(terms(j, slice(0, S))):
                                mm(oj, ka[:, k], qa, start=n == 0, stop=False)
                            last = mm(oj, head_pick[:, j, :], nm[:], start=False, stop=layer != GEO)
                            if layer == GEO:
                                last = mm(o[:, j * S:j * S + P], ident16[:], masks[:, 3, 0, :], start=False)
                    last.then_inc(psa_ready, 1)

            def values(seen, layer, u, c, g, i):
                pt = PT
                if layer in NARROW:
                    if g == 0:
                        pe.wait_ge(psa_taken, a_after["prepare", c, 0])
                    o = v_slot(seen)
                    for t in range(QT):
                        pe.wait_ge(psa_taken, a_after["exps", c, g] - (1 - t if layer != INFINI else 0))
                        q = slice(t * P, (t + 1) * P) if layer == INFINI else slice(t * P if layer == GEO else 0, S)
                        for j in range(GROUP):
                            last = mm(o[j * STRIP:(j + 1) * STRIP, q], V[u][:, t, GROUP * g + j, :], pt[:, t, j, q],
                                      start=t == 0 or layer == INFINI, stop=t == QT - 1 or layer == INFINI)
                    last.then_inc(psv_ready, 1)
                else:
                    pe.wait_ge(psa_taken, a_after["exps", c, g])
                    o = a_slot(seen)
                    for j in range(GROUP):
                        for t in range(QT):
                            last = mm(o[0:HD + 2, j * S:(j + 1) * S], VW[i % 3][:, t, j, :], pt[:, t, j, :],
                                      start=t == 0, stop=t == QT - 1)
                    last.then_inc(psa_ready, 1)

            def normalise(seen, layer, u, c, g, i):
                if layer in NARROW:
                    pe.wait_ge(psv_taken, v_after["values", c, g])
                    o = v_slot(seen)
                    for t in range(QT):
                        last = turn(o[:, t * P:(t + 1) * P], raw[:, t * P:(t + 1) * P], ident)
                    last.then_inc(psv_ready, 1)
                else:
                    pe.wait_ge(psa_taken, a_after["values", c, g])
                    for t in range(QT):
                        o = v_slot(seen)
                        for j in range(GROUP):
                            last = turn(o[:, j * (HD + 2):(j + 1) * (HD + 2)], raw_wide[:, j, t * P:(t + 1) * P],
                                        ident[0:HD + 2, 0:HD + 2])
                        last.then_inc(psv_ready, 1)

            def merge(seen, layer, u, c):
                if layer in NARROW:
                    pe.wait_ge(psv_taken, v_after["normalise", c, NG - 1])
                    o = v_slot(seen)
                    for t in range(QT):
                        last = turn(o[:, t * P:(t + 1) * P], mixed[u][:, t, :], ident)
                    last.then_inc(psv_ready, 1)
                if layer == WIDE:
                    pe.wait_ge(psv_taken, v_after["normalise", c, NG - 1])
                    for half in range(2):
                        o = a_slot(seen)
                        for p in range(4):
                            for t in range(QT):
                                c0 = (4 * half + p) * P
                                last = turn(o[:, p * S + t * P:p * S + (t + 1) * P], wide_mixed[:, t, c0:c0 + P], ident)
                        last.then_inc(psa_ready, 1)

            def output(seen, layer, u, c):
                if layer in NARROW:
                    pe.wait_ge(psv_taken, v_after["merge", c, 0])
                    parts = [mixedT[u][:]]
                if layer == WIDE:
                    pe.wait_ge(psa_taken, a_after["merge", c, 0])
                    parts = [wide_mixedT[:, p, :] for p in range(PAIRS)]
                if layer == MOE:
                    pe.wait_ge(psv_taken, v_after["project", c, 3])
                    parts = [hidden[u][:, k, :] for k in range(BLOCKS)]
                if layer == FFN:
                    pe.wait_ge(psa_taken, a_after["prepare", c, 0])
                    parts = [k_act[u][:]]
                o = v_slot(seen)
                for t in range(QT):
                    for n, part in enumerate(parts):
                        last = mm(o[:, t * D:(t + 1) * D], part[:, t * P:(t + 1) * P],
                                  W(layer, "o")[:, n * D:(n + 1) * D], start=n == 0, stop=n == len(parts) - 1)
                last.then_inc(psv_ready, 1)

            def recall(seen, u, s):
                if s == 0:
                    return
                pe.wait_ge(psv_taken, v_after["remember", u, s - 1])
                o = v_slot(seen)
                mm(o[0:SEG, 0:2 * D], sigT[u][:, 1, s * SEG:(s + 1) * SEG], MZ[u][:, :, :]).then_inc(psv_ready, 1)

            def remember(seen, u, s):
                pe.wait_ge(psv_taken, v_after["recall", u, s] if s else v_after["prepare", u, 0])
                o = v_slot(seen)
                mm(o[:, 0:2 * D], ktok[u][:, s, :], told[u][:, :, :]).then_inc(psv_ready, 1)

            def answer(seen, u, s):
                pe.wait_ge(psv_taken, v_after["remember", u, s])
                o = v_slot(seen)
                q = sigT[u][:, 0, (s + 1) * SEG:(s + 2) * SEG]
                mm(o[:, 0:SEG], MZ[u][:, 0, :], q)
                mm(o[:, SEG:2 * SEG], MZ[u][:, 1, :], q).then_inc(psv_ready, 1)

            with pe.Fori(0, ROUNDS) as it:
                seen = Tally()
                for what, c, g in STEPS:
                    layer, u = divmod(c, IN_FLIGHT)
                    i = 4 * c + g
                    if what == "enter":
                        enter(seen, c)
                    elif what == "to_columns":
                        to_columns(seen, u)
                    elif what == "prepare":
                        prepare(seen, layer, u, c)
                    elif what == "project":
                        project(seen, layer, u, c, g, i)
                    elif what == "maxima":
                        maxima(seen, layer, u, c, g, i)
                    elif what == "turn_max":
                        turn_max(seen, layer, u, c, g, i)
                    elif what == "exps":
                        exps(seen, layer, u, c, g, i)
                    elif what == "values":
                        values(seen, layer, u, c, g, i)
                    elif what == "normalise":
                        normalise(seen, layer, u, c, g, i)
                    elif what == "merge":
                        merge(seen, layer, u, c)
                    elif what == "output":
                        output(seen, layer, u, c)
                    elif what == "recall":
                        recall(seen, u, g)
                    elif what == "remember":
                        remember(seen, u, g)
                    elif what == "answer":
                        answer(seen, u, g)
                pe.drain().then_inc(round_over["pe"], 1)
                pe.wait_ge(next_round, it + 1)

        @block.scalar
        def _(act):
            def a_job(seen):
                n = seen.next("psa")
                act.wait_ge(psa_ready, n)
                return psa[(n - 1) % ASLOTS]

            act.wait_ge(table_loaded[INFINI], 16)
            act.activation(beta_tanh[:], W(INFINI, "beta"), ACT.Tanh, scale=0.5).then_inc(scalar_consts, 1)

            def to_columns(seen, u):
                o = a_job(seen)
                act.activation(xnT[u][:], o[:, 0:S], ACT.Copy).then_inc(psa_taken, 1)

            def prepare(seen, layer, u, c):
                if layer in NARROW:
                    if layer == INFINI and u == 0:
                        act.wait_ge(vector_consts, VECTOR_CONSTS)
                    o = a_job(seen)
                    for t in range(QT):
                        last = act.activation(V[u][:, t, :, 0:DK], o[:, t * P:(t + 1) * P].rearrange("p (h d) -> p h d", d=DK),
                                              ACT.Copy)
                    last.then_inc(psa_taken, 1)
                if layer == GEO:
                    o = a_job(seen)
                    act.activation(q3T[u][:].rearrange("p a s -> p (a s)"), o[:, 0:2 * S], ACT.Copy).then_inc(psa_taken, 1)
                if layer == INFINI:
                    act.wait_ge(clipped, seen.next("clipped"))
                    act.activation(sig_e[:], sig_e[:], ACT.Exp).then_inc(clip_exp, 1)
                    act.wait_ge(clipped, seen.next("clipped"))
                    act.activation(ktok_e[:], ktok_e[:], ACT.Exp).then_inc(clip_exp, 1)
                if layer == MOE:
                    act.wait_ge(top_found, seen.next("top_found"))
                    act.activation(gates[u][:], top8[u][:, :, 0:2], ACT.Tanh, scale=0.5).then_inc(top_gated, 1)
                if layer == FFN:
                    o = a_job(seen)
                    act.activation(k_relu[u][:], o[:, 0:S], ACT.Relu).then_inc(relu_done, 1)
                    act.wait_ge(relu_done, seen.next("relu_done"))
                    act.activation(k_act[u][:], k_relu[u][:], ACT.Square).then_inc(psa_taken, 1)
                    o = a_job(seen)
                    act.activation(r_tanh[u][:].rearrange("p t d -> p (t d)"), o[:, 0:QT * D], ACT.Tanh,
                                   scale=0.5).then_inc(psa_taken, 1)

            def write_y(seen, layer, g):
                n = seen.next("y")
                o = a_job(seen)
                y, yhi = Y[n % 2], Yhi[n % 2]
                if n > 2:
                    act.wait_ge(split_done, n - 2)
                if layer == CROSS:
                    for k, name in enumerate(("bq", "bk")):
                        bias = W(CROSS, name)[:, g:g + 1]
                        act.activation(y[:, k, :], o[:, k * S:(k + 1) * S], ACT.Identity, bias=bias)
                        last = act.activation(yhi[:, k, :], o[:, k * S:(k + 1) * S], ACT.Identity, bias=bias)
                    last.then_inc(psa_taken, 1)
                else:
                    act.activation(y[:].rearrange("p k s -> p (k s)"), o[:, 0:2 * S], ACT.Copy)
                    act.activation(yhi[:].rearrange("p k s -> p (k s)"), o[:, 0:2 * S], ACT.Copy).then_inc(psa_taken, 1)

            def project(seen, layer, u, c, g, i):
                if layer in NARROW:
                    if layer == CROSS and g == 0 and u == 0:
                        act.wait_ge(table_loaded[CROSS], 16)
                    write_y(seen, layer, g)
                if layer == WIDE:
                    o = a_job(seen)
                    for t in range(QT):
                        last = act.activation(VW[i % 3][:, t, :, 0:HD], o[:, t * S:(t + 1) * S].rearrange("p (h d) -> p h d", d=HD),
                                              ACT.Copy)
                    last.then_inc(psa_taken, 1)
                    for p in range(2):
                        write_y(seen, layer, g)
                if layer == MOE:
                    for blk in ([0, 1], [2, 3], [4], [5])[g]:
                        job = v_after["project", c, g] - v_jobs("project", MOE, g) + (2 * (blk % 2) if g < 2 else 0) + 1
                        act.wait_ge(psv_ready, job)
                        n = seen.next("gate")
                        if n > 2:
                            act.wait_ge(psv_taken, job - 1)
                        act.activation(gate_tanh[:, n % 2, :], psv[(job - 1) % VSLOTS][:, 0:S], ACT.Tanh,
                                       scale=0.5).then_inc(gate_done, 1)

            def exps(seen, layer, u, c, g, i):
                pt = PT
                if layer == INFINI:
                    o = a_job(seen)
                    for t in range(QT):
                        last = act.activation(pt[:, t, :, t * P:(t + 1) * P],
                                              o[:, t * GROUP * P:(t + 1) * GROUP * P].rearrange("p (j q) -> p j q", j=GROUP),
                                              ACT.Exp, scale=SCALE[layer])
                    last.then_inc(psa_taken, 1)
                    return
                for t in range(QT):
                    o = a_job(seen)
                    if layer == GEO and t == 1:
                        act.activation(pt[:, 1, :, P:S], o[:, 0:GROUP * P].rearrange("p (j q) -> p j q", j=GROUP),
                                       ACT.Exp, scale=SCALE[layer]).then_inc(psa_taken, 1)
                    else:
                        act.activation(pt[:, t, :, :].rearrange("p j q -> p (j q)"), o[:],
                                       ACT.Exp, scale=SCALE[layer]).then_inc(psa_taken, 1)

            def values(seen, layer, u, c, g, i):
                if layer == WIDE:
                    o = a_job(seen)
                    act.activation(raw_wide[:].rearrange("p j q -> p (j q)"), o[0:HD + 2, :], ACT.Copy).then_inc(psa_taken, 1)

            def merge(seen, layer, u, c):
                if layer == WIDE:
                    for half in range(2):
                        o = a_job(seen)
                        act.activation(wide_mixedT[:, 4 * half:4 * half + 4, :].rearrange("p k s -> p (k s)"), o[:],
                                       ACT.Copy).then_inc(psa_taken, 1)

            with act.Fori(0, ROUNDS) as it:
                seen = Tally()
                for what, c, g in STEPS:
                    layer, u = divmod(c, IN_FLIGHT)
                    i = 4 * c + g
                    if what == "enter":
                        o = a_job(seen)
                        act.activation(ctxT[c][:], o[:, 0:S], ACT.Copy).then_inc(psa_taken, 1)
                        to_columns(seen, c)
                    elif what == "to_columns":
                        to_columns(seen, u)
                    elif what == "prepare":
                        prepare(seen, layer, u, c)
                    elif what == "project":
                        project(seen, layer, u, c, g, i)
                    elif what == "exps":
                        exps(seen, layer, u, c, g, i)
                    elif what == "values":
                        values(seen, layer, u, c, g, i)
                    elif what == "merge":
                        merge(seen, layer, u, c)
                act.nop().then_inc(round_over["act"], 1)
                act.wait_ge(next_round, it + 1)

        @block.gpsimd
        def _(pool):
            for tile in (*QZ, *QW, NM):
                pool.memset(tile[:].bitcast(F32), 0.0).then_inc(pool_consts, 1)
            for u in range(IN_FLIGHT):
                pool.memset(combineT[u][:], 0.0).then_inc(pool_consts, 1)
            pool.memset(ln_power[:], -0.5).then_inc(pool_consts, 1)
            pool.wait_ge(pool_consts, POOL_CONSTS)
            with pool.Fori(0, ROUNDS) as it:
                seen = Tally()
                for what, c, g in STEPS:
                    u = c % IN_FLIGHT
                    if what == "enter" or (what == "output" and c // IN_FLIGHT < LAYERS - 1):
                        n = seen.next("norm")
                        pool.wait_ge(var_found, n)
                        pool.tensor_scalar(var_eps[u][:], meanvar[u][:, :, 1], LN_EPS, None, ALU.add).then_inc(var_shifted, 1)
                        pool.wait_ge(var_shifted, n)
                        pool.tensor_tensor(rstd[u][:], var_eps[u][:], ln_power[:], ALU.pow).then_inc(rstd_found, 1)
                pool.nop().then_inc(round_over["pool"], 1)
                pool.wait_ge(next_round, it + 1)

        @block.vector
        def _(dve):
            def v_job(seen):
                n = seen.next("psv")
                dve.wait_ge(psv_ready, n)
                return psv[(n - 1) % VSLOTS]

            def linked(seen, ins):
                ins.then_inc(dve_wrote, 1)
                dve.wait_ge(dve_wrote, seen.next("dve_wrote"))

            for u in range(IN_FLIGHT):
                dve.memset(V[u][:], 1.0).then_inc(vector_consts, 1)
                dve.memset(told[u][:, 1, :], 1.0).then_inc(vector_consts, 1)
                dve.memset(recalled[u][:, 0:SEG], 0.0).then_inc(vector_consts, 1)
            for t in VW:
                dve.memset(t[:, :, :, HD:HD + 2], 1.0).then_inc(vector_consts, 1)
            dve.wait_ge(consts_loaded, 16)
            dve.tensor_copy(ident16[:], ident).then_inc(vector_consts, 1)
            for k in range(4):
                m = C("masks")[:, k * P:(k + 1) * P]
                dve.tensor_copy(masks[:, k, :, :], m[:, None, :].to_broadcast([P, GROUP, P])).then_inc(vector_consts, 1)
            dve.tensor_copy(head_pick[:].rearrange("p j k -> p (j k)"), C("head_pick")).then_inc(vector_consts, 1)
            dve.wait_ge(table_loaded[FFN], 16)
            dve.tensor_scalar(one_less_mu[:, 0:1], W(FFN, "mu_r"), -1.0, 1.0, ALU.mult, ALU.add).then_inc(vector_consts, 1)
            dve.tensor_scalar(one_less_mu[:, 1:2], W(FFN, "mu_k"), -1.0, 1.0, ALU.mult, ALU.add).then_inc(vector_consts, 1)
            dve.wait_ge(scalar_consts, 1)
            dve.tensor_scalar(beta[:], beta_tanh[:], 0.5, 0.5, ALU.mult, ALU.add).then_inc(vector_consts, 1)
            dve.tensor_scalar(one_less_beta[:], beta_tanh[:], -0.5, 0.5, ALU.mult, ALU.add).then_inc(vector_consts, 1)
            dve.wait_ge(vector_consts, VECTOR_CONSTS)
            dve.wait_ge(pool_consts, POOL_CONSTS)

            def norm_stats(seen, u):
                for t in range(QT):
                    last = dve.bn_stats(stats[u][:, t, :], X[u][:, t, :])
                linked(seen, last)
                for t in range(QT):
                    last = dve.bn_aggr(meanvar[u][:, t, :], stats[u][:, t, :])
                last.then_inc(var_found, 1)

            def scale(seen, u):
                dve.wait_ge(rstd_found, seen.next("rstd_found"))
                for t in range(QT):
                    last = dve.tensor_scalar(xn[u][:, t, :], X[u][:, t, :], meanvar[u][:, t, 0:1], rstd[u][:, t:t + 1],
                                             ALU.subtract, ALU.mult)
                last.then_inc(xn_written, 1)

            def prepare(seen, layer, u, c):
                if layer == INFINI:
                    o1 = v_job(seen)
                    o1 = o1[:, 0:2 * S].rearrange("p (k s) -> p k s", k=2)
                    dve.tensor_scalar(sig_e[:], o1, 0.0, None, ALU.min).then_inc(clipped, 1)
                    o2 = v_job(seen)
                    o2 = o2[0:SEG, 0:(NSEG - 1) * D].rearrange("p (s d) -> p s d", d=D)
                    dve.tensor_scalar(ktok_e[:], o2, 0.0, None, ALU.min).then_inc(clipped, 1)
                    dve.wait_ge(clip_exp, seen.next("clip_exp"))
                    dve.scalar_tensor_tensor(out=sigT[u][:], in0=o1, scalar=0.0, in1=sig_e[:],
                                             op0=ALU.max, op1=ALU.add).then_inc(psv_taken, 1)
                    dve.wait_ge(clip_exp, seen.next("clip_exp"))
                    dve.scalar_tensor_tensor(out=ktok[u][:], in0=o2, scalar=0.0, in1=ktok_e[:],
                                             op0=ALU.max, op1=ALU.add).then_inc(psv_taken, 1)
                    o3 = v_job(seen)
                    o3 = o3[0:SEG, 0:(NSEG - 1) * D].rearrange("p (s d) -> p s d", d=D)
                    dve.tensor_copy(vtok[u][:], o3)
                    dve.tensor_copy(told[u][:, 0, :], o3[:, 0, :]).then_inc(psv_taken, 1)
                if layer == MOE:
                    o = v_job(seen)
                    linked(seen, dve.tensor_copy(logits[u][:].rearrange("p t e -> p (t e)"), o[:, 0:8 * QT]))
                    for t in range(QT):
                        last = dve.max(top8[u][:, t, :], logits[u][:, t, :])
                    n = seen.next("top_found")
                    last.then_inc(top_found, 1)
                    dve.wait_ge(top_found, n)
                    for t in range(QT):
                        last = dve.max_index(top_at[u][:, t, :], top8[u][:, t, :], logits[u][:, t, :])
                    linked(seen, last)
                    linked(seen, dve.tensor_copy(top_atf[u][:], top_at[u][:, :, 0:2]))
                    dve.wait_ge(top_gated, seen.next("top_gated"))
                    linked(seen, dve.tensor_scalar(gates[u][:], gates[u][:], 1.0, None, ALU.add))
                    for t in range(QT):
                        for k, dst in enumerate((combine, combine2)):
                            last = dve.tensor_scalar(dst[u][:, t, :], C("iota"), top_atf[u][:, t, k:k + 1],
                                                     gates[u][:, t, k:k + 1], ALU.is_equal, ALU.mult)
                    linked(seen, last)
                    dve.tensor_tensor(combine[u][:], combine[u][:], combine2[u][:], ALU.add).then_inc(psv_taken, 1)
                    o = v_job(seen)
                    dve.tensor_copy(combineT[u][0:EXPERTS, :], o[0:EXPERTS, 0:S]).then_inc(psv_taken, 1)
                if layer == FFN:
                    dve.wait_ge(psa_taken, columns_after(c))
                    for k in range(2):
                        dve.memset(shifted[u][:, k, 0:1], 0.0)
                        last = dve.tensor_scalar(shifted[u][:, k, 1:S], xnT[u][:, 0:S - 1], one_less_mu[:, k:k + 1],
                                                 None, ALU.mult)
                    linked(seen, last)
                    for k, mu in enumerate(("mu_r", "mu_k")):
                        last = dve.scalar_tensor_tensor(out=mixed_in[u][:, k, :], in0=xnT[u][:], scalar=W(FFN, mu),
                                                        in1=shifted[u][:, k, :], op0=ALU.mult, op1=ALU.add)
                    last.then_inc(mixes_done, 1)

            def project(seen, layer, u, c, g, i):
                if layer in NARROW:
                    n = seen.next("y")
                    dve.wait_ge(psa_taken, a_after["project", c, g])
                    y, yhi = Y[n % 2], Yhi[n % 2].bitcast(F32)
                    dve.scalar_tensor_tensor(out=KZ[i % 2][:], in0=yhi[:, 1, :], scalar=lo_k, in1=y[:, 1, :],
                                             op0=ALU.mult, op1=ALU.add)
                    for j in range(GROUP):
                        r = slice(j * STRIP, (j + 1) * STRIP)
                        last = dve.scalar_tensor_tensor(out=QZ[i % 2][r, j, :], in0=yhi[r, 0, :], scalar=lo_q[r, :],
                                                        in1=y[r, 0, :], op0=ALU.mult, op1=ALU.add)
                    last.then_inc(split_done, 1)
                if layer == WIDE:
                    for p in range(2):
                        n = seen.next("y")
                        dve.wait_ge(psa_taken, a_after["project", c, g] - 1 + p)
                        y, yhi = Y[n % 2], Yhi[n % 2].bitcast(F32)
                        dve.tensor_copy(KW[i % 2][:, 0, p, :], yhi[:, 1, :])
                        dve.tensor_tensor(KW[i % 2][:, 1, p, :], y[:, 1, :], yhi[:, 1, :], ALU.subtract)
                        for h in range(2):
                            r = slice(h * HD, (h + 1) * HD)
                            dve.tensor_copy(QW[i % 2][r, 0, p, h, :], yhi[r, 0, :])
                            last = dve.tensor_tensor(QW[i % 2][r, 1, p, h, :], y[r, 0, :], yhi[r, 0, :], ALU.subtract)
                        last.then_inc(split_done, 1)
                if layer == MOE:
                    for blk in ([0, 1], [2, 3], [4], [5])[g]:
                        o = v_job(seen)
                        n = seen.next("gate")
                        dve.wait_ge(gate_done, n)
                        linked(seen, dve.scalar_tensor_tensor(out=hidden_a[:], in0=gate_tanh[:, n % 2, :], scalar=1.0,
                                                              in1=o[:, 0:S], op0=ALU.add, op1=ALU.mult))
                        expert = blk < EXPERTS // 2
                        dst = hidden_b[:] if expert else hidden[u][:, blk, :]
                        dve.scalar_tensor_tensor(out=dst, in0=hidden_a[:], scalar=0.25 if expert else 0.5,
                                                 in1=o[:, S:2 * S], op0=ALU.mult, op1=ALU.mult).then_inc(psv_taken, 1)
                        if expert:
                            dve.wait_ge(psv_taken, seen.n["psv"])
                            o = v_job(seen)
                            dve.tensor_tensor(hidden[u][:, blk, :], hidden_b[:], o[:, 0:S], ALU.mult).then_inc(psv_taken, 1)

            def maxima(seen, layer, u, c, g, i):
                mx = max_neg
                for t in range(QT):
                    if layer == INFINI or (layer == GEO and t == 0):
                        o = v_job(seen)
                        dve.tensor_reduce(mx[:, t, :], o[:].rearrange("p (j k) -> p j k", j=GROUP), AX.X, ALU.max,
                                          negate=True).then_inc(psv_taken, 1)
                    else:
                        for p in range(2):
                            o = v_job(seen)
                            dve.tensor_reduce(mx[:, t, 2 * p:2 * p + 2], o[:].rearrange("p (j k) -> p j k", j=2), AX.X,
                                              ALU.max, negate=True).then_inc(psv_taken, 1)

            def turn_max(seen, layer, u, c, g, i):
                o = v_job(seen)
                nm = NM
                linked(seen, dve.tensor_copy(nm[0:GROUP, :], o[0:GROUP, 0:S]))
                dve.tensor_tensor(nm[STRIP:STRIP + GROUP, :], o[0:GROUP, 0:S], nm[0:GROUP, :].bitcast(F32),
                                  ALU.subtract).then_inc(psv_taken, 1)

            def values(seen, layer, u, c, g, i):
                if layer in NARROW:
                    o = v_job(seen)
                    dve.tensor_copy(raw[:], o[:, 0:S]).then_inc(psv_taken, 1)

            def normalise(seen, layer, u, c, g, i):
                r = rec
                if layer in NARROW:
                    o = v_job(seen)[:, 0:QT * P].rearrange("p (t j r) -> p t j r", t=QT, j=GROUP)
                    linked(seen, dve.reciprocal(r[:], o[:, :, :, DK]))
                    w = GROUP * DK
                    dst = mixed[u][:, :, g * w:(g + 1) * w].rearrange("p t (j d) -> p t j d", j=GROUP)
                    dve.tensor_tensor(dst, o[:, :, :, 0:DK], r[:, :, :, None].to_broadcast([P, QT, GROUP, DK]),
                                      ALU.mult).then_inc(psv_taken, 1)
                else:
                    w = GROUP * HD
                    for t in range(QT):
                        o = v_job(seen)[:, 0:GROUP * (HD + 2)].rearrange("p (j r) -> p j r", j=GROUP)
                        linked(seen, dve.reciprocal(r[:, t, :], o[:, :, HD]))
                        dst = wide_mixed[:, t, g * w:(g + 1) * w].rearrange("p (j d) -> p j d", j=GROUP)
                        dve.tensor_tensor(dst, o[:, :, 0:HD], r[:, t, :, None].to_broadcast([P, GROUP, HD]),
                                          ALU.mult).then_inc(psv_taken, 1)

            def merge(seen, layer, u, c):
                if layer not in NARROW:
                    return
                o = v_job(seen)[:, 0:S]
                if layer == INFINI:
                    dve.scalar_tensor_tensor(out=mixedT[u][:], in0=o, scalar=one_less_beta[:], in1=recalled[u][:],
                                             op0=ALU.mult, op1=ALU.add).then_inc(psv_taken, 1)
                elif layer == CROSS:
                    dve.tensor_scalar(mixedT[u][:], o, W(CROSS, "bv"), None, ALU.add).then_inc(psv_taken, 1)
                else:
                    dve.tensor_copy(mixedT[u][:], o).then_inc(psv_taken, 1)

            def output(seen, layer, u, c):
                o = v_job(seen)[:, 0:QT * D].rearrange("p (t d) -> p t d", t=QT)
                if layer == FFN:
                    dve.scalar_tensor_tensor(out=gated[u][:], in0=r_tanh[u][:], scalar=1.0, in1=o,
                                             op0=ALU.add, op1=ALU.mult).then_inc(psv_taken, 1)
                    dve.wait_ge(psv_taken, seen.n["psv"])
                    dve.scalar_tensor_tensor(out=X[u][:], in0=gated[u][:], scalar=0.5, in1=X[u][:],
                                             op0=ALU.mult, op1=ALU.add).then_inc(x_final, 1)
                    return
                dve.tensor_tensor(X[u][:], X[u][:], o, ALU.add).then_inc(psv_taken, 1)
                dve.wait_ge(psv_taken, seen.n["psv"])
                if layer == CROSS:
                    linked(seen, dve.tensor_tensor(X[u][:], X[u][:], W(CROSS, "bo")[:, None, :].to_broadcast([P, QT, D]),
                                                   ALU.add))
                norm_stats(seen, u)

            def recall(seen, u, s):
                if s == 0:
                    return
                o = v_job(seen)
                linked(seen, dve.tensor_scalar(v_prev[u][:, 1, :], o[0:SEG, D:2 * D], MEM_EPS, None, ALU.add))
                linked(seen, dve.reciprocal(v_prev[u][:, 1, :], v_prev[u][:, 1, :]))
                linked(seen, dve.tensor_tensor(v_prev[u][:, 0, :], v_prev[u][:, 1, :], o[0:SEG, 0:D], ALU.mult))
                dve.tensor_tensor(told[u][:, 0, :], vtok[u][:, s, :], v_prev[u][:, 0, :], ALU.subtract).then_inc(psv_taken, 1)

            def remember(seen, u, s):
                o = v_job(seen)[:, 0:2 * D].rearrange("p (k d) -> p k d", k=2)
                own = C("blocks")[:, None, :].to_broadcast([P, 2, D])
                if s == 0:
                    dve.tensor_tensor(MZ[u][:], o, own, ALU.mult).then_inc(psv_taken, 1)
                else:
                    linked(seen, dve.tensor_tensor(mz_new[u][:], o, own, ALU.mult))
                    dve.tensor_tensor(MZ[u][:], MZ[u][:], mz_new[u][:], ALU.add).then_inc(psv_taken, 1)

            def answer(seen, u, s):
                o = v_job(seen)
                linked(seen, dve.tensor_scalar(rec_den[u][:], o[:, SEG:2 * SEG], MEM_EPS, None, ALU.add))
                linked(seen, dve.reciprocal(rec_den[u][:], rec_den[u][:]))
                dve.scalar_tensor_tensor(out=recalled[u][:, (s + 1) * SEG:(s + 2) * SEG], in0=o[:, 0:SEG], scalar=beta[:],
                                         in1=rec_den[u][:], op0=ALU.mult, op1=ALU.mult).then_inc(psv_taken, 1)

            with dve.Fori(0, ROUNDS) as it:
                seen = Tally()
                for what, c, g in STEPS:
                    layer, u = divmod(c, IN_FLIGHT)
                    i = 4 * c + g
                    if what == "enter":
                        dve.wait_ge(x_loaded, 32 * IN_FLIGHT)
                        norm_stats(seen, c)
                        scale(seen, c)
                    elif what == "scale":
                        scale(seen, u)
                    elif what == "prepare":
                        prepare(seen, layer, u, c)
                    elif what == "project":
                        project(seen, layer, u, c, g, i)
                    elif what == "maxima":
                        maxima(seen, layer, u, c, g, i)
                    elif what == "turn_max":
                        turn_max(seen, layer, u, c, g, i)
                    elif what == "values":
                        values(seen, layer, u, c, g, i)
                    elif what == "normalise":
                        normalise(seen, layer, u, c, g, i)
                    elif what == "merge":
                        merge(seen, layer, u, c)
                    elif what == "output":
                        output(seen, layer, u, c)
                    elif what == "recall":
                        recall(seen, u, g)
                    elif what == "remember":
                        remember(seen, u, g)
                    elif what == "answer":
                        answer(seen, u, g)
                dve.nop().then_inc(round_over["dve"], 1)
                dve.wait_ge(next_round, it + 1)


def packed(w, parts):
    n = w.shape[1] // H
    o = np.zeros((w.shape[0], NG, GROUP, STRIP), w.dtype)
    for t in parts:
        o[:, :, :, 8 * t:8 * t + n] = w.reshape(w.shape[0], NG, GROUP, n)
    return o.reshape(w.shape[0], NG * P)


def lay_out(a):
    f = np.float32
    TERMS = (0, 1, 2)

    def column(v, n=1):
        return np.repeat(v, n).reshape(P, 1)

    q, k = a["L0_attn_W_q"].T, a["L0_attn_W_k"].T
    t0 = [packed(q, TERMS), packed(k, TERMS), q, k, a["L0_attn_W_v"].T, a["L0_attn_W_o"].T,
          column(a["L0_attn_beta_param"], DK)]
    t1 = [packed(a["L0_xattn_Wq"], TERMS), packed(a["L0_xattn_Wk"], TERMS), a["L0_xattn_Wv"], a["L0_xattn_Wo"],
          packed(a["L0_xattn_bq"].reshape(1, D), TERMS).reshape(NG, P).T,
          packed(a["L0_xattn_bk"].reshape(1, D), TERMS).reshape(NG, P).T,
          column(a["L0_xattn_bv"]), np.broadcast_to(a["L0_xattn_bo"].reshape(1, D), (P, D))]
    gu = a["L0_ffn_gate_up_w"]
    gate, up = gu[:, :, :64], gu[:, :, 64:]

    def by_pair(w):
        return w.transpose(1, 0, 2).reshape(P, EXPERTS * 64)

    down = np.concatenate([a["L0_ffn_down_w"].reshape(EXPERTS * 64, D), a["L0_ffn_shared_down_w"].T], 0)
    t2 = [a["L0_ffn_router_w"].T, by_pair(gate), a["L0_ffn_shared_gate_w"].T, by_pair(up),
          a["L0_ffn_shared_up_w"].T, down.reshape(BLOCKS, P, D).transpose(1, 0, 2).reshape(P, BLOCKS * D)]
    own = np.zeros((2, P, H, 4), f)
    for h in range(H):
        for d in range(3):
            own[0, 3 * h + d, h, d] = a["L1_attn_scale"][0]
            own[1, 3 * h + d, h, d] = 1.0
            own[:, 3 * h + d, h, 3] = a["L1_attn_head_dirs"][h, d]
    pad3 = [np.concatenate([a[n], np.zeros((P, P - 3 * H), f)], 1) for n in ("L1_attn_wq", "L1_attn_wk")]
    t3 = [*pad3, packed(own[0].reshape(P, 64), TERMS), packed(own[1].reshape(P, 64), TERMS), a["L1_attn_wv"],
          a["L1_attn_wo"]]
    t4 = [a["L1_xattn_w_q"], a["L1_xattn_w_k"], a["L1_xattn_w_v"],
          a["L1_xattn_w_o"].reshape(PAIRS, P, D).transpose(1, 0, 2).reshape(P, PAIRS * D)]
    t5 = [a["L1_ffn_W_r"].T, a["L1_ffn_W_k"].T, a["L1_ffn_W_v"].T, column(a["L1_ffn_mu_r"]), column(a["L1_ffn_mu_k"])]
    return [np.ascontiguousarray(np.concatenate(t, 1)) for t in (t0, t1, t2, t3, t4, t5)]


def constant_table():
    f = np.float32
    r = np.arange(P)
    down, along = r[:, None], r[None, :]
    same = down // SEG == along // SEG
    masks = [np.where(m, 0.0, NEG) for m in ((along <= down) & same, (down <= along) & same, along <= down, down <= along)]
    head_pick = np.zeros((P, GROUP, P))
    expert_pick = np.zeros((P, GROUP, P))
    for j in range(GROUP):
        head_pick[[j, STRIP + j], j, :] = 1
        expert_pick[2 * j, j, :64] = 1
        expert_pick[2 * j + 1, j, 64:] = 1
    lo = np.zeros((P, 2))
    lo[r % STRIP // 8 == 2, 0] = -1
    lo[r % STRIP // 8 == 1, 1] = -1
    parts = [np.eye(P), *masks, head_pick.reshape(P, -1), expert_pick.reshape(P, -1), down // DK == along // DK, lo,
             np.broadcast_to(np.arange(8), (P, 8))]
    return np.concatenate([np.asarray(p, f) for p in parts], 1)


def kernel(**inputs):
    import concourse.bacc as bacc
    from concourse.bass_utils import run_bass_kernel_spmd

    a = {k: np.asarray(v) for k, v in inputs.items()}
    nc = bacc.Bacc("TRN2", target_bir_lowering=False, num_devices=1)
    arrays = {"x": np.ascontiguousarray(a["x"]), "ctx_1024": np.ascontiguousarray(a["ctx_1024"]),
              "constants": constant_table()}
    for i, t in enumerate(lay_out(a)):
        arrays[f"table_{i}"] = t
    aps = {n: nc.dram_tensor(f"in_{n}", v.shape, F32, kind="ExternalInput").ap() for n, v in arrays.items()}
    out = nc.dram_tensor("out_0", (B, S, D), F32, kind="ExternalOutput").ap()
    build(nc, aps["x"], aps["ctx_1024"], [aps[f"table_{i}"] for i in range(LAYERS)], aps["constants"], out)
    r = run_bass_kernel_spmd(nc, [{f"in_{n}": v for n, v in arrays.items()}], core_ids=[0])
    return r.results[0]["out_0"]
```

```python
from contextlib import ExitStack

import numpy as np

import concourse.bass as bass
from concourse import mybir

F32 = mybir.dt.float32
F32R = mybir.dt.float32r
BF16 = mybir.dt.bfloat16
U32 = mybir.dt.uint32
ALU = mybir.AluOpType
ACT = mybir.ActivationFunctionType
AX = mybir.AxisListType

P = 128
B, S, D = 4, 256, 128
H = 16
QT = S // P
DK = D // H
HD = 64
SEG = 64
NSEG = S // SEG
EXPERTS = 8
GROUP = 4
NG = H // GROUP
STRIP = P // GROUP
BLOCKS = 6
PAIRS = H * HD // P
LN_EPS = 1e-5
MEM_EPS = 1e-6
NEG = -1e30

INFINI, CROSS, MOE, GEO, WIDE, FFN = range(6)
LAYERS = 6
NARROW = (INFINI, CROSS, GEO)
CHUNKS = LAYERS * B
UNITS = 4 * CHUNKS
SCALE = {INFINI: DK ** -0.5, CROSS: DK ** -0.5, GEO: 1.0, WIDE: HD ** -0.5}

COLUMNS = {
    INFINI: [("q", 128), ("k", 128), ("v", 128), ("o", 128), ("beta", 1)],
    CROSS: [("q", 128), ("k", 128), ("v", 128), ("o", 128), ("bq", 1), ("bk", 1), ("bv", 1), ("bo", 128)],
    MOE: [("router", 8), ("gate", BLOCKS * P), ("up", BLOCKS * P), ("o", BLOCKS * P)],
    GEO: [("q3", 128), ("k3", 128), ("q", 128), ("k", 128), ("v", 128), ("o", 128)],
    WIDE: [("q", 1024), ("k", 1024), ("v", 1024), ("o", 1024)],
    FFN: [("r", 128), ("k", 128), ("o", 128), ("mu_r", 1), ("mu_k", 1)],
}
CONSTANTS = [("ident", 128), ("expert_pick", 512), ("blocks", 128), ("iota", 8)]
ROUNDED = [("masks", 512), ("head_pick", 512)]
PICKS = 2 * 2 * P


def offsets(columns):
    at, out = 0, {}
    for name, n in columns:
        out[name] = (at, n)
        at += n
    return out, at


class Tally:

    def __init__(self):
        self.n = {}

    def next(self, name, by=1):
        self.n[name] = self.n.get(name, 0) + by
        return self.n[name]


def schedule():
    steps = []
    for s in range(-4, UNITS + 5):
        def chunk_at(offset):
            c, r = divmod(s - offset, 4)
            return c if r == 0 and 0 <= c < CHUNKS else None

        def attends(i):
            return 0 <= i < UNITS and (i // 4) // B in (INFINI, CROSS, GEO, WIDE)

        def step(name, i):
            steps.append((name, i // 4, i % 4))

        learning = [(c, s - (4 * c - 2)) for c in range(B) if 0 <= s - (4 * c - 2) < NSEG - 1]
        ended, scaled, starting, entering = chunk_at(4), chunk_at(5), chunk_at(-3), chunk_at(-4)
        if entering is not None and entering < B:
            steps.append(("enter", entering, 0))
        if attends(s + 1):
            step("maxima", s + 1)
        if attends(s - 1):
            step("normalise", s - 1)
        if scaled is not None and scaled // B < LAYERS - 1:
            steps.append(("to_columns", scaled, 0))
        if ended is not None and attends(4 * ended):
            steps.append(("merge", ended, 0))
        for c, n in learning:
            steps.append(("recall", c, n))
        if attends(s):
            step("exps", s)
        if attends(s + 1):
            step("turn_max", s + 1)
        for c, n in learning:
            steps.append(("remember", c, n))
        if 0 <= s + 2 < UNITS:
            step("project", s + 2)
        if starting is not None:
            steps.append(("prepare", starting, 0))
        if ended is not None:
            steps.append(("output", ended, 0))
        if attends(s):
            step("values", s)
        for c, n in learning:
            steps.append(("answer", c, n))
        if ended is not None and ended // B < LAYERS - 1:
            steps.append(("scale", ended, 0))
    return steps


def v_jobs(what, layer, g):
    if what == "prepare":
        return {INFINI: 3, CROSS: 1, GEO: 1, MOE: 2}.get(layer, 0)
    if what == "project":
        return {MOE: (4, 4, 1, 1)[g], WIDE: 2}.get(layer, 0)
    if what == "maxima":
        return {INFINI: 2, GEO: 3}.get(layer, 4)
    if what == "normalise":
        return 1 if layer in NARROW else 2
    if what in ("values", "merge"):
        return int(layer in NARROW)
    if what == "recall":
        return int(g > 0)
    return int(what in ("turn_max", "remember", "answer", "output"))


def a_jobs(what, layer, g):
    if what == "prepare":
        return {INFINI: 1, CROSS: 1, GEO: 2, FFN: 2}.get(layer, 0)
    if what == "project":
        return int(layer in NARROW or layer == WIDE)
    if what == "exps":
        return 1 if layer == INFINI else 2
    if what in ("values", "merge"):
        return {"values": 1, "merge": 2}[what] * (layer == WIDE)
    return {"enter": 2, "to_columns": 1}.get(what, 0)


def job_numbers(steps, jobs):
    n, after = 0, {}
    for what, c, g in steps:
        n += jobs(what, c // B if what != "enter" else -1, g)
        after[what, c, g] = n
    return after


def build(nc, x, ctx_in, tables, constants, picks, rounded, out):
    OFF = {}
    WIDTH = {}
    for layer in range(LAYERS):
        OFF[layer], WIDTH[layer] = offsets(COLUMNS[layer])
    CO, CW = offsets(CONSTANTS)
    RO, RW = offsets(ROUNDED)
    STEPS = schedule()
    v_after = job_numbers(STEPS, v_jobs)
    a_after = job_numbers(STEPS, a_jobs)

    def columns_after(c):
        return a_after["to_columns", c - B, 0] if c >= B else a_after["enter", c, 0]

    with ExitStack() as stack:
        def sb(name, shape, dt=F32):
            return stack.enter_context(nc.sbuf_tensor(name, shape, dt))

        def sem(name):
            return stack.enter_context(nc.semaphore(name))

        table = [sb(f"table{i}", [P, WIDTH[i]]) for i in range(LAYERS)]
        consts = sb("consts", [P, CW])

        def W(layer, name):
            a, n = OFF[layer][name]
            return table[layer][:, a:a + n]

        def C(name):
            a, n = CO[name]
            return consts[:, a:a + n]

        ident = C("ident")
        ident16 = sb("ident16", [P, P], BF16)
        masks = sb("masks", [P, 4, GROUP, P], BF16)
        head_pick = sb("head_pick", [P, GROUP, P], F32R)
        strip_pick = sb("strip_pick", [P, 2, 2, NG, P], F32R)
        beta = sb("beta", [P, 1])
        one_less_beta = sb("one_less_beta", [P, 1])
        beta_tanh = sb("beta_tanh", [P, 1])
        one_less_mu = sb("one_less_mu", [P, 2])
        ln_power = sb("ln_power", [P, QT])

        def each(name, shape, dt=F32):
            return [sb(f"{name}{u}", shape, dt) for u in range(B)]

        def two(name, shape, dt=F32):
            tiles = [sb(f"{name}{u}", shape, dt) for u in range(2)]
            return [tiles[u % 2] for u in range(B)]

        X = each("x", [P, QT, D])
        ctxT = each("ctxT", [P, S])
        xn = two("xn", [P, QT, D])
        xnT = each("xnT", [P, S])
        stats = two("stats", [P, QT, 6])
        meanvar = two("meanvar", [P, QT, 2])
        var_eps = two("var_eps", [P, QT])
        rstd = two("rstd", [P, QT])
        V = two("v_ones", [P, QT, H, STRIP])
        q3T = two("q3T", [P, 2, S])
        mixed = two("mixed", [P, QT, D])
        mixedT = two("mixedT", [P, S])
        ctx_rows = [*mixed[0:2], *(m[:].rearrange("p (t d) -> p t d", t=QT) for m in mixedT[0:2])]
        wide_mixed = sb("wide_mixed", [P, QT, H * HD])
        wide_mixedT = sb("wide_mixedT", [P, PAIRS, S])
        sigT = two("sigT", [P, 2, S])
        sig_e = sb("sig_e", [P, 2, S])
        ktok = two("ktok", [SEG, NSEG - 1, D])
        ktok_e = sb("ktok_e", [SEG, NSEG - 1, D])
        vtok = two("vtok", [SEG, NSEG - 1, D])
        MZ = two("mz", [P, 2, D])
        mz_new = two("mz_new", [P, 2, D])
        told = two("told", [SEG, 2, D])
        v_prev = two("v_prev", [SEG, 2, D])
        recalled = two("recalled", [P, S])
        rec_den = two("rec_den", [P, SEG])
        top8 = two("top8", [P, QT, 8])
        top_at = two("top_at", [P, QT, 8], U32)
        top_atf = two("top_atf", [P, QT, 2])
        gates = two("gates", [P, QT, 2])
        combine = two("combine", [P, QT, 8])
        combine2 = two("combine2", [P, QT, 8])
        logits = two("logits", [P, QT, 8])
        combineT = two("combineT", [P, S])
        gate_tanh = sb("gate_tanh", [P, 2, S])
        hidden_a = sb("hidden_a", [P, S])
        hidden_b = sb("hidden_b", [P, S])
        hidden = [wide_mixed[:].rearrange("p t (k s) -> p (t k) s", s=S)[:, 0:BLOCKS, :], wide_mixedT[:, 0:BLOCKS, :]] * 2
        shifted = q3T
        mixed_in = sigT
        k_relu = two("k_relu", [P, S])
        k_act = two("k_act", [P, S])
        r_tanh = two("r_tanh", [P, QT, D])
        gated = two("gated", [P, QT, D])

        QKhi = sb("qk_high", [P, 2, S], F32R)
        QKlo = sb("qk_low", [P, 2, S], F32R)
        QZ = [sb(f"qz{i}", [P, GROUP, S], F32R) for i in range(2)]
        KZ = [sb(f"kz{i}", [P, S], F32R) for i in range(2)]
        QW = [sb(f"qw{i}", [P, GROUP, S], F32R) for i in range(2)]
        KWhi = [sb(f"kw_high{i}", [P, GROUP, S], F32R) for i in range(2)]
        KWlo = [sb(f"kw_low{i}", [P, GROUP, S], F32R) for i in range(2)]
        VW = [sb(f"vw{i}", [P, QT, GROUP, HD + 2]) for i in range(3)]
        max_neg = sb("max_neg", [P, QT, GROUP])
        NM = sb("nm", [P, S], F32R)
        PT = sb("pt", [P, QT, GROUP, S])
        raw = sb("raw", [P, S])
        raw_wide = sb("raw_wide", [HD + 2, GROUP, S])
        rec = sb("rec", [P, QT, GROUP])

        VSLOTS, ASLOTS = 4, 2
        psv = [stack.enter_context(nc.psum_tensor(f"psv{i}", [P, 512], F32)) for i in range(VSLOTS)]
        psa = [stack.enter_context(nc.psum_tensor(f"psa{i}", [P, 1024], F32)) for i in range(ASLOTS)]

        table_loaded = [sem(f"table_loaded{i}") for i in range(LAYERS)]
        consts_loaded = sem("consts_loaded")
        vector_consts = sem("vector_consts")
        pool_consts = sem("pool_consts")
        scalar_consts = sem("scalar_consts")
        x_loaded = [sem(f"x_loaded{u}") for u in range(B)]
        stored = sem("stored")
        psv_ready = sem("psv_ready")
        psv_taken = sem("psv_taken")
        psa_ready = sem("psa_ready")
        psa_taken = sem("psa_taken")
        high_done = sem("high_done")
        var_found = sem("var_found")
        var_shifted = sem("var_shifted")
        rstd_found = sem("rstd_found")
        xn_written = sem("xn_written")
        clipped = sem("clipped")
        clip_exp = sem("clip_exp")
        top_found = sem("top_found")
        top_gated = sem("top_gated")
        gate_done = sem("gate_done")
        mixes_done = sem("mixes_done")
        relu_done = sem("relu_done")
        x_final = sem("x_final")
        dve_wrote = sem("dve_wrote")
        POOL_CONSTS, VECTOR_CONSTS = 8, 22

        block = stack.enter_context(nc.Block())

        @block.sync
        def _(sp):
            def rows(dram, b):
                return dram[b, :, :].rearrange("(t p) d -> p t d", p=P)

            def load(u):
                sp.dma_start(X[u][:], rows(x, u)).then_inc(x_loaded[u], 16)
                sp.dma_start(ctx_rows[u][:], rows(ctx_in, u)).then_inc(x_loaded[u], 16)

            load(0)
            sp.dma_start(consts[:], constants).then_inc(consts_loaded, 16)
            sp.dma_start(PT[:].rearrange("p t j q -> p (t j q)")[:, 0:PICKS], picks).then_inc(consts_loaded, 16)
            sp.dma_start(wide_mixed[:].rearrange("p t w -> p (t w)")[:, 0:RW], rounded).then_inc(consts_loaded, 16)
            sp.dma_start(table[INFINI][:], tables[INFINI]).then_inc(table_loaded[INFINI], 16)
            for u in range(1, B):
                load(u)
            for i in range(INFINI + 1, LAYERS):
                sp.dma_start(table[i][:], tables[i]).then_inc(table_loaded[i], 16)
            for u in range(B):
                sp.wait_ge(x_final, u + 1)
                sp.dma_start(rows(out, u), X[u][:]).then_inc(stored, 16)
            sp.wait_ge(stored, 16 * B)

        @block.tensor
        def _(pe):
            def a_slot(seen):
                n = seen.next("psa")
                if n > ASLOTS:
                    pe.wait_ge(psa_taken, n - ASLOTS)
                return psa[(n - 1) % ASLOTS]

            def v_slot(seen):
                n = seen.next("psv")
                if n > VSLOTS:
                    pe.wait_ge(psv_taken, n - VSLOTS)
                return psv[(n - 1) % VSLOTS]

            def mm(o, l, r, start=True, stop=True):
                return pe.matmul(o, l, r, start=start, stop=stop)

            def turn(o, i, idn):
                return pe.transpose(o, i, idn)

            def enter(seen, u):
                if u == 0:
                    pe.wait_ge(consts_loaded, 48)
                pe.wait_ge(x_loaded[u], 32)
                o = a_slot(seen)
                for t in range(QT):
                    last = turn(o[:, t * P:(t + 1) * P], ctx_rows[u][:, t, :], ident)
                last.then_inc(psa_ready, 1)
                to_columns(seen, u)

            def to_columns(seen, u):
                pe.wait_ge(xn_written, seen.next("xn_written"))
                o = a_slot(seen)
                for t in range(QT):
                    last = turn(o[:, t * P:(t + 1) * P], xn[u][:, t, :], ident)
                last.then_inc(psa_ready, 1)

            def prepare(seen, layer, u, c):
                pe.wait_ge(psa_taken, columns_after(c))
                if u == 0:
                    pe.wait_ge(table_loaded[layer], 16)
                if layer == INFINI and u == 0:
                    pe.wait_ge(vector_consts, VECTOR_CONSTS)
                    pe.wait_ge(pool_consts, POOL_CONSTS)
                src = ctxT[u] if layer == CROSS else xnT[u]
                if layer == GEO:
                    o = a_slot(seen)
                    mm(o[:, 0:S], W(GEO, "q3"), xnT[u][:])
                    mm(o[:, S:2 * S], W(GEO, "k3"), xnT[u][:]).then_inc(psa_ready, 1)
                if layer in NARROW:
                    o = a_slot(seen)
                    for t in range(QT):
                        last = mm(o[:, t * P:(t + 1) * P], src[:, t * P:(t + 1) * P], W(layer, "v"))
                    last.then_inc(psa_ready, 1)
                    qs, ks = (q3T[u][:, 0, :], q3T[u][:, 1, :]) if layer == GEO else (xnT[u][:], src[:])
                    if layer == GEO:
                        pe.wait_ge(psa_taken, a_after["prepare", c, 0] - 1)
                    o = v_slot(seen)
                    mm(o[:, 0:S], W(layer, "q"), qs)
                    mm(o[:, S:2 * S], W(layer, "k"), ks).then_inc(psv_ready, 1)
                if layer == INFINI:
                    for name in ("k", "v"):
                        o = v_slot(seen)
                        for s in range(NSEG - 1):
                            last = mm(o[0:SEG, s * D:(s + 1) * D], xnT[u][:, s * SEG:(s + 1) * SEG], W(INFINI, name))
                        last.then_inc(psv_ready, 1)
                if layer == MOE:
                    o = v_slot(seen)
                    for t in range(QT):
                        last = mm(o[:, 8 * t:8 * t + 8], xnT[u][:, t * P:(t + 1) * P], W(MOE, "router"))
                    last.then_inc(psv_ready, 1)
                    pe.wait_ge(psv_taken, v_after["prepare", c, 0] - 1)
                    o = v_slot(seen)
                    for t in range(QT):
                        last = turn(o[0:8, t * P:(t + 1) * P], combine[u][:, t, :], ident)
                    last.then_inc(psv_ready, 1)
                if layer == FFN:
                    pe.wait_ge(mixes_done, seen.next("mixes_done"))
                    o = a_slot(seen)
                    mm(o[:, 0:S], W(FFN, "k"), mixed_in[u][:, 1, :]).then_inc(psa_ready, 1)
                    o = a_slot(seen)
                    for t in range(QT):
                        last = mm(o[:, t * D:(t + 1) * D], mixed_in[u][:, 0, t * P:(t + 1) * P], W(FFN, "r"))
                    last.then_inc(psa_ready, 1)

            def project(seen, layer, u, c, g, i):
                if layer in NARROW:
                    if g == 0:
                        pe.wait_ge(psv_taken, v_after["prepare", c, 0])
                    o = a_slot(seen)
                    for k in range(2):
                        ok = o[:, k * S:(k + 1) * S]
                        mm(ok, strip_pick[:, k, 0, g, :], QKhi[:, k, :], stop=False)
                        last = mm(ok, strip_pick[:, k, 1, g, :], QKlo[:, k, :], start=False)
                    last.then_inc(psa_ready, 1)
                if layer == WIDE:
                    o = a_slot(seen)
                    for t in range(QT):
                        last = mm(o[:, t * S:(t + 1) * S], ctxT[u][:, t * P:(t + 1) * P],
                                  W(WIDE, "v")[:, g * S:(g + 1) * S])
                    last.then_inc(psa_ready, 1)
                    for p in range(2):
                        w = (2 * g + p) * P
                        o = v_slot(seen)
                        mm(o[:, 0:S], W(WIDE, "q")[:, w:w + P], xnT[u][:])
                        mm(o[:, S:2 * S], W(WIDE, "k")[:, w:w + P], ctxT[u][:]).then_inc(psv_ready, 1)
                if layer == MOE:
                    if g == 0:
                        pe.wait_ge(psv_taken, v_after["prepare", c, 0])
                    for blk in ([0, 1], [2, 3], [4], [5])[g]:
                        o = v_slot(seen)
                        w = slice(blk * P, (blk + 1) * P)
                        mm(o[:, 0:S], W(MOE, "gate")[:, w], xnT[u][:])
                        mm(o[:, S:2 * S], W(MOE, "up")[:, w], xnT[u][:]).then_inc(psv_ready, 1)
                        if blk < EXPERTS // 2:
                            o = v_slot(seen)
                            mm(o[:, 0:S], C("expert_pick")[:, w], combineT[u][:]).then_inc(psv_ready, 1)

            def score_terms(layer, i):
                if layer in NARROW:
                    return lambda j, q: [(QZ[i % 2][:, j, q], KZ[i % 2][:])]
                qw, khi, klo = QW[i % 2], KWhi[i % 2], KWlo[i % 2]
                return lambda j, q: [(qw[:, j, q], khi[:, j, :]), (qw[:, j, q], klo[:, j, :])]

            def maxima(seen, layer, u, c, g, i):
                if layer != WIDE:
                    pe.wait_ge(psa_taken, a_after["project", c, g])
                terms = score_terms(layer, i)
                kind = 0 if layer == INFINI else 1
                for t in range(QT):
                    q = slice(t * P, (t + 1) * P)
                    if layer == INFINI or (layer == GEO and t == 0):
                        o = v_slot(seen)
                        mm(o[:], ident16[:], masks[:, 2 * kind, :, :], stop=False)
                        for j in range(GROUP):
                            (qa, ka), = terms(j, q)
                            last = mm(o[:, j * P:(j + 1) * P], qa, ka[:, q], start=False, stop=j == GROUP - 1)
                        last.then_inc(psv_ready, 1)
                    else:
                        for p in range(2):
                            if layer == WIDE and t == 0:
                                pe.wait_ge(psv_taken, v_after["project", c, g] - 1 + p)
                            o = v_slot(seen)
                            for h in range(2):
                                tt = terms(2 * p + h, q)
                                for n, (qa, ka) in enumerate(tt):
                                    last = mm(o[:, h * S:(h + 1) * S], qa, ka, start=n == 0,
                                              stop=n == len(tt) - 1 and layer != GEO)
                                if layer == GEO:
                                    last = mm(o[:, h * S + P:(h + 1) * S], ident16[:], masks[:, 2, 0, :],
                                              start=False)
                            last.then_inc(psv_ready, 1)

            def turn_max(seen, layer, u, c, g, i):
                pe.wait_ge(psv_taken, v_after["maxima", c, g])
                o = v_slot(seen)
                for t in range(QT):
                    last = turn(o[0:GROUP, t * P:(t + 1) * P], max_neg[:, t, :], ident)
                last.then_inc(psv_ready, 1)

            def exps(seen, layer, u, c, g, i):
                pe.wait_ge(psv_taken, v_after["turn_max", c, g])
                terms = score_terms(layer, i)
                nm = NM
                if layer == INFINI:
                    o = a_slot(seen)
                    for t in range(QT):
                        q = slice(t * P, (t + 1) * P)
                        c0 = t * GROUP * P
                        mm(o[:, c0:c0 + GROUP * P], ident16[:], masks[:, 1, :, :], stop=False)
                        for j in range(GROUP):
                            (qa, ka), = terms(j, q)
                            mm(o[:, c0 + j * P:c0 + (j + 1) * P], ka[:, q], qa, start=False, stop=False)
                            last = mm(o[:, c0 + j * P:c0 + (j + 1) * P], head_pick[:, j, :], nm[:, q],
                                      start=False, stop=j == GROUP - 1)
                    last.then_inc(psa_ready, 1)
                    return
                for t in range(QT):
                    k = slice(t * P, (t + 1) * P)
                    o = a_slot(seen)
                    if layer == GEO and t == 1:
                        mm(o[:, 0:GROUP * P], ident16[:], masks[:, 3, :, :], stop=False)
                        for j in range(GROUP):
                            (qa, ka), = terms(j, k)
                            mm(o[:, j * P:(j + 1) * P], ka[:, k], qa, start=False, stop=False)
                            last = mm(o[:, j * P:(j + 1) * P], head_pick[:, j, :], nm[:, k],
                                      start=False, stop=j == GROUP - 1)
                    else:
                        for j in range(GROUP):
                            oj = o[:, j * S:(j + 1) * S]
                            for n, (qa, ka) in enumerate(terms(j, slice(0, S))):
                                mm(oj, ka[:, k], qa, start=n == 0, stop=False)
                            last = mm(oj, head_pick[:, j, :], nm[:], start=False, stop=layer != GEO)
                            if layer == GEO:
                                last = mm(o[:, j * S:j * S + P], ident16[:], masks[:, 3, 0, :], start=False)
                    last.then_inc(psa_ready, 1)

            def values(seen, layer, u, c, g, i):
                pt = PT
                if layer in NARROW:
                    if g == 0:
                        pe.wait_ge(psa_taken, a_after["prepare", c, 0])
                    o = v_slot(seen)
                    for t in range(QT):
                        pe.wait_ge(psa_taken, a_after["exps", c, g] - (1 - t if layer != INFINI else 0))
                        q = slice(t * P, (t + 1) * P) if layer == INFINI else slice(t * P if layer == GEO else 0, S)
                        for j in range(GROUP):
                            last = mm(o[j * STRIP:(j + 1) * STRIP, q], V[u][:, t, GROUP * g + j, :], pt[:, t, j, q],
                                      start=t == 0 or layer == INFINI, stop=t == QT - 1 or layer == INFINI)
                    last.then_inc(psv_ready, 1)
                else:
                    pe.wait_ge(psa_taken, a_after["exps", c, g])
                    o = a_slot(seen)
                    for j in range(GROUP):
                        for t in range(QT):
                            last = mm(o[0:HD + 2, j * S:(j + 1) * S], VW[i % 3][:, t, j, :], pt[:, t, j, :],
                                      start=t == 0, stop=t == QT - 1)
                    last.then_inc(psa_ready, 1)

            def normalise(seen, layer, u, c, g, i):
                if layer in NARROW:
                    pe.wait_ge(psv_taken, v_after["values", c, g])
                    o = v_slot(seen)
                    for t in range(QT):
                        last = turn(o[:, t * P:(t + 1) * P], raw[:, t * P:(t + 1) * P], ident)
                    last.then_inc(psv_ready, 1)
                else:
                    pe.wait_ge(psa_taken, a_after["values", c, g])
                    for t in range(QT):
                        o = v_slot(seen)
                        for j in range(GROUP):
                            last = turn(o[:, j * (HD + 2):(j + 1) * (HD + 2)], raw_wide[:, j, t * P:(t + 1) * P],
                                        ident[0:HD + 2, 0:HD + 2])
                        last.then_inc(psv_ready, 1)

            def merge(seen, layer, u, c):
                if layer in NARROW:
                    pe.wait_ge(psv_taken, v_after["normalise", c, NG - 1])
                    o = v_slot(seen)
                    for t in range(QT):
                        last = turn(o[:, t * P:(t + 1) * P], mixed[u][:, t, :], ident)
                    last.then_inc(psv_ready, 1)
                if layer == WIDE:
                    pe.wait_ge(psv_taken, v_after["normalise", c, NG - 1])
                    for half in range(2):
                        o = a_slot(seen)
                        for p in range(4):
                            for t in range(QT):
                                c0 = (4 * half + p) * P
                                last = turn(o[:, p * S + t * P:p * S + (t + 1) * P], wide_mixed[:, t, c0:c0 + P], ident)
                        last.then_inc(psa_ready, 1)

            def output(seen, layer, u, c):
                if layer in NARROW:
                    pe.wait_ge(psv_taken, v_after["merge", c, 0])
                    parts = [mixedT[u][:]]
                if layer == WIDE:
                    pe.wait_ge(psa_taken, a_after["merge", c, 0])
                    parts = [wide_mixedT[:, p, :] for p in range(PAIRS)]
                if layer == MOE:
                    pe.wait_ge(psv_taken, v_after["project", c, 3])
                    parts = [hidden[u][:, k, :] for k in range(BLOCKS)]
                if layer == FFN:
                    pe.wait_ge(psa_taken, a_after["prepare", c, 0])
                    parts = [k_act[u][:]]
                o = v_slot(seen)
                for t in range(QT):
                    for n, part in enumerate(parts):
                        last = mm(o[:, t * D:(t + 1) * D], part[:, t * P:(t + 1) * P],
                                  W(layer, "o")[:, n * D:(n + 1) * D], start=n == 0, stop=n == len(parts) - 1)
                last.then_inc(psv_ready, 1)

            def recall(seen, u, s):
                if s == 0:
                    return
                pe.wait_ge(psv_taken, v_after["remember", u, s - 1])
                o = v_slot(seen)
                mm(o[0:SEG, 0:2 * D], sigT[u][:, 1, s * SEG:(s + 1) * SEG], MZ[u][:, :, :]).then_inc(psv_ready, 1)

            def remember(seen, u, s):
                pe.wait_ge(psv_taken, v_after["recall", u, s] if s else v_after["prepare", u, 0])
                o = v_slot(seen)
                mm(o[:, 0:2 * D], ktok[u][:, s, :], told[u][:, :, :]).then_inc(psv_ready, 1)

            def answer(seen, u, s):
                pe.wait_ge(psv_taken, v_after["remember", u, s])
                o = v_slot(seen)
                q = sigT[u][:, 0, (s + 1) * SEG:(s + 2) * SEG]
                mm(o[:, 0:SEG], MZ[u][:, 0, :], q)
                mm(o[:, SEG:2 * SEG], MZ[u][:, 1, :], q).then_inc(psv_ready, 1)

            seen = Tally()
            for what, c, g in STEPS:
                layer, u = divmod(c, B)
                i = 4 * c + g
                if what == "enter":
                    enter(seen, c)
                elif what == "to_columns":
                    to_columns(seen, u)
                elif what == "prepare":
                    prepare(seen, layer, u, c)
                elif what == "project":
                    project(seen, layer, u, c, g, i)
                elif what == "maxima":
                    maxima(seen, layer, u, c, g, i)
                elif what == "turn_max":
                    turn_max(seen, layer, u, c, g, i)
                elif what == "exps":
                    exps(seen, layer, u, c, g, i)
                elif what == "values":
                    values(seen, layer, u, c, g, i)
                elif what == "normalise":
                    normalise(seen, layer, u, c, g, i)
                elif what == "merge":
                    merge(seen, layer, u, c)
                elif what == "output":
                    output(seen, layer, u, c)
                elif what == "recall":
                    recall(seen, u, g)
                elif what == "remember":
                    remember(seen, u, g)
                elif what == "answer":
                    answer(seen, u, g)

        @block.scalar
        def _(act):
            def a_job(seen):
                n = seen.next("psa")
                act.wait_ge(psa_ready, n)
                return psa[(n - 1) % ASLOTS]

            act.wait_ge(table_loaded[INFINI], 16)
            act.activation(beta_tanh[:], W(INFINI, "beta"), ACT.Tanh, scale=0.5).then_inc(scalar_consts, 1)

            def to_columns(seen, u):
                o = a_job(seen)
                act.activation(xnT[u][:], o[:, 0:S], ACT.Copy).then_inc(psa_taken, 1)

            def prepare(seen, layer, u, c):
                if layer == INFINI and u == 0:
                    act.wait_ge(vector_consts, VECTOR_CONSTS)
                    act.wait_ge(pool_consts, POOL_CONSTS)
                if layer == CROSS and u == 0:
                    act.wait_ge(table_loaded[CROSS], 16)
                if layer == GEO:
                    o = a_job(seen)
                    act.activation(q3T[u][:].rearrange("p a s -> p (a s)"), o[:, 0:2 * S], ACT.Copy).then_inc(psa_taken, 1)
                if layer in NARROW:
                    o = a_job(seen)
                    for t in range(QT):
                        last = act.activation(V[u][:, t, :, 0:DK], o[:, t * P:(t + 1) * P].rearrange("p (h d) -> p h d", d=DK),
                                              ACT.Copy)
                    last.then_inc(psa_taken, 1)
                    job = v_after["prepare", c, 0] - v_jobs("prepare", layer, 0) + 1
                    act.wait_ge(psv_ready, job)
                    o = psv[(job - 1) % VSLOTS]
                    if layer == CROSS:
                        for k, name in enumerate(("bq", "bk")):
                            last = act.activation(QKhi[:, k, :], o[:, k * S:(k + 1) * S], ACT.Identity, bias=W(CROSS, name))
                    else:
                        last = act.activation(QKhi[:].rearrange("p k s -> p (k s)"), o[:, 0:2 * S], ACT.Copy)
                    last.then_inc(high_done, 1)
                if layer == INFINI:
                    act.wait_ge(clipped, seen.next("clipped"))
                    act.activation(sig_e[:], sig_e[:], ACT.Exp).then_inc(clip_exp, 1)
                    act.wait_ge(clipped, seen.next("clipped"))
                    act.activation(ktok_e[:], ktok_e[:], ACT.Exp).then_inc(clip_exp, 1)
                if layer == MOE:
                    act.wait_ge(top_found, seen.next("top_found"))
                    act.activation(gates[u][:], top8[u][:, :, 0:2], ACT.Tanh, scale=0.5).then_inc(top_gated, 1)
                if layer == FFN:
                    o = a_job(seen)
                    act.activation(k_relu[u][:], o[:, 0:S], ACT.Relu).then_inc(relu_done, 1)
                    act.wait_ge(relu_done, seen.next("relu_done"))
                    act.activation(k_act[u][:], k_relu[u][:], ACT.Square).then_inc(psa_taken, 1)
                    o = a_job(seen)
                    act.activation(r_tanh[u][:].rearrange("p t d -> p (t d)"), o[:, 0:QT * D], ACT.Tanh,
                                   scale=0.5).then_inc(psa_taken, 1)

            def project(seen, layer, u, c, g, i):
                if layer in NARROW:
                    o = a_job(seen)
                    for j in range(GROUP):
                        r = slice(j * STRIP, (j + 1) * STRIP)
                        act.activation(QZ[i % 2][r, j, :], o[r, 0:S], ACT.Copy)
                    act.activation(KZ[i % 2][:], o[:, S:2 * S], ACT.Copy).then_inc(psa_taken, 1)
                if layer == WIDE:
                    o = a_job(seen)
                    for t in range(QT):
                        last = act.activation(VW[i % 3][:, t, :, 0:HD], o[:, t * S:(t + 1) * S].rearrange("p (h d) -> p h d", d=HD),
                                              ACT.Copy)
                    last.then_inc(psa_taken, 1)
                    for p in range(2):
                        job = v_after["project", c, g] - 1 + p
                        act.wait_ge(psv_ready, job)
                        o = psv[(job - 1) % VSLOTS]
                        for h in range(2):
                            own, other = slice(h * HD, (h + 1) * HD), slice((1 - h) * HD, (2 - h) * HD)
                            act.activation(QW[i % 2][own, 2 * p + h, :], o[own, 0:S], ACT.Copy)
                            act.activation(KWhi[i % 2][own, 2 * p + h, :], o[own, S:2 * S], ACT.Copy)
                            last = act.activation(KWhi[i % 2][other, 2 * p + h, :], o[own, S:2 * S], ACT.Copy)
                        last.then_inc(high_done, 1)
                if layer == MOE:
                    for blk in ([0, 1], [2, 3], [4], [5])[g]:
                        job = v_after["project", c, g] - v_jobs("project", MOE, g) + (2 * (blk % 2) if g < 2 else 0) + 1
                        act.wait_ge(psv_ready, job)
                        n = seen.next("gate")
                        if n > 2:
                            act.wait_ge(psv_taken, job - 1)
                        act.activation(gate_tanh[:, n % 2, :], psv[(job - 1) % VSLOTS][:, 0:S], ACT.Tanh,
                                       scale=0.5).then_inc(gate_done, 1)

            def exps(seen, layer, u, c, g, i):
                pt = PT
                if layer == INFINI:
                    o = a_job(seen)
                    for t in range(QT):
                        last = act.activation(pt[:, t, :, t * P:(t + 1) * P],
                                              o[:, t * GROUP * P:(t + 1) * GROUP * P].rearrange("p (j q) -> p j q", j=GROUP),
                                              ACT.Exp, scale=SCALE[layer])
                    last.then_inc(psa_taken, 1)
                    return
                for t in range(QT):
                    o = a_job(seen)
                    if layer == GEO and t == 1:
                        act.activation(pt[:, 1, :, P:S], o[:, 0:GROUP * P].rearrange("p (j q) -> p j q", j=GROUP),
                                       ACT.Exp, scale=SCALE[layer]).then_inc(psa_taken, 1)
                    else:
                        act.activation(pt[:, t, :, :].rearrange("p j q -> p (j q)"), o[:],
                                       ACT.Exp, scale=SCALE[layer]).then_inc(psa_taken, 1)

            def values(seen, layer, u, c, g, i):
                if layer == WIDE:
                    o = a_job(seen)
                    act.activation(raw_wide[:].rearrange("p j q -> p (j q)"), o[0:HD + 2, :], ACT.Copy).then_inc(psa_taken, 1)

            def merge(seen, layer, u, c):
                if layer == WIDE:
                    for half in range(2):
                        o = a_job(seen)
                        act.activation(wide_mixedT[:, 4 * half:4 * half + 4, :].rearrange("p k s -> p (k s)"), o[:],
                                       ACT.Copy).then_inc(psa_taken, 1)

            seen = Tally()
            for what, c, g in STEPS:
                layer, u = divmod(c, B)
                i = 4 * c + g
                if what == "enter":
                    o = a_job(seen)
                    act.activation(ctxT[c][:], o[:, 0:S], ACT.Copy).then_inc(psa_taken, 1)
                    to_columns(seen, c)
                elif what == "to_columns":
                    to_columns(seen, u)
                elif what == "prepare":
                    prepare(seen, layer, u, c)
                elif what == "project":
                    project(seen, layer, u, c, g, i)
                elif what == "exps":
                    exps(seen, layer, u, c, g, i)
                elif what == "values":
                    values(seen, layer, u, c, g, i)
                elif what == "merge":
                    merge(seen, layer, u, c)

        @block.gpsimd
        def _(pool):
            for tile in (*QZ, *KWlo, NM):
                pool.memset(tile[:].bitcast(F32), 0.0).then_inc(pool_consts, 1)
            for u in range(2):
                pool.memset(combineT[u][:], 0.0).then_inc(pool_consts, 1)
            pool.memset(ln_power[:], -0.5).then_inc(pool_consts, 1)
            pool.wait_ge(pool_consts, POOL_CONSTS)
            seen = Tally()
            for what, c, g in STEPS:
                u = c % B
                if what == "enter" or (what == "output" and c // B < LAYERS - 1):
                    n = seen.next("norm")
                    pool.wait_ge(var_found, n)
                    pool.tensor_scalar(var_eps[u][:], meanvar[u][:, :, 1], LN_EPS, None, ALU.add).then_inc(var_shifted, 1)
                    pool.wait_ge(var_shifted, n)
                    pool.tensor_tensor(rstd[u][:], var_eps[u][:], ln_power[:], ALU.pow).then_inc(rstd_found, 1)

        @block.vector
        def _(dve):
            def v_job(seen):
                n = seen.next("psv")
                dve.wait_ge(psv_ready, n)
                return psv[(n - 1) % VSLOTS]

            def linked(seen, ins):
                ins.then_inc(dve_wrote, 1)
                dve.wait_ge(dve_wrote, seen.next("dve_wrote"))

            dve.memset(strip_pick[:].rearrange("p k i g m -> p (k i g m)").bitcast(F32), 0.0).then_inc(vector_consts, 1)
            for u in range(2):
                dve.memset(V[u][:], 1.0).then_inc(vector_consts, 1)
                dve.memset(told[u][:, 1, :], 1.0).then_inc(vector_consts, 1)
                dve.memset(recalled[u][:, 0:SEG], 0.0).then_inc(vector_consts, 1)
            for t in VW:
                dve.memset(t[:, :, :, HD:HD + 2], 1.0).then_inc(vector_consts, 1)
            dve.wait_ge(consts_loaded, 48)
            dve.tensor_copy(ident16[:], ident).then_inc(vector_consts, 1)
            for k in range(4):
                a = RO["masks"][0] + k * P
                m = wide_mixed[:].rearrange("p t w -> p (t w)")[:, a:a + P]
                dve.tensor_copy(masks[:, k, :, :], m[:, None, :].to_broadcast([P, GROUP, P])).then_inc(vector_consts, 1)
            a, n = RO["head_pick"]
            dve.tensor_copy(head_pick[:].rearrange("p j k -> p (j k)"),
                            wide_mixed[:].rearrange("p t w -> p (t w)")[:, a:a + n]).then_inc(vector_consts, 1)
            dve.wait_ge(vector_consts, 1)
            for g in range(NG):
                r = slice(g * STRIP, (g + 1) * STRIP)
                m = PT[:].rearrange("p t j q -> p (t j q)")[r, 0:PICKS].rearrange("p (k i m) -> p k i m", k=2, i=2)
                dve.tensor_copy(strip_pick[r, :, :, g, :], m).then_inc(vector_consts, 1)
            dve.wait_ge(scalar_consts, 1)
            dve.tensor_scalar(beta[:], beta_tanh[:], 0.5, 0.5, ALU.mult, ALU.add).then_inc(vector_consts, 1)
            dve.tensor_scalar(one_less_beta[:], beta_tanh[:], -0.5, 0.5, ALU.mult, ALU.add).then_inc(vector_consts, 1)
            dve.wait_ge(vector_consts, VECTOR_CONSTS)
            dve.wait_ge(pool_consts, POOL_CONSTS)

            def norm_stats(seen, u):
                for t in range(QT):
                    last = dve.bn_stats(stats[u][:, t, :], X[u][:, t, :])
                linked(seen, last)
                for t in range(QT):
                    last = dve.bn_aggr(meanvar[u][:, t, :], stats[u][:, t, :])
                last.then_inc(var_found, 1)

            def scale(seen, u):
                dve.wait_ge(rstd_found, seen.next("rstd_found"))
                for t in range(QT):
                    last = dve.tensor_scalar(xn[u][:, t, :], X[u][:, t, :], meanvar[u][:, t, 0:1], rstd[u][:, t:t + 1],
                                             ALU.subtract, ALU.mult)
                last.then_inc(xn_written, 1)

            def prepare(seen, layer, u, c):
                if layer in NARROW:
                    o1 = v_job(seen)
                    o1 = o1[:, 0:2 * S].rearrange("p (k s) -> p k s", k=2)
                    dve.wait_ge(high_done, seen.next("high_done"))
                    if layer == CROSS:
                        for k, name in enumerate(("bq", "bk")):
                            last = dve.scalar_tensor_tensor(out=QKlo[:, k, :], in0=o1[:, k, :], scalar=W(CROSS, name),
                                                            in1=QKhi[:, k, :].bitcast(F32), op0=ALU.add, op1=ALU.subtract)
                    else:
                        last = dve.tensor_tensor(QKlo[:], o1, QKhi[:].bitcast(F32), ALU.subtract)
                    if layer != INFINI:
                        last.then_inc(psv_taken, 1)
                if layer == INFINI:
                    dve.tensor_scalar(sig_e[:], o1, 0.0, None, ALU.min).then_inc(clipped, 1)
                    o2 = v_job(seen)
                    o2 = o2[0:SEG, 0:(NSEG - 1) * D].rearrange("p (s d) -> p s d", d=D)
                    dve.tensor_scalar(ktok_e[:], o2, 0.0, None, ALU.min).then_inc(clipped, 1)
                    dve.wait_ge(clip_exp, seen.next("clip_exp"))
                    dve.scalar_tensor_tensor(out=sigT[u][:], in0=o1, scalar=0.0, in1=sig_e[:],
                                             op0=ALU.max, op1=ALU.add).then_inc(psv_taken, 1)
                    dve.wait_ge(clip_exp, seen.next("clip_exp"))
                    dve.scalar_tensor_tensor(out=ktok[u][:], in0=o2, scalar=0.0, in1=ktok_e[:],
                                             op0=ALU.max, op1=ALU.add).then_inc(psv_taken, 1)
                    o3 = v_job(seen)
                    o3 = o3[0:SEG, 0:(NSEG - 1) * D].rearrange("p (s d) -> p s d", d=D)
                    dve.tensor_copy(vtok[u][:], o3)
                    dve.tensor_copy(told[u][:, 0, :], o3[:, 0, :]).then_inc(psv_taken, 1)
                if layer == MOE:
                    o = v_job(seen)
                    linked(seen, dve.tensor_copy(logits[u][:].rearrange("p t e -> p (t e)"), o[:, 0:8 * QT]))
                    for t in range(QT):
                        last = dve.max(top8[u][:, t, :], logits[u][:, t, :])
                    n = seen.next("top_found")
                    last.then_inc(top_found, 1)
                    dve.wait_ge(top_found, n)
                    for t in range(QT):
                        last = dve.max_index(top_at[u][:, t, :], top8[u][:, t, :], logits[u][:, t, :])
                    linked(seen, last)
                    linked(seen, dve.tensor_copy(top_atf[u][:], top_at[u][:, :, 0:2]))
                    dve.wait_ge(top_gated, seen.next("top_gated"))
                    linked(seen, dve.tensor_scalar(gates[u][:], gates[u][:], 1.0, None, ALU.add))
                    for t in range(QT):
                        for k, dst in enumerate((combine, combine2)):
                            last = dve.tensor_scalar(dst[u][:, t, :], C("iota"), top_atf[u][:, t, k:k + 1],
                                                     gates[u][:, t, k:k + 1], ALU.is_equal, ALU.mult)
                    linked(seen, last)
                    dve.tensor_tensor(combine[u][:], combine[u][:], combine2[u][:], ALU.add).then_inc(psv_taken, 1)
                    o = v_job(seen)
                    dve.tensor_copy(combineT[u][0:EXPERTS, :], o[0:EXPERTS, 0:S]).then_inc(psv_taken, 1)
                if layer == FFN:
                    dve.wait_ge(psa_taken, columns_after(c))
                    if u == 0:
                        dve.wait_ge(table_loaded[FFN], 16)
                        for k, mu in enumerate(("mu_r", "mu_k")):
                            last = dve.tensor_scalar(one_less_mu[:, k:k + 1], W(FFN, mu), -1.0, 1.0, ALU.mult, ALU.add)
                        linked(seen, last)
                    for k in range(2):
                        dve.memset(shifted[u][:, k, 0:1], 0.0)
                        last = dve.tensor_scalar(shifted[u][:, k, 1:S], xnT[u][:, 0:S - 1], one_less_mu[:, k:k + 1],
                                                 None, ALU.mult)
                    linked(seen, last)
                    for k, mu in enumerate(("mu_r", "mu_k")):
                        last = dve.scalar_tensor_tensor(out=mixed_in[u][:, k, :], in0=xnT[u][:], scalar=W(FFN, mu),
                                                        in1=shifted[u][:, k, :], op0=ALU.mult, op1=ALU.add)
                    last.then_inc(mixes_done, 1)

            def project(seen, layer, u, c, g, i):
                if layer == WIDE:
                    for p in range(2):
                        o = v_job(seen)
                        dve.wait_ge(high_done, seen.next("high_done"))
                        for h in range(2):
                            own, other = slice(h * HD, (h + 1) * HD), slice((1 - h) * HD, (2 - h) * HD)
                            j = 2 * p + h
                            dve.tensor_tensor(QW[i % 2][other, j, :], o[own, 0:S], QW[i % 2][own, j, :].bitcast(F32),
                                              ALU.subtract)
                            last = dve.tensor_tensor(KWlo[i % 2][own, j, :], o[own, S:2 * S],
                                                     KWhi[i % 2][own, j, :].bitcast(F32), ALU.subtract)
                        last.then_inc(psv_taken, 1)
                if layer == MOE:
                    for blk in ([0, 1], [2, 3], [4], [5])[g]:
                        o = v_job(seen)
                        n = seen.next("gate")
                        dve.wait_ge(gate_done, n)
                        linked(seen, dve.scalar_tensor_tensor(out=hidden_a[:], in0=gate_tanh[:, n % 2, :], scalar=1.0,
                                                              in1=o[:, 0:S], op0=ALU.add, op1=ALU.mult))
                        expert = blk < EXPERTS // 2
                        dst = hidden_b[:] if expert else hidden[u][:, blk, :]
                        dve.scalar_tensor_tensor(out=dst, in0=hidden_a[:], scalar=0.25 if expert else 0.5,
                                                 in1=o[:, S:2 * S], op0=ALU.mult, op1=ALU.mult).then_inc(psv_taken, 1)
                        if expert:
                            dve.wait_ge(psv_taken, seen.n["psv"])
                            o = v_job(seen)
                            dve.tensor_tensor(hidden[u][:, blk, :], hidden_b[:], o[:, 0:S], ALU.mult).then_inc(psv_taken, 1)

            def maxima(seen, layer, u, c, g, i):
                mx = max_neg
                for t in range(QT):
                    if layer == INFINI or (layer == GEO and t == 0):
                        o = v_job(seen)
                        dve.tensor_reduce(mx[:, t, :], o[:].rearrange("p (j k) -> p j k", j=GROUP), AX.X, ALU.max,
                                          negate=True).then_inc(psv_taken, 1)
                    else:
                        for p in range(2):
                            o = v_job(seen)
                            dve.tensor_reduce(mx[:, t, 2 * p:2 * p + 2], o[:].rearrange("p (j k) -> p j k", j=2), AX.X,
                                              ALU.max, negate=True).then_inc(psv_taken, 1)

            def turn_max(seen, layer, u, c, g, i):
                o = v_job(seen)
                nm = NM
                linked(seen, dve.tensor_copy(nm[0:GROUP, :], o[0:GROUP, 0:S]))
                dve.tensor_tensor(nm[STRIP:STRIP + GROUP, :], o[0:GROUP, 0:S], nm[0:GROUP, :].bitcast(F32),
                                  ALU.subtract).then_inc(psv_taken, 1)

            def values(seen, layer, u, c, g, i):
                if layer in NARROW:
                    o = v_job(seen)
                    dve.tensor_copy(raw[:], o[:, 0:S]).then_inc(psv_taken, 1)

            def normalise(seen, layer, u, c, g, i):
                r = rec
                if layer in NARROW:
                    o = v_job(seen)[:, 0:QT * P].rearrange("p (t j r) -> p t j r", t=QT, j=GROUP)
                    linked(seen, dve.reciprocal(r[:], o[:, :, :, DK]))
                    w = GROUP * DK
                    dst = mixed[u][:, :, g * w:(g + 1) * w].rearrange("p t (j d) -> p t j d", j=GROUP)
                    dve.tensor_tensor(dst, o[:, :, :, 0:DK], r[:, :, :, None].to_broadcast([P, QT, GROUP, DK]),
                                      ALU.mult).then_inc(psv_taken, 1)
                else:
                    w = GROUP * HD
                    for t in range(QT):
                        o = v_job(seen)[:, 0:GROUP * (HD + 2)].rearrange("p (j r) -> p j r", j=GROUP)
                        linked(seen, dve.reciprocal(r[:, t, :], o[:, :, HD]))
                        dst = wide_mixed[:, t, g * w:(g + 1) * w].rearrange("p (j d) -> p j d", j=GROUP)
                        dve.tensor_tensor(dst, o[:, :, 0:HD], r[:, t, :, None].to_broadcast([P, GROUP, HD]),
                                          ALU.mult).then_inc(psv_taken, 1)

            def merge(seen, layer, u, c):
                if layer not in NARROW:
                    return
                o = v_job(seen)[:, 0:S]
                if layer == INFINI:
                    dve.scalar_tensor_tensor(out=mixedT[u][:], in0=o, scalar=one_less_beta[:], in1=recalled[u][:],
                                             op0=ALU.mult, op1=ALU.add).then_inc(psv_taken, 1)
                elif layer == CROSS:
                    dve.tensor_scalar(mixedT[u][:], o, W(CROSS, "bv"), None, ALU.add).then_inc(psv_taken, 1)
                else:
                    dve.tensor_copy(mixedT[u][:], o).then_inc(psv_taken, 1)

            def output(seen, layer, u, c):
                o = v_job(seen)[:, 0:QT * D].rearrange("p (t d) -> p t d", t=QT)
                if layer == FFN:
                    dve.scalar_tensor_tensor(out=gated[u][:], in0=r_tanh[u][:], scalar=1.0, in1=o,
                                             op0=ALU.add, op1=ALU.mult).then_inc(psv_taken, 1)
                    dve.wait_ge(psv_taken, seen.n["psv"])
                    dve.scalar_tensor_tensor(out=X[u][:], in0=gated[u][:], scalar=0.5, in1=X[u][:],
                                             op0=ALU.mult, op1=ALU.add).then_inc(x_final, 1)
                    return
                dve.tensor_tensor(X[u][:], X[u][:], o, ALU.add).then_inc(psv_taken, 1)
                dve.wait_ge(psv_taken, seen.n["psv"])
                if layer == CROSS:
                    linked(seen, dve.tensor_tensor(X[u][:], X[u][:], W(CROSS, "bo")[:, None, :].to_broadcast([P, QT, D]),
                                                   ALU.add))
                norm_stats(seen, u)

            def recall(seen, u, s):
                if s == 0:
                    return
                o = v_job(seen)
                linked(seen, dve.tensor_scalar(v_prev[u][:, 1, :], o[0:SEG, D:2 * D], MEM_EPS, None, ALU.add))
                linked(seen, dve.reciprocal(v_prev[u][:, 1, :], v_prev[u][:, 1, :]))
                linked(seen, dve.tensor_tensor(v_prev[u][:, 0, :], v_prev[u][:, 1, :], o[0:SEG, 0:D], ALU.mult))
                dve.tensor_tensor(told[u][:, 0, :], vtok[u][:, s, :], v_prev[u][:, 0, :], ALU.subtract).then_inc(psv_taken, 1)

            def remember(seen, u, s):
                o = v_job(seen)[:, 0:2 * D].rearrange("p (k d) -> p k d", k=2)
                own = C("blocks")[:, None, :].to_broadcast([P, 2, D])
                if s == 0:
                    dve.tensor_tensor(MZ[u][:], o, own, ALU.mult).then_inc(psv_taken, 1)
                else:
                    linked(seen, dve.tensor_tensor(mz_new[u][:], o, own, ALU.mult))
                    dve.tensor_tensor(MZ[u][:], MZ[u][:], mz_new[u][:], ALU.add).then_inc(psv_taken, 1)

            def answer(seen, u, s):
                o = v_job(seen)
                linked(seen, dve.tensor_scalar(rec_den[u][:], o[:, SEG:2 * SEG], MEM_EPS, None, ALU.add))
                linked(seen, dve.reciprocal(rec_den[u][:], rec_den[u][:]))
                dve.scalar_tensor_tensor(out=recalled[u][:, (s + 1) * SEG:(s + 2) * SEG], in0=o[:, 0:SEG], scalar=beta[:],
                                         in1=rec_den[u][:], op0=ALU.mult, op1=ALU.mult).then_inc(psv_taken, 1)

            seen = Tally()
            for what, c, g in STEPS:
                layer, u = divmod(c, B)
                i = 4 * c + g
                if what == "enter":
                    dve.wait_ge(x_loaded[c], 32)
                    if c >= 2:
                        dve.wait_ge(psa_taken, a_after["enter", c - 2, 0])
                    norm_stats(seen, c)
                    scale(seen, c)
                elif what == "scale":
                    scale(seen, u)
                elif what == "prepare":
                    prepare(seen, layer, u, c)
                elif what == "project":
                    project(seen, layer, u, c, g, i)
                elif what == "maxima":
                    maxima(seen, layer, u, c, g, i)
                elif what == "turn_max":
                    turn_max(seen, layer, u, c, g, i)
                elif what == "values":
                    values(seen, layer, u, c, g, i)
                elif what == "normalise":
                    normalise(seen, layer, u, c, g, i)
                elif what == "merge":
                    merge(seen, layer, u, c)
                elif what == "output":
                    output(seen, layer, u, c)
                elif what == "recall":
                    recall(seen, u, g)
                elif what == "remember":
                    remember(seen, u, g)
                elif what == "answer":
                    answer(seen, u, g)


def lay_out(a):
    f = np.float32
    def column(v, n=1):
        return np.repeat(v, n).reshape(P, 1)

    q, k = a["L0_attn_W_q"].T, a["L0_attn_W_k"].T
    t0 = [q, k, a["L0_attn_W_v"].T, a["L0_attn_W_o"].T, column(a["L0_attn_beta_param"], DK)]
    t1 = [a["L0_xattn_Wq"], a["L0_xattn_Wk"], a["L0_xattn_Wv"], a["L0_xattn_Wo"], column(a["L0_xattn_bq"]),
          column(a["L0_xattn_bk"]), column(a["L0_xattn_bv"]), np.broadcast_to(a["L0_xattn_bo"].reshape(1, D), (P, D))]
    gu = a["L0_ffn_gate_up_w"]
    gate, up = gu[:, :, :64], gu[:, :, 64:]

    def by_pair(w):
        return w.transpose(1, 0, 2).reshape(P, EXPERTS * 64)

    down = np.concatenate([a["L0_ffn_down_w"].reshape(EXPERTS * 64, D), a["L0_ffn_shared_down_w"].T], 0)
    t2 = [a["L0_ffn_router_w"].T, by_pair(gate), a["L0_ffn_shared_gate_w"].T, by_pair(up),
          a["L0_ffn_shared_up_w"].T, down.reshape(BLOCKS, P, D).transpose(1, 0, 2).reshape(P, BLOCKS * D)]
    own = np.zeros((2, P, H, DK), f)
    for h in range(H):
        for d in range(3):
            own[0, 3 * h + d, h, d] = a["L1_attn_scale"][0]
            own[1, 3 * h + d, h, d] = 1.0
            own[:, 3 * h + d, h, 3] = a["L1_attn_head_dirs"][h, d]
    pad3 = [np.concatenate([a[n], np.zeros((P, P - 3 * H), f)], 1) for n in ("L1_attn_wq", "L1_attn_wk")]
    t3 = [*pad3, own[0].reshape(P, D), own[1].reshape(P, D), a["L1_attn_wv"],
          a["L1_attn_wo"]]
    t4 = [a["L1_xattn_w_q"], a["L1_xattn_w_k"], a["L1_xattn_w_v"],
          a["L1_xattn_w_o"].reshape(PAIRS, P, D).transpose(1, 0, 2).reshape(P, PAIRS * D)]
    t5 = [a["L1_ffn_W_r"].T, a["L1_ffn_W_k"].T, a["L1_ffn_W_v"].T, column(a["L1_ffn_mu_r"]), column(a["L1_ffn_mu_k"])]
    return [np.ascontiguousarray(np.concatenate(t, 1)) for t in (t0, t1, t2, t3, t4, t5)]


def constant_table():
    f = np.float32
    r = np.arange(P)
    down, along = r[:, None], r[None, :]
    same = down // SEG == along // SEG
    masks = [np.where(m, 0.0, NEG) for m in ((along <= down) & same, (down <= along) & same, along <= down, down <= along)]
    head_pick = np.zeros((P, GROUP, P))
    expert_pick = np.zeros((P, GROUP, P))
    for j in range(GROUP):
        head_pick[[j, STRIP + j], j, :] = 1
        expert_pick[2 * j, j, :64] = 1
        expert_pick[2 * j + 1, j, 64:] = 1
    strip_pick = np.zeros((P, 2, 2, P))
    for k, parts in enumerate((((0, 1), (2,)), ((0, 2), (1,)))):
        for part, places in enumerate(parts):
            for h in range(H):
                for place in places:
                    for d in range(DK):
                        strip_pick[h * DK + d, k, part, h % GROUP * STRIP + place * DK + d] = 1
    kept = [np.eye(P), expert_pick.reshape(P, -1), down // DK == along // DK, np.broadcast_to(np.arange(8), (P, 8))]
    return (np.concatenate([np.asarray(p, f) for p in kept], 1), strip_pick.reshape(P, -1).astype(f),
            np.concatenate([np.asarray(p, f) for p in (*masks, head_pick.reshape(P, -1))], 1))


def kernel(**inputs):
    import concourse.bacc as bacc
    from concourse.bass_utils import run_bass_kernel_spmd

    a = {k: np.asarray(v) for k, v in inputs.items()}
    nc = bacc.Bacc("TRN2", target_bir_lowering=False, num_devices=1)
    arrays = {"x": np.ascontiguousarray(a["x"]), "ctx_1024": np.ascontiguousarray(a["ctx_1024"]),
              **dict(zip(("constants", "picks", "rounded"), constant_table()))}
    for i, t in enumerate(lay_out(a)):
        arrays[f"table_{i}"] = t
    aps = {n: nc.dram_tensor(f"in_{n}", v.shape, F32, kind="ExternalInput").ap() for n, v in arrays.items()}
    out = nc.dram_tensor("out_0", (B, S, D), F32, kind="ExternalOutput").ap()
    build(nc, aps["x"], aps["ctx_1024"], [aps[f"table_{i}"] for i in range(LAYERS)], aps["constants"],
          aps["picks"], aps["rounded"], out)
    r = run_bass_kernel_spmd(nc, [{f"in_{n}": v for n, v in arrays.items()}], core_ids=[0])
    return r.results[0]["out_0"]
```

```python
from contextlib import ExitStack

import numpy as np

import concourse.bass as bass
from concourse import mybir

F32 = mybir.dt.float32
F32R = mybir.dt.float32r
BF16 = mybir.dt.bfloat16
U32 = mybir.dt.uint32
ALU = mybir.AluOpType
ACT = mybir.ActivationFunctionType
AX = mybir.AxisListType

P = 128
B, S, D = 4, 256, 128
H = 16
QT = S // P
DK = D // H
HD = 64
SEG = 64
NSEG = S // SEG
EXPERTS = 8
GROUP = 4
NG = H // GROUP
STRIP = P // GROUP
BLOCKS = 6
PAIRS = H * HD // P
LN_EPS = 1e-5
MEM_EPS = 1e-6
NEG = -1e30

INFINI, CROSS, MOE, GEO, WIDE, FFN = range(6)
LAYERS = 6
NARROW = (INFINI, CROSS, GEO)
CHUNKS = LAYERS * B
SCALE = {INFINI: DK ** -0.5, CROSS: DK ** -0.5, GEO: 1.0, WIDE: HD ** -0.5}

COLUMNS = {
    INFINI: [("q", 128), ("k", 128), ("v", 128), ("o", 128), ("beta", H)],
    CROSS: [("q", 128), ("k", 128), ("v", 128), ("o", 128), ("bq", 1), ("bk", 1), ("bv", 1), ("bo", 128)],
    MOE: [("expert_pick", 512), ("router", 8), ("gate", BLOCKS * P), ("up", BLOCKS * P), ("o", BLOCKS * P)],
    GEO: [("q3", 128), ("k3", 128), ("q", 128), ("k", 128), ("v", 128), ("o", 128)],
    WIDE: [("o", H * HD)],
    FFN: [("r", 128), ("k", 128), ("o", 128), ("mu_r", 1), ("mu_k", 1)],
}
SPLIT = [("q", H * HD), ("k", H * HD), ("v", H * HD)]
PIECES = 12
CONSTANTS = [("ident", 128), ("blocks", D + H), ("iota", 8)]
ROUNDED = [("masks", 512), ("head_pick", 512)]
PICKS = 2 * 2 * P


def offsets(columns):
    at, out = 0, {}
    for name, n in columns:
        out[name] = (at, n)
        at += n
    return out, at


class Tally:

    def __init__(self):
        self.n = {}

    def next(self, name, by=1):
        self.n[name] = self.n.get(name, 0) + by
        return self.n[name]


WHEN = {
    INFINI: {
        "enter": -6, "ones": -5.5, "enter_scale": -5, "enter_columns": -4.5, "constants": -4.4,
        "prepare": -2.55, "parts": -1.92, "recall": -1.7, "project": -1.6, "remember": -1.5, "answer": -1.1,
        "maxima0": -1.0, "maxima1": -0.66, "turn_max": -0.48, "exps1": 0.03, "exps0": 0.15, "values": 0.78,
        "normalise": 1.13, "merge": 4.34, "output": 4.67, "scale": 4.99, "to_columns": 6.09,
    },
    CROSS: {
        "prepare": -2.0, "parts": -1.92, "project": -1.6, "maxima1": -1.04, "maxima0": -0.83,
        "turn_max": -0.48, "exps1": 0.03, "exps0": 0.15, "values": 0.78, "normalise": 1.06, "merge": 4.34,
        "output": 4.67, "scale": 4.99, "to_columns": 5.45,
    },
    MOE: {
        "prepare": 5.78, "turn_gates": 6.06, "block0": 6.27, "block1": 6.78, "block2": 7.44, "block3": 7.86,
        "block4": 8.59, "block5": 9.28, "output": 9.92, "scale": 10.2, "to_columns": 11.95,
    },
    GEO: {
        "prepare": -2.08, "parts": -1.92, "project": -1.6, "maxima0": -1.0, "maxima1": -0.78,
        "turn_max": -0.48, "exps1": 0.03, "exps0": 0.15, "values": 0.78, "normalise": 1.13, "merge": 4.34,
        "output": 4.67, "scale": 4.99, "to_columns": 5.45,
    },
    WIDE: {
        "prepare": -3.21, "parts": -2.3, "project": -1.6, "maxima0": -1.19, "maxima1": -1.19,
        "turn_max": -0.85, "exps0": -0.22, "exps1": -0.05, "values": 0.46, "normalise": 1.02, "merge": 4.22,
        "output": 4.6, "scale": 4.96, "to_columns": 5.16,
    },
    FFN: {
        "prepare": 5.65, "channel": 5.85, "output": 6.72,
    },
}


def schedule():
    steps = []
    attentions = (INFINI, CROSS, GEO, WIDE)
    for c in range(CHUNKS):
        layer, u = divmod(c, B)
        after = {MOE: CROSS, FFN: WIDE}.get(layer, layer)
        start = 4 * (B * attentions.index(after) + u)
        when = WHEN[layer]

        def step(name, g=0, later=0):
            steps.append((start + when[name] + later, name, c, g))

        if layer == INFINI:
            step("enter")
            step("enter_scale")
            step("enter_columns")
            for n in range(NSEG - 1):
                for name in ("recall", "remember", "answer"):
                    step(name, n, n)
            if u == 0:
                step("ones")
                step("constants")
        step("prepare")
        if layer in attentions:
            step("parts")
        if layer == FFN:
            step("channel")
        if layer == MOE:
            step("turn_gates")
            for block in range(BLOCKS):
                steps.append((start + when[f"block{block}"], "project", c, block))
        if layer in attentions:
            for g in range(NG):
                for name in ("project", "maxima0", "maxima1", "turn_max", "exps0", "exps1", "values", "normalise"):
                    if layer != INFINI or name != "exps1":
                        step(name, g, g)
        if layer in attentions:
            step("merge")
        step("output")
        if layer < LAYERS - 1:
            step("scale")
            step("to_columns")
    return [(name, c, g) for _, name, c, g in sorted(steps, key=lambda st: st[0])]


def v_jobs(what, layer, g):
    if what == "parts":
        return {INFINI: 2, WIDE: 0}.get(layer, 1)
    if what == "prepare":
        return int(layer == MOE)
    if what == "project":
        return {MOE: 2 if g < EXPERTS // 2 else 1, WIDE: 2}.get(layer, 0)
    if what in ("maxima0", "maxima1"):
        return 1 if layer == INFINI or (layer == GEO and what == "maxima0") else 2
    if what == "normalise":
        return 1 if layer in NARROW else 2
    if what == "merge":
        return int(layer in NARROW)
    if what == "recall":
        return int(g > 0)
    return int(what in ("turn_max", "remember", "answer", "output", "turn_gates"))


def a_jobs(what, layer, g):
    if what == "prepare":
        return {INFINI: 1, CROSS: 1, GEO: 2}.get(layer, 0)
    if what == "channel":
        return 2
    if what == "project":
        return int(layer in NARROW or layer == WIDE)
    if what == "merge":
        return PAIRS // 2 if layer == WIDE else 0
    if what in ("exps0", "exps1"):
        return 1 if layer == GEO and what == "exps1" else 2
    if what == "values":
        return 2 if layer == WIDE else 1
    return int(what in ("values", "exps0", "exps1", "enter", "enter_columns", "to_columns"))


def job_numbers(steps, jobs):
    n, after = 0, {}
    for what, c, g in steps:
        n += jobs(what, c // B, g)
        after[what, c, g] = n
    return after


def build(nc, x, ctx_in, tables, to_split, constants, picks, rounded, out):
    OFF = {}
    WIDTH = {}
    for layer in range(LAYERS):
        OFF[layer], WIDTH[layer] = offsets(COLUMNS[layer])
    CO, CW = offsets(CONSTANTS)
    RO, RW = offsets(ROUNDED)
    SO, SW = offsets(SPLIT)
    STEPS = schedule()
    v_after = job_numbers(STEPS, v_jobs)
    a_after = job_numbers(STEPS, a_jobs)

    def columns_after(c):
        return a_after["to_columns", c - B, 0] if c >= B else a_after["enter_columns", c, 0]

    def exps_job(layer, c, g, t, j):
        name = f"exps{t if layer != INFINI else 0}"
        one = layer == GEO and t == 1
        return a_after[name, c, g] - (0 if one else 1 - j // 2)

    with ExitStack() as stack:
        def sb(name, shape, dt=F32):
            return stack.enter_context(nc.sbuf_tensor(name, shape, dt))

        def sem(name):
            return stack.enter_context(nc.semaphore(name))

        table = [sb(f"table{i}", [P, WIDTH[i]]) for i in range(LAYERS)]
        consts = sb("consts", [P, CW])
        split_high = sb("split_high", [P, SW], F32R)
        split_low = sb("split_low", [P, SW], F32R)
        whole = sb("whole", [P, 2, SW // PIECES])

        def W(layer, name):
            a, n = OFF[layer][name]
            return table[layer][:, a:a + n]

        def segment(s):
            return slice(s % 2 * SEG, s % 2 * SEG + SEG)

        def C(name):
            a, n = CO[name]
            return consts[:, a:a + n]

        def halves(name, a, n):
            a += SO[name][0]
            return split_high[:, a:a + n], split_low[:, a:a + n]

        ident = C("ident")
        ident16 = sb("ident16", [P, P], BF16)
        masks = sb("masks", [P, 4, GROUP, P], BF16)
        head_pick = sb("head_pick", [P, GROUP, P], F32R)
        strip_pick = sb("strip_pick", [P, 2, 2, NG, P], F32R)
        beta = sb("beta", [P, H])
        one_less_beta = sb("one_less_beta", [P, H])
        beta_tanh = sb("beta_tanh", [P, H])
        one_less_mu = sb("one_less_mu", [P, 2])
        ln_power = sb("ln_power", [P, QT])

        def each(name, shape, dt=F32):
            return [sb(f"{name}{u}", shape, dt) for u in range(B)]

        def two(name, shape, dt=F32):
            tiles = [sb(f"{name}{u}", shape, dt) for u in range(2)]
            return [tiles[u % 2] for u in range(B)]

        X = each("x", [P, QT, D])
        ctxT = each("ctxT", [P, S])
        xn = each("xn", [P, QT, D])
        xnT = each("xnT", [P, S])
        stats = two("stats", [P, QT, 6])
        meanvar = two("meanvar", [P, QT, 2])
        var_eps = two("var_eps", [P, QT])
        rstd = two("rstd", [P, QT])
        V = two("v_ones", [P, QT, H, STRIP])
        q3T = two("q3T", [P, 2, S])
        mixed = two("mixed", [P, QT, D])
        mixedT = two("mixedT", [P, S])
        ctx_rows = [*mixed[0:2], *(m[:].rearrange("p (t d) -> p t d", t=QT) for m in mixedT[0:2])]
        wide_mixed = sb("wide_mixed", [P, QT, H * HD])
        wide_mixedT = sb("wide_mixedT", [P, PAIRS, S])
        sigT = two("sigT", [P, 2, S])
        sig_e = sb("sig_e", [P, 2, S])
        ktok = two("ktok", [P, QT, D])
        ktok_e = sb("ktok_e", [P, QT, D])
        MZ = two("mz", [P, D + H])
        mz_new = two("mz_new", [P, D + H])
        told = two("told", [P, D + H])
        rec_den = two("rec_den", [P, 2, H])
        recalled = two("recalled", [P, QT, D])
        top8 = two("top8", [P, QT, 8])
        top_at = two("top_at", [P, QT, 8], U32)
        top_atf = two("top_atf", [P, QT, 2])
        gates = two("gates", [P, QT, 2])
        combine = two("combine", [P, QT, 8])
        combine2 = two("combine2", [P, QT, 8])
        logits = two("logits", [P, QT, 8])
        combineT = two("combineT", [P, S], F32R)
        expert_pick = sb("expert_pick", [P, EXPERTS // 2 * P], F32R)
        gate_tanh = sb("gate_tanh", [P, 2, S])
        hidden_a = sb("hidden_a", [P, 2, S])
        hidden_b = sb("hidden_b", [P, S])
        hidden = [wide_mixed[:].rearrange("p t (k s) -> p (t k) s", s=S)[:, 0:BLOCKS, :], wide_mixedT[:, 0:BLOCKS, :]] * 2
        shifted = q3T
        mixed_in = sigT
        k_relu = two("k_relu", [P, S])
        k_act = two("k_act", [P, S])
        r_tanh = two("r_tanh", [P, QT, D])
        gated = two("gated", [P, QT, D])

        QKhi = sb("qk_high", [P, 2, S], F32R)
        QKlo = sb("qk_low", [P, 2, S], F32R)
        QZ = [sb(f"qz{i}", [P, GROUP, S], F32R) for i in range(2)]
        KZ = [sb(f"kz{i}", [P, S], F32R) for i in range(2)]
        QW = [sb(f"qw{i}", [P, GROUP, S], F32R) for i in range(2)]
        KWhi = [sb(f"kw_high{i}", [P, GROUP, S], F32R) for i in range(2)]
        KWlo = [sb(f"kw_low{i}", [P, GROUP, S], F32R) for i in range(2)]
        VW = [sb(f"vw{i}", [P, QT, GROUP, HD + 2]) for i in range(3)]
        max_neg = sb("max_neg", [P, QT, GROUP])
        NM = sb("nm", [P, S], F32R)
        PT = sb("pt", [P, QT, GROUP, S])
        raw = sb("raw", [P, S])
        raw_wide = sb("raw_wide", [HD + 2, GROUP, S])
        rec = sb("rec", [P, QT, GROUP])

        VSLOTS, ASLOTS = 4, 4
        psv = [stack.enter_context(nc.psum_tensor(f"psv{i}", [P, 512], F32)) for i in range(VSLOTS)]
        psa = [stack.enter_context(nc.psum_tensor(f"psa{i}", [P, 512], F32)) for i in range(ASLOTS)]

        table_loaded = [sem(f"table_loaded{i}") for i in range(LAYERS)]
        piece_loaded = [sem(f"piece_loaded{i}") for i in range(2)]
        weights_split = sem("weights_split")
        inputs_split = sem("inputs_split")
        consts_loaded = sem("consts_loaded")
        scratch_loaded = sem("scratch_loaded")
        vector_consts = sem("vector_consts")
        pool_consts = sem("pool_consts")
        scalar_consts = sem("scalar_consts")
        x_loaded = [sem(f"x_loaded{u}") for u in range(B)]
        ctx_loaded = [sem(f"ctx_loaded{u}") for u in range(B)]
        stored = sem("stored")
        psv_ready = sem("psv_ready")
        psv_taken = sem("psv_taken")
        psa_ready = sem("psa_ready")
        psa_taken = sem("psa_taken")
        high_done = sem("high_done")
        var_found = sem("var_found")
        var_shifted = sem("var_shifted")
        rstd_found = sem("rstd_found")
        xn_written = sem("xn_written")
        clipped = sem("clipped")
        clip_exp = sem("clip_exp")
        top_found = sem("top_found")
        combined = sem("combined")
        top_gated = sem("top_gated")
        gate_done = sem("gate_done")
        mixes_done = sem("mixes_done")
        relu_done = sem("relu_done")
        x_final = sem("x_final")
        dve_wrote = sem("dve_wrote")
        POOL_CONSTS, VECTOR_ONES, VECTOR_CONSTS = 9, 6, 21

        block = stack.enter_context(nc.Block())

        @block.sync
        def _(sp):
            def rows(dram, b):
                return dram[b, :, :].rearrange("(t p) d -> p t d", p=P)

            def load(u):
                sp.dma_start(X[u][:], rows(x, u)).then_inc(x_loaded[u], 16)
                sp.dma_start(ctx_rows[u][:], rows(ctx_in, u)).then_inc(ctx_loaded[u], 16)

            load(0)
            sp.dma_start(consts[:], constants).then_inc(consts_loaded, 16)
            sp.dma_start(table[INFINI][:], tables[INFINI]).then_inc(table_loaded[INFINI], 16)
            sp.dma_start(PT[:].rearrange("p t j q -> p (t j q)")[:, 0:PICKS], picks).then_inc(scratch_loaded, 16)
            sp.dma_start(wide_mixed[:].rearrange("p t w -> p (t w)")[:, 0:RW], rounded).then_inc(scratch_loaded, 16)
            for u in range(1, B):
                load(u)
            for i in range(INFINI + 1, LAYERS):
                sp.dma_start(table[i][:], tables[i]).then_inc(table_loaded[i], 16)
            for n in range(PIECES):
                if n >= 2:
                    sp.wait_ge(weights_split, 2 * (n - 1))
                sp.dma_start(whole[:, n % 2, :], to_split[:, n * SW // PIECES:(n + 1) * SW // PIECES]).then_inc(
                    piece_loaded[n % 2], 16)
            for u in range(B):
                sp.wait_ge(x_final, u + 1)
                sp.dma_start(rows(out, u), X[u][:]).then_inc(stored, 16)
            sp.wait_ge(stored, 16 * B)

        @block.tensor
        def _(pe):
            def a_slot(seen):
                n = seen.next("psa")
                if n > ASLOTS:
                    pe.wait_ge(psa_taken, n - ASLOTS)
                return psa[(n - 1) % ASLOTS]

            def v_slot(seen):
                n = seen.next("psv")
                if n > VSLOTS:
                    pe.wait_ge(psv_taken, n - VSLOTS)
                return psv[(n - 1) % VSLOTS]

            def mm(o, l, r, start=True, stop=True):
                return pe.matmul(o, l, r, start=start, stop=stop)

            def turn(o, i, idn):
                return pe.transpose(o, i, idn)

            def enter(seen, u):
                if u == 0:
                    pe.wait_ge(consts_loaded, 16)
                pe.wait_ge(ctx_loaded[u], 16)
                o = a_slot(seen)
                for t in range(QT):
                    last = turn(o[:, t * P:(t + 1) * P], ctx_rows[u][:, t, :], ident)
                last.then_inc(psa_ready, 1)

            def to_columns(seen, u):
                pe.wait_ge(xn_written, seen.next("xn_written"))
                o = a_slot(seen)
                for t in range(QT):
                    last = turn(o[:, t * P:(t + 1) * P], xn[u][:, t, :], ident)
                last.then_inc(psa_ready, 1)

            def prepare(seen, layer, u, c):
                pe.wait_ge(psa_taken, columns_after(c))
                if u == 0:
                    pe.wait_ge(table_loaded[layer], 16)
                src = ctxT[u] if layer == CROSS else xnT[u]
                if layer == GEO:
                    o = a_slot(seen)
                    mm(o[:, 0:S], W(GEO, "q3"), xnT[u][:])
                    mm(o[:, S:2 * S], W(GEO, "k3"), xnT[u][:]).then_inc(psa_ready, 1)
                if layer in NARROW:
                    o = a_slot(seen)
                    for t in range(QT):
                        last = mm(o[:, t * P:(t + 1) * P], src[:, t * P:(t + 1) * P], W(layer, "v"))
                    last.then_inc(psa_ready, 1)
                if layer == MOE:
                    o = v_slot(seen)
                    for t in range(QT):
                        last = mm(o[:, 8 * t:8 * t + 8], xnT[u][:, t * P:(t + 1) * P], W(MOE, "router"))
                    last.then_inc(psv_ready, 1)

            def parts(seen, layer, u, c):
                if layer == WIDE:
                    return
                src = ctxT[u] if layer == CROSS else xnT[u]
                qs, ks = (q3T[u][:, 0, :], q3T[u][:, 1, :]) if layer == GEO else (xnT[u][:], src[:])
                if layer == GEO:
                    pe.wait_ge(psa_taken, a_after["prepare", c, 0] - 1)
                o = v_slot(seen)
                mm(o[:, 0:S], W(layer, "q"), qs)
                mm(o[:, S:2 * S], W(layer, "k"), ks).then_inc(psv_ready, 1)
                if layer == INFINI:
                    o = v_slot(seen)
                    for t in range(QT):
                        last = mm(o[:, t * D:(t + 1) * D], xnT[u][:, t * P:(t + 1) * P], W(INFINI, "k"))
                    last.then_inc(psv_ready, 1)
            def turn_gates(seen, u):
                pe.wait_ge(combined, seen.next("combined"))
                o = v_slot(seen)
                for t in range(QT):
                    last = turn(o[0:8, t * P:(t + 1) * P], combine[u][:, t, :], ident)
                last.then_inc(psv_ready, 1)

            def channel(seen, u):
                pe.wait_ge(mixes_done, seen.next("mixes_done"))
                o = a_slot(seen)
                mm(o[:, 0:S], W(FFN, "k"), mixed_in[u][:, 1, :]).then_inc(psa_ready, 1)
                o = a_slot(seen)
                for t in range(QT):
                    last = mm(o[:, t * D:(t + 1) * D], mixed_in[u][:, 0, t * P:(t + 1) * P], W(FFN, "r"))
                last.then_inc(psa_ready, 1)

            def project(seen, layer, u, c, g, i):
                if layer in NARROW:
                    if g == 0:
                        pe.wait_ge(psv_taken, v_after["parts", c, 0])
                    if c == 0 and g == 0:
                        pe.wait_ge(vector_consts, VECTOR_CONSTS)
                        pe.wait_ge(pool_consts, POOL_CONSTS)
                    o = a_slot(seen)
                    for k in range(2):
                        ok = o[:, k * S:(k + 1) * S]
                        mm(ok, strip_pick[:, k, 0, g, :], QKhi[:, k, :], stop=False)
                        last = mm(ok, strip_pick[:, k, 1, g, :], QKlo[:, k, :], start=False)
                    last.then_inc(psa_ready, 1)
                if layer == WIDE:
                    if g == 0:
                        pe.wait_ge(inputs_split, seen.next("inputs_split"))
                    if c == WIDE * B and g == 0:
                        pe.wait_ge(weights_split, 2 * PIECES)

                    def thrice(o, stationary, moving):
                        (sh, sl), (mh, ml) = stationary, moving
                        mm(o, sh, mh, stop=False)
                        mm(o, sh, ml, start=False, stop=False)
                        return mm(o, sl, mh, start=False)

                    x_parts, ctx_parts = [(QKhi[:, k, :], QKlo[:, k, :]) for k in range(2)]
                    o = a_slot(seen)
                    for t in range(QT):
                        last = thrice(o[:, t * S:(t + 1) * S], [part[:, t * P:(t + 1) * P] for part in ctx_parts],
                                      halves("v", g * S, S))
                    last.then_inc(psa_ready, 1)
                    for p in range(2):
                        w = (2 * g + p) * P
                        o = v_slot(seen)
                        thrice(o[:, 0:S], halves("q", w, P), x_parts)
                        thrice(o[:, S:2 * S], halves("k", w, P), ctx_parts).then_inc(psv_ready, 1)
                if layer == MOE:
                    if g == 0:
                        pe.wait_ge(psv_taken, v_after["turn_gates", c, 0])
                    blk = g
                    o = v_slot(seen)
                    w = slice(blk * P, (blk + 1) * P)
                    mm(o[:, 0:S], W(MOE, "gate")[:, w], xnT[u][:])
                    mm(o[:, S:2 * S], W(MOE, "up")[:, w], xnT[u][:]).then_inc(psv_ready, 1)
                    if blk < EXPERTS // 2:
                        o = v_slot(seen)
                        mm(o[:, 0:S], expert_pick[:, w], combineT[u][:]).then_inc(psv_ready, 1)

            def score_terms(layer, i):
                if layer in NARROW:
                    return lambda j, q: [(QZ[i % 2][:, j, q], KZ[i % 2][:])]
                qw, khi, klo = QW[i % 2], KWhi[i % 2], KWlo[i % 2]
                return lambda j, q: [(qw[:, j, q], khi[:, j, :]), (qw[:, j, q], klo[:, j, :])]

            def maxima(seen, layer, u, c, g, i, t):
                if layer != WIDE:
                    pe.wait_ge(psa_taken, a_after["project", c, g])
                terms = score_terms(layer, i)
                kind = 0 if layer == INFINI else 1
                q = slice(t * P, (t + 1) * P)
                if layer == INFINI or (layer == GEO and t == 0):
                    o = v_slot(seen)
                    mm(o[:], ident16[:], masks[:, 2 * kind, :, :], stop=False)
                    for j in range(GROUP):
                        (qa, ka), = terms(j, q)
                        last = mm(o[:, j * P:(j + 1) * P], qa, ka[:, q], start=False, stop=j == GROUP - 1)
                    last.then_inc(psv_ready, 1)
                else:
                    for p in range(2):
                        if layer == WIDE:
                            pe.wait_ge(psv_taken, v_after["project", c, g] - 1 + p)
                        o = v_slot(seen)
                        for h in range(2):
                            tt = terms(2 * p + h, q)
                            for n, (qa, ka) in enumerate(tt):
                                last = mm(o[:, h * S:(h + 1) * S], qa, ka, start=n == 0,
                                          stop=n == len(tt) - 1 and layer != GEO)
                            if layer == GEO:
                                last = mm(o[:, h * S + P:(h + 1) * S], ident16[:], masks[:, 2, 0, :],
                                          start=False)
                        last.then_inc(psv_ready, 1)

            def turn_max(seen, layer, u, c, g, i):
                pe.wait_ge(psv_taken, max(v_after["maxima0", c, g], v_after["maxima1", c, g]))
                o = v_slot(seen)
                for t in range(QT):
                    last = turn(o[0:GROUP, t * P:(t + 1) * P], max_neg[:, t, :], ident)
                last.then_inc(psv_ready, 1)

            def exps(seen, layer, u, c, g, i, t):
                pe.wait_ge(psv_taken, v_after["turn_max", c, g])
                if layer == WIDE:
                    terms = score_terms(layer, i)
                    k = slice(t * P, (t + 1) * P)
                    for b in range(2):
                        o = a_slot(seen)
                        for h in range(2):
                            oj = o[:, h * S:(h + 1) * S]
                            for n, (qa, ka) in enumerate(terms(2 * b + h, slice(0, S))):
                                mm(oj, ka[:, k], qa, start=n == 0, stop=False)
                            last = mm(oj, head_pick[:, 2 * b + h, :], NM[:], start=False)
                        last.then_inc(psa_ready, 1)
                    return
                qz, kz = QZ[i % 2], KZ[i % 2]
                if layer == GEO and t == 1:
                    k = slice(P, S)
                    o = a_slot(seen)
                    mm(o[:], ident16[:], masks[:, 3, :, :], stop=False)
                    mm(o[:], kz[:, k], qz[:, :, k], start=False, stop=False)
                    for j in range(GROUP):
                        last = mm(o[:, j * P:(j + 1) * P], head_pick[:, j, :], NM[:, k], start=False, stop=j == GROUP - 1)
                    last.then_inc(psa_ready, 1)
                    return
                for b in range(2):
                    o = a_slot(seen)
                    heads = o[:].rearrange("p (h q) -> p h q", h=2)
                    if layer == INFINI:
                        mm(o[:], ident16[:], masks[:, 1, :, :], stop=False)
                        for tile in range(QT):
                            q = slice(tile * P, (tile + 1) * P)
                            mm(heads[:, :, q], kz[:, q], qz[:, 2 * b:2 * b + 2, q], start=False, stop=False)
                    else:
                        mm(heads, kz[:, t * P:(t + 1) * P], qz[:, 2 * b:2 * b + 2, :], stop=False)
                    for h in range(2):
                        last = mm(heads[:, h, :], head_pick[:, 2 * b + h, :], NM[:], start=False, stop=h == 1 and layer != GEO)
                    if layer == GEO:
                        last = mm(heads[:, :, 0:P], ident16[:], masks[:, 3, 0:2, :], start=False)
                    last.then_inc(psa_ready, 1)

            def values(seen, layer, u, c, g, i):
                pt = PT
                if layer in NARROW:
                    if g == 0:
                        pe.wait_ge(psa_taken, a_after["prepare", c, 0])
                    o = a_slot(seen)
                    for t in range(QT):
                        q = slice(t * P, (t + 1) * P) if layer == INFINI else slice(t * P if layer == GEO else 0, S)
                        for j in range(GROUP):
                            if j % 2 == 0:
                                pe.wait_ge(psa_taken, exps_job(layer, c, g, t, j))
                            exp = pt[:, t, j, 0:P] if layer == INFINI else pt[:, t, j, q]
                            last = mm(o[j * STRIP:(j + 1) * STRIP, q], V[u][:, t, GROUP * g + j, :], exp,
                                      start=t == 0 or layer == INFINI, stop=t == QT - 1 or layer == INFINI)
                    last.then_inc(psa_ready, 1)
                else:
                    for b in range(2):
                        pe.wait_ge(psa_taken, max(exps_job(layer, c, g, t, 2 * b) for t in range(QT)))
                        o = a_slot(seen)
                        for h in range(2):
                            for t in range(QT):
                                last = mm(o[0:HD + 2, h * S:(h + 1) * S], VW[i % 3][:, t, 2 * b + h, :],
                                          pt[:, t, 2 * b + h, :], start=t == 0, stop=t == QT - 1)
                        last.then_inc(psa_ready, 1)

            def normalise(seen, layer, u, c, g, i):
                if layer in NARROW:
                    pe.wait_ge(psa_taken, a_after["values", c, g])
                    o = v_slot(seen)
                    for t in range(QT):
                        last = turn(o[:, t * P:(t + 1) * P], raw[:, t * P:(t + 1) * P], ident)
                    last.then_inc(psv_ready, 1)
                else:
                    pe.wait_ge(psa_taken, a_after["values", c, g])
                    for t in range(QT):
                        o = v_slot(seen)
                        for j in range(GROUP):
                            last = turn(o[:, j * (HD + 2):(j + 1) * (HD + 2)], raw_wide[:, j, t * P:(t + 1) * P],
                                        ident[0:HD + 2, 0:HD + 2])
                        last.then_inc(psv_ready, 1)

            def merge(seen, layer, u, c):
                if layer in NARROW:
                    pe.wait_ge(psv_taken, v_after["normalise", c, NG - 1])
                    o = v_slot(seen)
                    for t in range(QT):
                        last = turn(o[:, t * P:(t + 1) * P], mixed[u][:, t, :], ident)
                    last.then_inc(psv_ready, 1)
                if layer == WIDE:
                    pe.wait_ge(psv_taken, v_after["normalise", c, NG - 1])
                    for two_pairs in range(PAIRS // 2):
                        o = a_slot(seen)
                        for p in range(2):
                            for t in range(QT):
                                c0 = (2 * two_pairs + p) * P
                                last = turn(o[:, p * S + t * P:p * S + (t + 1) * P], wide_mixed[:, t, c0:c0 + P], ident)
                        last.then_inc(psa_ready, 1)

            def output(seen, layer, u, c):
                if layer in NARROW:
                    pe.wait_ge(psv_taken, v_after["merge", c, 0])
                    parts = [mixedT[u][:]]
                if layer == WIDE:
                    pe.wait_ge(psa_taken, a_after["merge", c, 0])
                    parts = [wide_mixedT[:, p, :] for p in range(PAIRS)]
                if layer == MOE:
                    pe.wait_ge(psv_taken, v_after["project", c, BLOCKS - 1])
                    parts = [hidden[u][:, k, :] for k in range(BLOCKS)]
                if layer == FFN:
                    pe.wait_ge(psa_taken, a_after["channel", c, 0])
                    parts = [k_act[u][:]]
                o = v_slot(seen)
                for t in range(QT):
                    for n, part in enumerate(parts):
                        last = mm(o[:, t * D:(t + 1) * D], part[:, t * P:(t + 1) * P],
                                  W(layer, "o")[:, n * D:(n + 1) * D], start=n == 0, stop=n == len(parts) - 1)
                last.then_inc(psv_ready, 1)

            def recall(seen, u, s):
                if s == 0:
                    return
                pe.wait_ge(psv_taken, v_after["remember", u, s - 1])
                o = v_slot(seen)
                mm(o[segment(s), 0:D + H], sigT[u][:, 1, s * SEG:(s + 1) * SEG], MZ[u][:]).then_inc(psv_ready, 1)

            def remember(seen, u, s):
                pe.wait_ge(psv_taken, v_after["recall", u, s] if s else v_after["parts", u, 0])
                o = v_slot(seen)
                mm(o[:, 0:D + H], ktok[u][segment(s), s // 2, :], told[u][segment(s), :]).then_inc(psv_ready, 1)

            def answer(seen, u, s):
                pe.wait_ge(psv_taken, v_after["remember", u, s])
                o = v_slot(seen)
                n = s + 1
                mm(o[segment(n), 0:D + H], sigT[u][:, 0, n * SEG:(n + 1) * SEG], MZ[u][:]).then_inc(psv_ready, 1)

            seen = Tally()
            for what, c, g in STEPS:
                layer, u = divmod(c, B)
                i = 4 * c + g
                if what == "enter":
                    enter(seen, c)
                elif what in ("to_columns", "enter_columns"):
                    to_columns(seen, u)
                elif what == "prepare":
                    prepare(seen, layer, u, c)
                elif what == "parts":
                    parts(seen, layer, u, c)
                elif what == "turn_gates":
                    turn_gates(seen, u)
                elif what == "channel":
                    channel(seen, u)
                elif what == "project":
                    project(seen, layer, u, c, g, i)
                elif what in ("maxima0", "maxima1"):
                    maxima(seen, layer, u, c, g, i, int(what[-1]))
                elif what == "turn_max":
                    turn_max(seen, layer, u, c, g, i)
                elif what in ("exps0", "exps1"):
                    exps(seen, layer, u, c, g, i, int(what[-1]))
                elif what == "values":
                    values(seen, layer, u, c, g, i)
                elif what == "normalise":
                    normalise(seen, layer, u, c, g, i)
                elif what == "merge":
                    merge(seen, layer, u, c)
                elif what == "output":
                    output(seen, layer, u, c)
                elif what == "recall":
                    recall(seen, u, g)
                elif what == "remember":
                    remember(seen, u, g)
                elif what == "answer":
                    answer(seen, u, g)

        @block.scalar
        def _(act):
            def a_job(seen):
                n = seen.next("psa")
                act.wait_ge(psa_ready, n)
                return psa[(n - 1) % ASLOTS]

            gate_jobs = []
            act.wait_ge(table_loaded[INFINI], 16)
            act.activation(beta_tanh[:], W(INFINI, "beta"), ACT.Tanh, scale=0.5).then_inc(scalar_consts, 1)

            def to_columns(seen, u):
                o = a_job(seen)
                act.activation(xnT[u][:], o[:, 0:S], ACT.Copy).then_inc(psa_taken, 1)

            def prepare(seen, layer, u, c):
                if layer == INFINI and u == 0:
                    act.wait_ge(vector_consts, VECTOR_ONES)
                if layer == CROSS and u == 0:
                    act.wait_ge(table_loaded[CROSS], 16)
                if layer == GEO:
                    o = a_job(seen)
                    act.activation(q3T[u][:].rearrange("p a s -> p (a s)"), o[:, 0:2 * S], ACT.Copy).then_inc(psa_taken, 1)
                if layer in NARROW:
                    o = a_job(seen)
                    for t in range(QT):
                        last = act.activation(V[u][:, t, :, 0:DK], o[:, t * P:(t + 1) * P].rearrange("p (h d) -> p h d", d=DK),
                                              ACT.Copy)
                    last.then_inc(psa_taken, 1)
                if layer == MOE:
                    act.wait_ge(top_found, seen.next("top_found"))
                    act.activation(gates[u][:], top8[u][:, :, 0:2], ACT.Tanh, scale=0.5).then_inc(top_gated, 1)

            def parts(seen, layer, u, c):
                if layer == WIDE:
                    act.wait_ge(psa_taken, columns_after(c))
                    act.activation(QKhi[:, 0, :], xnT[u][:], ACT.Copy)
                    act.activation(QKhi[:, 1, :], ctxT[u][:], ACT.Copy).then_inc(high_done, 1)
                    return
                job = v_after["parts", c, 0] - v_jobs("parts", layer, 0) + 1
                act.wait_ge(psv_ready, job)
                o = psv[(job - 1) % VSLOTS]
                if layer == CROSS:
                    for k, name in enumerate(("bq", "bk")):
                        last = act.activation(QKhi[:, k, :], o[:, k * S:(k + 1) * S], ACT.Identity, bias=W(CROSS, name))
                else:
                    last = act.activation(QKhi[:].rearrange("p k s -> p (k s)"), o[:, 0:2 * S], ACT.Copy)
                last.then_inc(high_done, 1)
                if layer == INFINI:
                    act.wait_ge(clipped, seen.next("clipped"))
                    act.activation(sig_e[:], sig_e[:], ACT.Exp).then_inc(clip_exp, 1)
                    act.wait_ge(clipped, seen.next("clipped"))
                    act.activation(ktok_e[:], ktok_e[:], ACT.Exp).then_inc(clip_exp, 1)
            def channel(seen, u):
                o = a_job(seen)
                act.activation(k_relu[u][:], o[:, 0:S], ACT.Relu).then_inc(relu_done, 1)
                act.wait_ge(relu_done, seen.next("relu_done"))
                act.activation(k_act[u][:], k_relu[u][:], ACT.Square).then_inc(psa_taken, 1)
                o = a_job(seen)
                act.activation(r_tanh[u][:].rearrange("p t d -> p (t d)"), o[:, 0:QT * D], ACT.Tanh,
                               scale=0.5).then_inc(psa_taken, 1)

            def project(seen, layer, u, c, g, i):
                if layer in NARROW:
                    o = a_job(seen)
                    for j in range(GROUP):
                        r = slice(j * STRIP, (j + 1) * STRIP)
                        act.activation(QZ[i % 2][r, j, :], o[r, 0:S], ACT.Copy)
                    act.activation(KZ[i % 2][:], o[:, S:2 * S], ACT.Copy).then_inc(psa_taken, 1)
                if layer == WIDE:
                    o = a_job(seen)
                    for t in range(QT):
                        last = act.activation(VW[i % 3][:, t, :, 0:HD], o[:, t * S:(t + 1) * S].rearrange("p (h d) -> p h d", d=HD),
                                              ACT.Copy)
                    last.then_inc(psa_taken, 1)
                    for p in range(2):
                        job = v_after["project", c, g] - 1 + p
                        act.wait_ge(psv_ready, job)
                        o = psv[(job - 1) % VSLOTS]
                        for h in range(2):
                            own, other = slice(h * HD, (h + 1) * HD), slice((1 - h) * HD, (2 - h) * HD)
                            act.activation(QW[i % 2][own, 2 * p + h, :], o[own, 0:S], ACT.Copy)
                            act.activation(KWhi[i % 2][own, 2 * p + h, :], o[own, S:2 * S], ACT.Copy)
                            last = act.activation(KWhi[i % 2][other, 2 * p + h, :], o[own, S:2 * S], ACT.Copy)
                        last.then_inc(high_done, 1)
                if layer == MOE:
                    blk = g
                    job = v_after["project", c, g] - v_jobs("project", MOE, g) + 1
                    act.wait_ge(psv_ready, job)
                    n = seen.next("gate")
                    if n > 2:
                        act.wait_ge(psv_taken, gate_jobs[n - 3])
                    gate_jobs.append(job)
                    act.activation(gate_tanh[:, n % 2, :], psv[(job - 1) % VSLOTS][:, 0:S], ACT.Tanh,
                                   scale=0.5).then_inc(gate_done, 1)

            def exps(seen, layer, u, c, g, i, t):
                pt = PT
                if layer == GEO and t == 1:
                    o = a_job(seen)
                    act.activation(pt[:, 1, :, P:S], o[:].rearrange("p (j q) -> p j q", j=GROUP),
                                   ACT.Exp, scale=SCALE[layer]).then_inc(psa_taken, 1)
                    return
                for b in range(2):
                    o = a_job(seen)
                    if layer == INFINI:
                        act.activation(pt[:, :, 2 * b:2 * b + 2, 0:P].rearrange("p t j q -> p j t q"),
                                       o[:].rearrange("p (j t q) -> p j t q", j=2, t=QT),
                                       ACT.Exp, scale=SCALE[layer]).then_inc(psa_taken, 1)
                    else:
                        act.activation(pt[:, t, 2 * b:2 * b + 2, :].rearrange("p j q -> p (j q)"), o[:],
                                       ACT.Exp, scale=SCALE[layer]).then_inc(psa_taken, 1)

            def values(seen, layer, u, c, g, i):
                if layer in NARROW:
                    o = a_job(seen)
                    act.activation(raw[:], o[:, 0:S], ACT.Copy).then_inc(psa_taken, 1)
                    return
                for b in range(2):
                    o = a_job(seen)
                    act.activation(raw_wide[:, 2 * b:2 * b + 2, :].rearrange("p j q -> p (j q)"), o[0:HD + 2, :],
                                   ACT.Copy).then_inc(psa_taken, 1)

            def merge(seen, layer, u, c):
                if layer == WIDE:
                    for two_pairs in range(PAIRS // 2):
                        o = a_job(seen)
                        act.activation(wide_mixedT[:, 2 * two_pairs:2 * two_pairs + 2, :].rearrange("p k s -> p (k s)"),
                                       o[:], ACT.Copy).then_inc(psa_taken, 1)

            seen = Tally()
            for what, c, g in STEPS:
                layer, u = divmod(c, B)
                i = 4 * c + g
                if what == "enter":
                    o = a_job(seen)
                    act.activation(ctxT[c][:], o[:, 0:S], ACT.Copy).then_inc(psa_taken, 1)
                elif what in ("to_columns", "enter_columns"):
                    to_columns(seen, u)
                elif what == "prepare":
                    prepare(seen, layer, u, c)
                elif what == "parts":
                    parts(seen, layer, u, c)
                elif what == "channel":
                    channel(seen, u)
                elif what == "project":
                    project(seen, layer, u, c, g, i)
                elif what in ("exps0", "exps1"):
                    exps(seen, layer, u, c, g, i, int(what[-1]))
                elif what == "values":
                    values(seen, layer, u, c, g, i)
                elif what == "merge":
                    merge(seen, layer, u, c)

        @block.gpsimd
        def _(pool):
            def zeros(*tiles):
                for tile in tiles:
                    pool.memset(tile[:].bitcast(F32), 0.0).then_inc(pool_consts, 1)

            pool.memset(ln_power[:], -0.5).then_inc(pool_consts, 1)
            zeros(strip_pick, *QZ)
            pool.wait_ge(pool_consts, 4)
            seen = Tally()
            for what, c, g in STEPS:
                u = c % B
                if what == "constants":
                    zeros(NM, *KWlo, *combineT[0:2])
                if what == "enter" or (what == "output" and c // B < LAYERS - 1):
                    n = seen.next("norm")
                    pool.wait_ge(var_found, n)
                    pool.tensor_scalar(var_eps[u][:], meanvar[u][:, :, 1], LN_EPS, None, ALU.add).then_inc(var_shifted, 1)
                    pool.wait_ge(var_shifted, n)
                    pool.tensor_tensor(rstd[u][:], var_eps[u][:], ln_power[:], ALU.pow).then_inc(rstd_found, 1)
                if what == "output" and c // B in (INFINI, CROSS, MOE):
                    n = seen.next("piece") - 1
                    pool.wait_ge(piece_loaded[n % 2], 16 * (n // 2 + 1))
                    w = slice(n * SW // PIECES, (n + 1) * SW // PIECES)
                    pool.tensor_copy(split_high[:, w], whole[:, n % 2, :]).then_inc(weights_split, 1)
                    pool.wait_ge(weights_split, seen.next("weights_split"))
                    pool.tensor_tensor(split_low[:, w], whole[:, n % 2, :], split_high[:, w].bitcast(F32),
                                       ALU.subtract).then_inc(weights_split, 1)
                    seen.next("weights_split")

        @block.vector
        def _(dve):
            def v_job(seen):
                n = seen.next("psv")
                dve.wait_ge(psv_ready, n)
                return psv[(n - 1) % VSLOTS]

            def linked(seen, ins):
                ins.then_inc(dve_wrote, 1)
                dve.wait_ge(dve_wrote, seen.next("dve_wrote"))

            def make_ones():
                for u in range(2):
                    dve.memset(V[u][:], 1.0).then_inc(vector_consts, 1)
                    dve.memset(told[u][:, D:D + H], 1.0).then_inc(vector_consts, 1)
                    dve.memset(recalled[u][segment(0), 0, :], 0.0).then_inc(vector_consts, 1)

            def make_constants():
                dve.wait_ge(consts_loaded, 16)
                dve.tensor_copy(ident16[:], ident).then_inc(vector_consts, 1)
                dve.wait_ge(scratch_loaded, 32)
                dve.wait_ge(pool_consts, 2)
                for g in range(NG):
                    r = slice(g * STRIP, (g + 1) * STRIP)
                    m = PT[:].rearrange("p t j q -> p (t j q)")[r, 0:PICKS].rearrange("p (k i m) -> p k i m", k=2, i=2)
                    dve.tensor_copy(strip_pick[r, :, :, g, :], m).then_inc(vector_consts, 1)
                for k in range(4):
                    a = RO["masks"][0] + k * P
                    m = wide_mixed[:].rearrange("p t w -> p (t w)")[:, a:a + P]
                    dve.tensor_copy(masks[:, k, :, :], m[:, None, :].to_broadcast([P, GROUP, P])).then_inc(vector_consts, 1)
                a, n = RO["head_pick"]
                dve.tensor_copy(head_pick[:].rearrange("p j k -> p (j k)"),
                                wide_mixed[:].rearrange("p t w -> p (t w)")[:, a:a + n]).then_inc(vector_consts, 1)
                dve.wait_ge(scalar_consts, 1)
                dve.tensor_scalar(beta[:], beta_tanh[:], 0.5, 0.5, ALU.mult, ALU.add).then_inc(vector_consts, 1)
                dve.tensor_scalar(one_less_beta[:], beta_tanh[:], -0.5, 0.5, ALU.mult, ALU.add).then_inc(vector_consts, 1)
                for t in VW:
                    dve.memset(t[:, :, :, HD:HD + 2], 1.0).then_inc(vector_consts, 1)
                dve.wait_ge(vector_consts, VECTOR_CONSTS)
                dve.wait_ge(pool_consts, POOL_CONSTS)

            def norm_stats(seen, u):
                for t in range(QT):
                    last = dve.bn_stats(stats[u][:, t, :], X[u][:, t, :])
                linked(seen, last)
                for t in range(QT):
                    last = dve.bn_aggr(meanvar[u][:, t, :], stats[u][:, t, :])
                last.then_inc(var_found, 1)

            def scale(seen, u):
                dve.wait_ge(rstd_found, seen.next("rstd_found"))
                for t in range(QT):
                    last = dve.tensor_scalar(xn[u][:, t, :], X[u][:, t, :], meanvar[u][:, t, 0:1], rstd[u][:, t:t + 1],
                                             ALU.subtract, ALU.mult)
                last.then_inc(xn_written, 1)

            def turn_gates(seen, u):
                o = v_job(seen)
                if u == 0:
                    dve.tensor_copy(expert_pick[:], W(MOE, "expert_pick"))
                linked(seen, dve.tensor_copy(combineT[u][0:EXPERTS, :], o[0:EXPERTS, 0:S]))
                dve.tensor_tensor(combineT[u][STRIP:STRIP + EXPERTS, :], o[0:EXPERTS, 0:S],
                                  combineT[u][0:EXPERTS, :].bitcast(F32), ALU.subtract).then_inc(psv_taken, 1)

            def parts(seen, layer, u, c):
                if layer == WIDE:
                    dve.wait_ge(high_done, seen.next("high_done"))
                    for k, whole in enumerate((xnT, ctxT)):
                        last = dve.tensor_tensor(QKlo[:, k, :], whole[u][:], QKhi[:, k, :].bitcast(F32), ALU.subtract)
                    last.then_inc(inputs_split, 1)
                    return
                o1 = v_job(seen)
                o1 = o1[:, 0:2 * S].rearrange("p (k s) -> p k s", k=2)
                dve.wait_ge(high_done, seen.next("high_done"))
                if layer == CROSS:
                    for k, name in enumerate(("bq", "bk")):
                        last = dve.scalar_tensor_tensor(out=QKlo[:, k, :], in0=o1[:, k, :], scalar=W(CROSS, name),
                                                        in1=QKhi[:, k, :].bitcast(F32), op0=ALU.add, op1=ALU.subtract)
                else:
                    last = dve.tensor_tensor(QKlo[:], o1, QKhi[:].bitcast(F32), ALU.subtract)
                if layer != INFINI:
                    last.then_inc(psv_taken, 1)
                if layer == INFINI:
                    dve.tensor_scalar(sig_e[:], o1, 0.0, None, ALU.min).then_inc(clipped, 1)
                    o2 = v_job(seen)
                    o2 = o2[:, 0:QT * D].rearrange("p (t d) -> p t d", d=D)
                    dve.tensor_scalar(ktok_e[:], o2, 0.0, None, ALU.min).then_inc(clipped, 1)
                    dve.wait_ge(clip_exp, seen.next("clip_exp"))
                    dve.scalar_tensor_tensor(out=sigT[u][:], in0=o1, scalar=0.0, in1=sig_e[:],
                                             op0=ALU.max, op1=ALU.add).then_inc(psv_taken, 1)
                    dve.wait_ge(psa_taken, a_after["prepare", c, 0])
                    dve.tensor_copy(told[u][segment(0), 0:D].rearrange("p (h d) -> p h d", h=H), V[u][segment(0), 0, :, 0:DK])
                    dve.wait_ge(clip_exp, seen.next("clip_exp"))
                    dve.scalar_tensor_tensor(out=ktok[u][:], in0=o2, scalar=0.0, in1=ktok_e[:],
                                             op0=ALU.max, op1=ALU.add).then_inc(psv_taken, 1)

            def prepare(seen, layer, u, c):
                if layer == MOE:
                    o = v_job(seen)
                    dve.tensor_copy(logits[u][:].rearrange("p t e -> p (t e)"), o[:, 0:8 * QT]).then_inc(psv_taken, 1)
                    dve.wait_ge(psv_taken, seen.n["psv"])
                    for t in range(QT):
                        last = dve.max(top8[u][:, t, :], logits[u][:, t, :])
                    n = seen.next("top_found")
                    last.then_inc(top_found, 1)
                    dve.wait_ge(top_found, n)
                    for t in range(QT):
                        last = dve.max_index(top_at[u][:, t, :], top8[u][:, t, :], logits[u][:, t, :])
                    linked(seen, last)
                    linked(seen, dve.tensor_copy(top_atf[u][:], top_at[u][:, :, 0:2]))
                    dve.wait_ge(top_gated, seen.next("top_gated"))
                    linked(seen, dve.tensor_scalar(gates[u][:], gates[u][:], 1.0, None, ALU.add))
                    for t in range(QT):
                        for k, dst in enumerate((combine, combine2)):
                            last = dve.tensor_scalar(dst[u][:, t, :], C("iota"), top_atf[u][:, t, k:k + 1],
                                                     gates[u][:, t, k:k + 1], ALU.is_equal, ALU.mult)
                    linked(seen, last)
                    dve.tensor_tensor(combine[u][:], combine[u][:], combine2[u][:], ALU.add).then_inc(combined, 1)
                if layer == FFN:
                    dve.wait_ge(psa_taken, columns_after(c))
                    if u == 0:
                        dve.wait_ge(table_loaded[FFN], 16)
                        for k, mu in enumerate(("mu_r", "mu_k")):
                            last = dve.tensor_scalar(one_less_mu[:, k:k + 1], W(FFN, mu), -1.0, 1.0, ALU.mult, ALU.add)
                        linked(seen, last)
                    for k in range(2):
                        dve.memset(shifted[u][:, k, 0:1], 0.0)
                        last = dve.tensor_scalar(shifted[u][:, k, 1:S], xnT[u][:, 0:S - 1], one_less_mu[:, k:k + 1],
                                                 None, ALU.mult)
                    linked(seen, last)
                    for k, mu in enumerate(("mu_r", "mu_k")):
                        last = dve.scalar_tensor_tensor(out=mixed_in[u][:, k, :], in0=xnT[u][:], scalar=W(FFN, mu),
                                                        in1=shifted[u][:, k, :], op0=ALU.mult, op1=ALU.add)
                    last.then_inc(mixes_done, 1)

            def project(seen, layer, u, c, g, i):
                if layer == WIDE:
                    for p in range(2):
                        o = v_job(seen)
                        dve.wait_ge(high_done, seen.next("high_done"))
                        for h in range(2):
                            own, other = slice(h * HD, (h + 1) * HD), slice((1 - h) * HD, (2 - h) * HD)
                            j = 2 * p + h
                            dve.tensor_tensor(QW[i % 2][other, j, :], o[own, 0:S], QW[i % 2][own, j, :].bitcast(F32),
                                              ALU.subtract)
                            last = dve.tensor_tensor(KWlo[i % 2][own, j, :], o[own, S:2 * S],
                                                     KWhi[i % 2][own, j, :].bitcast(F32), ALU.subtract)
                        last.then_inc(psv_taken, 1)
                if layer == MOE:
                    blk = g
                    o = v_job(seen)
                    n = seen.next("gate")
                    dve.wait_ge(gate_done, n)
                    linked(seen, dve.scalar_tensor_tensor(out=hidden_a[:, n % 2, :], in0=gate_tanh[:, n % 2, :], scalar=1.0,
                                                          in1=o[:, 0:S], op0=ALU.add, op1=ALU.mult))
                    expert = blk < EXPERTS // 2
                    dst = hidden_b[:] if expert else hidden[u][:, blk, :]
                    dve.scalar_tensor_tensor(out=dst, in0=hidden_a[:, n % 2, :], scalar=0.25 if expert else 0.5,
                                             in1=o[:, S:2 * S], op0=ALU.mult, op1=ALU.mult).then_inc(psv_taken, 1)
                    if expert:
                        dve.wait_ge(psv_taken, seen.n["psv"])
                        o = v_job(seen)
                        dve.tensor_tensor(hidden[u][:, blk, :], hidden_b[:], o[:, 0:S], ALU.mult).then_inc(psv_taken, 1)

            def maxima(seen, layer, u, c, g, i, t):
                mx = max_neg
                if layer == INFINI or (layer == GEO and t == 0):
                    o = v_job(seen)
                    dve.tensor_reduce(mx[:, t, :], o[:].rearrange("p (j k) -> p j k", j=GROUP), AX.X, ALU.max,
                                      negate=True).then_inc(psv_taken, 1)
                else:
                    for p in range(2):
                        o = v_job(seen)
                        dve.tensor_reduce(mx[:, t, 2 * p:2 * p + 2], o[:].rearrange("p (j k) -> p j k", j=2), AX.X,
                                          ALU.max, negate=True).then_inc(psv_taken, 1)

            def turn_max(seen, layer, u, c, g, i):
                o = v_job(seen)
                nm = NM
                linked(seen, dve.tensor_copy(nm[0:GROUP, :], o[0:GROUP, 0:S]))
                dve.tensor_tensor(nm[STRIP:STRIP + GROUP, :], o[0:GROUP, 0:S], nm[0:GROUP, :].bitcast(F32),
                                  ALU.subtract).then_inc(psv_taken, 1)

            def normalise(seen, layer, u, c, g, i):
                r = rec
                if layer in NARROW:
                    o = v_job(seen)[:, 0:QT * P].rearrange("p (t j r) -> p t j r", t=QT, j=GROUP)
                    linked(seen, dve.reciprocal(r[:], o[:, :, :, DK]))
                    if layer == INFINI:
                        share = one_less_beta[:, None, GROUP * g:GROUP * (g + 1)].to_broadcast([P, QT, GROUP])
                        linked(seen, dve.tensor_tensor(r[:], r[:], share, ALU.mult))
                    w = GROUP * DK
                    dst = mixed[u][:, :, g * w:(g + 1) * w].rearrange("p t (j d) -> p t j d", j=GROUP)
                    last = dve.tensor_tensor(dst, o[:, :, :, 0:DK], r[:, :, :, None].to_broadcast([P, QT, GROUP, DK]),
                                             ALU.mult)
                    if layer == INFINI and g == NG - 1:
                        linked(seen, last)
                        last = dve.tensor_tensor(mixed[u][:], mixed[u][:], recalled[u][:], ALU.add)
                    last.then_inc(psv_taken, 1)
                else:
                    w = GROUP * HD
                    for t in range(QT):
                        o = v_job(seen)[:, 0:GROUP * (HD + 2)].rearrange("p (j r) -> p j r", j=GROUP)
                        linked(seen, dve.reciprocal(r[:, t, :], o[:, :, HD]))
                        dst = wide_mixed[:, t, g * w:(g + 1) * w].rearrange("p (j d) -> p j d", j=GROUP)
                        dve.tensor_tensor(dst, o[:, :, 0:HD], r[:, t, :, None].to_broadcast([P, GROUP, HD]),
                                          ALU.mult).then_inc(psv_taken, 1)

            def merge(seen, layer, u, c):
                if layer not in NARROW:
                    return
                o = v_job(seen)[:, 0:S]
                if layer == CROSS:
                    dve.tensor_scalar(mixedT[u][:], o, W(CROSS, "bv"), None, ALU.add).then_inc(psv_taken, 1)
                else:
                    dve.tensor_copy(mixedT[u][:], o).then_inc(psv_taken, 1)

            def output(seen, layer, u, c):
                o = v_job(seen)[:, 0:QT * D].rearrange("p (t d) -> p t d", t=QT)
                if layer == FFN:
                    dve.scalar_tensor_tensor(out=gated[u][:], in0=r_tanh[u][:], scalar=1.0, in1=o,
                                             op0=ALU.add, op1=ALU.mult).then_inc(psv_taken, 1)
                    dve.wait_ge(psv_taken, seen.n["psv"])
                    dve.scalar_tensor_tensor(out=X[u][:], in0=gated[u][:], scalar=0.5, in1=X[u][:],
                                             op0=ALU.mult, op1=ALU.add).then_inc(x_final, 1)
                    return
                dve.tensor_tensor(X[u][:], X[u][:], o, ALU.add).then_inc(psv_taken, 1)
                dve.wait_ge(psv_taken, seen.n["psv"])
                if layer == CROSS:
                    linked(seen, dve.tensor_tensor(X[u][:], X[u][:], W(CROSS, "bo")[:, None, :].to_broadcast([P, QT, D]),
                                                   ALU.add))
                norm_stats(seen, u)

            def recall(seen, u, s):
                if s == 0:
                    return
                o = v_job(seen)[segment(s), :]
                r = rec_den[u][segment(s), 0, :]
                t = told[u][segment(s), 0:D].rearrange("p (h d) -> p h d", h=H)
                linked(seen, dve.tensor_scalar(r, o[:, D:D + H], MEM_EPS, None, ALU.add))
                linked(seen, dve.reciprocal(r, r))
                linked(seen, dve.tensor_tensor(t, o[:, 0:D].rearrange("p (h d) -> p h d", h=H),
                                               r[:, :, None].to_broadcast([SEG, H, DK]), ALU.mult))
                dve.tensor_tensor(t, V[u][segment(s), s // 2, :, 0:DK], t, ALU.subtract).then_inc(psv_taken, 1)

            def remember(seen, u, s):
                o = v_job(seen)[:, 0:D + H]
                own = C("blocks")
                if s == 0:
                    dve.tensor_tensor(MZ[u][:], o, own, ALU.mult).then_inc(psv_taken, 1)
                else:
                    linked(seen, dve.tensor_tensor(mz_new[u][:], o, own, ALU.mult))
                    dve.tensor_tensor(MZ[u][:], MZ[u][:], mz_new[u][:], ALU.add).then_inc(psv_taken, 1)

            def answer(seen, u, s):
                n = s + 1
                o = v_job(seen)[segment(n), :]
                r = rec_den[u][segment(n), 1, :]
                linked(seen, dve.tensor_scalar(r, o[:, D:D + H], MEM_EPS, None, ALU.add))
                linked(seen, dve.reciprocal(r, r))
                linked(seen, dve.tensor_tensor(r, r, beta[segment(n), :], ALU.mult))
                dve.tensor_tensor(recalled[u][segment(n), n // 2, :].rearrange("p (h d) -> p h d", h=H),
                                  o[:, 0:D].rearrange("p (h d) -> p h d", h=H),
                                  r[:, :, None].to_broadcast([SEG, H, DK]), ALU.mult).then_inc(psv_taken, 1)

            seen = Tally()
            for what, c, g in STEPS:
                layer, u = divmod(c, B)
                i = 4 * c + g
                if what == "enter":
                    dve.wait_ge(x_loaded[c], 16)
                    norm_stats(seen, c)
                elif what == "ones":
                    make_ones()
                elif what == "constants":
                    make_constants()
                elif what == "enter_scale":
                    scale(seen, c)
                elif what == "scale":
                    scale(seen, u)
                elif what == "prepare":
                    prepare(seen, layer, u, c)
                elif what == "parts":
                    parts(seen, layer, u, c)
                elif what == "turn_gates":
                    turn_gates(seen, u)
                elif what == "project":
                    project(seen, layer, u, c, g, i)
                elif what in ("maxima0", "maxima1"):
                    maxima(seen, layer, u, c, g, i, int(what[-1]))
                elif what == "turn_max":
                    turn_max(seen, layer, u, c, g, i)
                elif what == "normalise":
                    normalise(seen, layer, u, c, g, i)
                elif what == "merge":
                    merge(seen, layer, u, c)
                elif what == "output":
                    output(seen, layer, u, c)
                elif what == "recall":
                    recall(seen, u, g)
                elif what == "remember":
                    remember(seen, u, g)
                elif what == "answer":
                    answer(seen, u, g)


def lay_out(a):
    f = np.float32
    def column(v, n=1):
        return np.repeat(v, n).reshape(P, 1)

    q, k = a["L0_attn_W_q"].T, a["L0_attn_W_k"].T
    t0 = [q, k, a["L0_attn_W_v"].T, a["L0_attn_W_o"].T, np.broadcast_to(a["L0_attn_beta_param"].reshape(1, H), (P, H))]
    t1 = [a["L0_xattn_Wq"], a["L0_xattn_Wk"], a["L0_xattn_Wv"], a["L0_xattn_Wo"], column(a["L0_xattn_bq"]),
          column(a["L0_xattn_bk"]), column(a["L0_xattn_bv"]), np.broadcast_to(a["L0_xattn_bo"].reshape(1, D), (P, D))]
    gu = a["L0_ffn_gate_up_w"]
    gate, up = gu[:, :, :64], gu[:, :, 64:]

    def by_pair(w):
        return w.transpose(1, 0, 2).reshape(P, EXPERTS * 64)

    down = np.concatenate([a["L0_ffn_down_w"].reshape(EXPERTS * 64, D), a["L0_ffn_shared_down_w"].T], 0)
    expert_pick = np.zeros((P, GROUP, P), f)
    for j in range(GROUP):
        expert_pick[[2 * j, STRIP + 2 * j], j, :64] = 1
        expert_pick[[2 * j + 1, STRIP + 2 * j + 1], j, 64:] = 1
    t2 = [expert_pick.reshape(P, -1), a["L0_ffn_router_w"].T, by_pair(gate), a["L0_ffn_shared_gate_w"].T, by_pair(up),
          a["L0_ffn_shared_up_w"].T, down.reshape(BLOCKS, P, D).transpose(1, 0, 2).reshape(P, BLOCKS * D)]
    own = np.zeros((2, P, H, DK), f)
    for h in range(H):
        for d in range(3):
            own[0, 3 * h + d, h, d] = a["L1_attn_scale"][0]
            own[1, 3 * h + d, h, d] = 1.0
            own[:, 3 * h + d, h, 3] = a["L1_attn_head_dirs"][h, d]
    pad3 = [np.concatenate([a[n], np.zeros((P, P - 3 * H), f)], 1) for n in ("L1_attn_wq", "L1_attn_wk")]
    t3 = [*pad3, own[0].reshape(P, D), own[1].reshape(P, D), a["L1_attn_wv"],
          a["L1_attn_wo"]]
    t4 = [a["L1_xattn_w_o"].reshape(PAIRS, P, D).transpose(1, 0, 2).reshape(P, PAIRS * D)]
    t5 = [a["L1_ffn_W_r"].T, a["L1_ffn_W_k"].T, a["L1_ffn_W_v"].T, column(a["L1_ffn_mu_r"]), column(a["L1_ffn_mu_k"])]
    return [np.ascontiguousarray(np.concatenate(t, 1)) for t in (t0, t1, t2, t3, t4, t5)]


def constant_table():
    f = np.float32
    r = np.arange(P)
    down, along = r[:, None], r[None, :]
    same = down // SEG == along // SEG
    masks = [np.where(m, 0.0, NEG) for m in ((along <= down) & same, (down <= along) & same, along <= down, down <= along)]
    head_pick = np.zeros((P, GROUP, P))
    for j in range(GROUP):
        head_pick[[j, STRIP + j], j, :] = 1
    strip_pick = np.zeros((P, 2, 2, P))
    for k, parts in enumerate((((0, 1), (2,)), ((0, 2), (1,)))):
        for part, places in enumerate(parts):
            for h in range(H):
                for place in places:
                    for d in range(DK):
                        strip_pick[h * DK + d, k, part, h % GROUP * STRIP + place * DK + d] = 1
    kept = [np.eye(P), down // DK == along // DK, down // DK == np.arange(H)[None, :],
            np.broadcast_to(np.arange(8), (P, 8))]
    return (np.concatenate([np.asarray(p, f) for p in kept], 1), strip_pick.reshape(P, -1).astype(f),
            np.concatenate([np.asarray(p, f) for p in (*masks, head_pick.reshape(P, -1))], 1))


def kernel(**inputs):
    import concourse.bacc as bacc
    from concourse.bass_utils import run_bass_kernel_spmd

    a = {k: np.asarray(v) for k, v in inputs.items()}
    nc = bacc.Bacc("TRN2", target_bir_lowering=False, num_devices=1)
    arrays = {"x": np.ascontiguousarray(a["x"]), "ctx_1024": np.ascontiguousarray(a["ctx_1024"]),
              **dict(zip(("constants", "picks", "rounded"), constant_table()))}
    arrays["to_split"] = np.concatenate([a["L1_xattn_w_q"], a["L1_xattn_w_k"], a["L1_xattn_w_v"]], 1)
    for i, t in enumerate(lay_out(a)):
        arrays[f"table_{i}"] = t
    aps = {n: nc.dram_tensor(f"in_{n}", v.shape, F32, kind="ExternalInput").ap() for n, v in arrays.items()}
    out = nc.dram_tensor("out_0", (B, S, D), F32, kind="ExternalOutput").ap()
    build(nc, aps["x"], aps["ctx_1024"], [aps[f"table_{i}"] for i in range(LAYERS)], aps["to_split"], aps["constants"],
          aps["picks"], aps["rounded"], out)
    r = run_bass_kernel_spmd(nc, [{f"in_{n}": v for n, v in arrays.items()}], core_ids=[0])
    return r.results[0]["out_0"]
```
